# Optimizing a Trainium2 kernel written in Bass

```python
import numpy as np
import jax
import jax.numpy as jnp

def _softmax(x, axis=-1):
    return jax.nn.softmax(x, axis=axis)

def _gelu(x):
    return jax.nn.gelu(x, approximate=True)

def _silu(x):
    return jax.nn.silu(x)

def _sigmoid(x):
    return jax.nn.sigmoid(x)

def _layernorm(x, axis=-1, eps=1e-05):
    m = jnp.mean(x, axis=axis, keepdims=True)
    v = jnp.var(x, axis=axis, keepdims=True)
    return (x - m) / jnp.sqrt(v + eps)

def _scatter_add(tgt, idx, src, axis=0):
    return tgt.at[idx].add(src)

def _segment_sum(src, seg, n):
    return jax.ops.segment_sum(src, seg, n)
kernel_name = 'mk_decoder_preln_d2_seqx_r8_b2d60a'

def setup_inputs(seed: int=0):
    np.random.seed(seed)
    _w = jnp.asarray

    def _rec_inputs():
        import jax
        import jax.numpy as jnp
        _rk = jax.random.key(seed)
        x = -9.806e-05 + 1 * jax.random.normal(jax.random.fold_in(_rk, 1), (64, 128, 128), jnp.float32)
        _lenS = 128 - jax.random.randint(jax.random.fold_in(_rk, 7), (64,), 0, max(1, 128 // 4) + 1, jnp.int32)
        _lenS2 = 77 - jax.random.randint(jax.random.fold_in(_rk, 8), (64,), 0, max(1, 77 // 4) + 1, jnp.int32)
        _ctx_1024P = jax.random.normal(jax.random.fold_in(_rk, 11), (64, 16, 128), jnp.float32)
        _ctx_1024c = jax.random.dirichlet(jax.random.fold_in(_rk, 511), 0.3 * jnp.ones((16,), jnp.float32), (64, 77))
        _ctx_1024t = jnp.einsum('bsk,bkd->bsd', _ctx_1024c, _ctx_1024P)
        _ctx_1024t = _ctx_1024t * jax.lax.rsqrt(jnp.mean(jnp.square(_ctx_1024t)) + 1e-12) * 0.953939
        ctx_1024 = -1.52775e-05 + 0.999936 * (_ctx_1024t + 0.3 * jax.random.normal(jax.random.fold_in(_rk, 611), (64, 77, 128), jnp.float32))
        return (x, ctx_1024)
    x, ctx_1024 = _rec_inputs()

    def _L0_attn_setup():
        import jax, jax.numpy as jnp
        import numpy as np
        B, S, H = (8, 128, 128)
        HEADS = 8
        HD = H // HEADS
        LAMBDA_INIT = 0.8
        LN_EPS = 1e-05
        key = jax.random.key(seed)
        ks = jax.random.split(key, 16)
        xavier = float(np.sqrt(6.0 / (H + H)))
        inp = {'hidden_states': jax.random.normal(ks[0], (B, S, H), dtype=jnp.float32), 'Wq': jax.random.uniform(ks[1], (H, H), jnp.float32, -xavier, xavier), 'bq': jnp.zeros((H,), jnp.float32), 'Wk': jax.random.uniform(ks[2], (H, H), jnp.float32, -xavier, xavier), 'bk': jnp.zeros((H,), jnp.float32), 'Wv': jax.random.uniform(ks[3], (H, H), jnp.float32, -xavier, xavier), 'bv': jnp.zeros((H,), jnp.float32), 'Wo': jax.random.uniform(ks[4], (H, H), jnp.float32, -xavier, xavier), 'bo': jnp.zeros((H,), jnp.float32), 'lambda_q1': 0.02 * jax.random.normal(ks[5], (HD,), jnp.float32), 'lambda_k1': 0.02 * jax.random.normal(ks[6], (HD,), jnp.float32), 'lambda_q2': 0.02 * jax.random.normal(ks[7], (HD,), jnp.float32), 'lambda_k2': 0.02 * jax.random.normal(ks[8], (HD,), jnp.float32), 'ln_w': jnp.ones((H,), jnp.float32), 'ln_b': jnp.zeros((H,), jnp.float32)}
        return inp
    _L0_attn_all = _L0_attn_setup()
    _L0_attn_in = {k: v for k, v in _L0_attn_all.items() if k in ('Wq', 'bq', 'Wk', 'bk', 'Wv', 'bv', 'Wo', 'bo', 'lambda_q1', 'lambda_k1', 'lambda_q2', 'lambda_k2', 'ln_w', 'ln_b')}
    del _L0_attn_all

    def _L0_xattn_setup():
        import jax, jax.numpy as jnp
        import numpy as np
        D = 128
        NUM_ITERS = 3
        EPS = 1e-06
        SCALE = D ** (-0.5)

        def rmsnorm(x, w, eps=EPS):
            return x * jax.lax.rsqrt(jnp.mean(x * x, axis=-1, keepdims=True) + eps) * w

        def gru_cell(x, h, wih, whh, bih, bhh):
            gx = x @ wih.T + bih
            gh = h @ whh.T + bhh
            xr, xz, xn = jnp.split(gx, 3, axis=-1)
            hr, hz, hn = jnp.split(gh, 3, axis=-1)
            r = jax.nn.sigmoid(xr + hr)
            z = jax.nn.sigmoid(xz + hz)
            n = jnp.tanh(xn + r * hn)
            return (1.0 - z) * n + z * h
        key = jax.random.key(seed)
        ks = jax.random.split(key, 8)
        B, K, M, d = (8, 64, 512, D)
        w_std = d ** (-0.5)
        return {'slots': jax.random.normal(ks[0], (B, K, d), jnp.float32), 'P': jax.random.normal(ks[1], (B, M, d), jnp.float32), 'Wq': jax.random.normal(ks[2], (d, d), jnp.float32) * w_std, 'Wk': jax.random.normal(ks[3], (d, d), jnp.float32) * w_std, 'Wv': jax.random.normal(ks[4], (d, d), jnp.float32) * w_std, 'gru_wih': jax.random.normal(ks[5], (3 * d, d), jnp.float32) * w_std, 'gru_whh': jax.random.normal(ks[6], (3 * d, d), jnp.float32) * w_std, 'gru_bih': jnp.zeros((3 * d,), jnp.float32), 'gru_bhh': jnp.zeros((3 * d,), jnp.float32), 'slot_norm_w': jnp.ones((d,), jnp.float32), 'input_norm_w': jnp.ones((d,), jnp.float32)}
    _L0_xattn_all = _L0_xattn_setup()
    _L0_xattn_in = {k: v for k, v in _L0_xattn_all.items() if k in ('Wq', 'Wk', 'Wv', 'gru_wih', 'gru_whh', 'gru_bih', 'gru_bhh', 'slot_norm_w', 'input_norm_w')}
    del _L0_xattn_all

    def _L0_ffn_setup():
        import jax, jax.numpy as jnp
        import numpy as np
        DIM = 128
        NUM_EXPERTS = 8
        TOP_K = 2
        HIDDEN = 4 * DIM // TOP_K
        BS, SLEN = (1, 256)

        def _moe(x, gate_w, w_up, w_down, expert_bias):
            bs, slen, dim = x.shape
            xf = x.reshape(-1, dim)
            scores = jax.nn.sigmoid(xf @ gate_w.T)
            biased = scores + expert_bias
            _, sel = jax.lax.top_k(biased, TOP_K)
            top_scores = jnp.take_along_axis(scores, sel, axis=-1)

            def body(acc, ew):
                e, wu, wd = ew
                w_t = jnp.sum(jnp.where(sel == e, top_scores, 0.0), axis=-1)
                xe = xf * w_t[:, None]
                h = jnp.square(jax.nn.relu(xe @ wu.T))
                return (acc + h @ wd.T, None)
            out0 = jnp.zeros_like(xf)
            out, _ = jax.lax.scan(body, out0, (jnp.arange(NUM_EXPERTS), w_up, w_down))
            return out.reshape(bs, slen, dim)
        key = jax.random.key(seed)
        k0, k1, k2, k3 = jax.random.split(key, 4)
        x = jax.random.normal(k0, (BS, SLEN, DIM), dtype=jnp.float32)
        gate_w = jax.random.normal(k1, (NUM_EXPERTS, DIM), dtype=jnp.float32) * 0.02
        w_up = jax.random.normal(k2, (NUM_EXPERTS, HIDDEN, DIM), dtype=jnp.float32) * 0.02
        w_down = jax.random.normal(k3, (NUM_EXPERTS, DIM, HIDDEN), dtype=jnp.float32) * 0.02
        expert_bias = jnp.zeros((NUM_EXPERTS,), dtype=jnp.float32)
        return {'x': x, 'gate_w': gate_w, 'w_up': w_up, 'w_down': w_down, 'expert_bias': expert_bias}
    _L0_ffn_all = _L0_ffn_setup()
    _L0_ffn_in = {k: v for k, v in _L0_ffn_all.items() if k in ('gate_w', 'w_up', 'w_down', 'expert_bias')}
    del _L0_ffn_all

    def _L1_attn_setup():
        import jax, jax.numpy as jnp
        import numpy as np
        import math
        NUM_HEADS = 8
        EMB = 128
        HEAD_DIM = 128
        B, T = (1, 512)

        def sinusoidal_pe(T, d, dtype=jnp.float32):
            pos = jnp.arange(T, dtype=dtype)[:, None]
            inv_freq = jnp.exp(-math.log(10000.0) * jnp.arange(0, d, 2, dtype=dtype) / d)
            ang = pos * inv_freq[None, :]
            pe = jnp.zeros((T, d), dtype=dtype)
            pe = pe.at[:, 0::2].set(jnp.sin(ang))
            pe = pe.at[:, 1::2].set(jnp.cos(ang))
            return pe
        key = jax.random.key(seed)
        ks = jax.random.split(key, 6)
        s = lambda fan_in: 1.0 / math.sqrt(fan_in)
        x = jax.random.normal(ks[0], (B, T, EMB), dtype=jnp.float32)
        Wq = jax.random.normal(ks[1], (EMB, NUM_HEADS * HEAD_DIM), dtype=jnp.float32) * s(EMB)
        bq = jax.random.normal(ks[2], (NUM_HEADS * HEAD_DIM,), dtype=jnp.float32) * s(EMB)
        Wkv = jax.random.normal(ks[3], (EMB, 2 * HEAD_DIM), dtype=jnp.float32) * s(EMB)
        bkv = jax.random.normal(ks[4], (2 * HEAD_DIM,), dtype=jnp.float32) * s(EMB)
        Wo = jax.random.normal(ks[5], (NUM_HEADS * HEAD_DIM, EMB), dtype=jnp.float32) * s(NUM_HEADS * HEAD_DIM)
        return {'x': x, 'Wq': Wq, 'bq': bq, 'Wkv': Wkv, 'bkv': bkv, 'Wo': Wo}
    _L1_attn_all = _L1_attn_setup()
    _L1_attn_in = {k: v for k, v in _L1_attn_all.items() if k in ('Wq', 'bq', 'Wkv', 'bkv', 'Wo')}
    del _L1_attn_all

    def _L1_xattn_setup():
        import jax, jax.numpy as jnp
        import numpy as np
        D_MODEL = 128
        NUM_HEADS = 16
        STRIDE_LIST = [1, 2, 4, 8, 1, 2, 4, 8, 1, 2, 4, 8, 1, 2, 4, 8]
        HEAD_DIM = D_MODEL // NUM_HEADS
        key = jax.random.key(seed)
        ks = jax.random.split(key, 8)
        B, T, S = (4, 128, 512)
        w_scale = 0.02
        return {'decoder_input': jax.random.normal(ks[0], (B, T, D_MODEL), jnp.float32), 'encoder_output': jax.random.normal(ks[1], (B, S, D_MODEL), jnp.float32), 'Wq': jax.random.normal(ks[2], (D_MODEL, D_MODEL), jnp.float32) * w_scale, 'bq': jnp.zeros((D_MODEL,), jnp.float32), 'Wk': jax.random.normal(ks[3], (D_MODEL, D_MODEL), jnp.float32) * w_scale, 'bk': jnp.zeros((D_MODEL,), jnp.float32), 'Wv': jax.random.normal(ks[4], (D_MODEL, D_MODEL), jnp.float32) * w_scale, 'bv': jnp.zeros((D_MODEL,), jnp.float32), 'Wo': jax.random.normal(ks[5], (D_MODEL, D_MODEL), jnp.float32) * w_scale, 'bo': jnp.zeros((D_MODEL,), jnp.float32)}
    _L1_xattn_all = _L1_xattn_setup()
    _L1_xattn_in = {k: v for k, v in _L1_xattn_all.items() if k in ('Wq', 'bq', 'Wk', 'bk', 'Wv', 'bv', 'Wo', 'bo')}
    del _L1_xattn_all

    def _L1_ffn_setup():
        import jax, jax.numpy as jnp
        import numpy as np
        THRESHOLD = 0.1
        key = jax.random.key(seed)
        k1, k2, k3 = jax.random.split(key, 3)
        B, S, D, E = (4, 512, 128, 8)
        inputs = jax.random.normal(k1, (B, S, D), dtype=jnp.float32)
        gate_w = jax.random.normal(k2, (D, E), dtype=jnp.float32) * 0.02
        gate_b = jnp.zeros((E,), dtype=jnp.float32)
        expert_w = jax.random.normal(k3, (E, D, D), dtype=jnp.float32) * 0.02
        expert_b = jnp.zeros((E, D), dtype=jnp.float32)
        return {'inputs': inputs, 'gate_w': gate_w, 'gate_b': gate_b, 'expert_w': expert_w, 'expert_b': expert_b}
    _L1_ffn_all = _L1_ffn_setup()
    _L1_ffn_in = {k: v for k, v in _L1_ffn_all.items() if k in ('gate_w', 'gate_b', 'expert_w', 'expert_b')}
    del _L1_ffn_all
    return {'x': x, 'ctx_1024': ctx_1024, 'L0_attn_Wq': _L0_attn_in['Wq'], 'L0_attn_bq': _L0_attn_in['bq'], 'L0_attn_Wk': _L0_attn_in['Wk'], 'L0_attn_bk': _L0_attn_in['bk'], 'L0_attn_Wv': _L0_attn_in['Wv'], 'L0_attn_bv': _L0_attn_in['bv'], 'L0_attn_Wo': _L0_attn_in['Wo'], 'L0_attn_bo': _L0_attn_in['bo'], 'L0_attn_lambda_q1': _L0_attn_in['lambda_q1'], 'L0_attn_lambda_k1': _L0_attn_in['lambda_k1'], 'L0_attn_lambda_q2': _L0_attn_in['lambda_q2'], 'L0_attn_lambda_k2': _L0_attn_in['lambda_k2'], 'L0_attn_ln_w': _L0_attn_in['ln_w'], 'L0_attn_ln_b': _L0_attn_in['ln_b'], 'L0_xattn_Wq': _L0_xattn_in['Wq'], 'L0_xattn_Wk': _L0_xattn_in['Wk'], 'L0_xattn_Wv': _L0_xattn_in['Wv'], 'L0_xattn_gru_wih': _L0_xattn_in['gru_wih'], 'L0_xattn_gru_whh': _L0_xattn_in['gru_whh'], 'L0_xattn_gru_bih': _L0_xattn_in['gru_bih'], 'L0_xattn_gru_bhh': _L0_xattn_in['gru_bhh'], 'L0_xattn_slot_norm_w': _L0_xattn_in['slot_norm_w'], 'L0_xattn_input_norm_w': _L0_xattn_in['input_norm_w'], 'L0_ffn_gate_w': _L0_ffn_in['gate_w'], 'L0_ffn_w_up': _L0_ffn_in['w_up'], 'L0_ffn_w_down': _L0_ffn_in['w_down'], 'L0_ffn_expert_bias': _L0_ffn_in['expert_bias'], 'L1_attn_Wq': _L1_attn_in['Wq'], 'L1_attn_bq': _L1_attn_in['bq'], 'L1_attn_Wkv': _L1_attn_in['Wkv'], 'L1_attn_bkv': _L1_attn_in['bkv'], 'L1_attn_Wo': _L1_attn_in['Wo'], 'L1_xattn_Wq': _L1_xattn_in['Wq'], 'L1_xattn_bq': _L1_xattn_in['bq'], 'L1_xattn_Wk': _L1_xattn_in['Wk'], 'L1_xattn_bk': _L1_xattn_in['bk'], 'L1_xattn_Wv': _L1_xattn_in['Wv'], 'L1_xattn_bv': _L1_xattn_in['bv'], 'L1_xattn_Wo': _L1_xattn_in['Wo'], 'L1_xattn_bo': _L1_xattn_in['bo'], 'L1_ffn_gate_w': _L1_ffn_in['gate_w'], 'L1_ffn_gate_b': _L1_ffn_in['gate_b'], 'L1_ffn_expert_w': _L1_ffn_in['expert_w'], 'L1_ffn_expert_b': _L1_ffn_in['expert_b']}

def reference(x, ctx_1024, L0_attn_Wq, L0_attn_bq, L0_attn_Wk, L0_attn_bk, L0_attn_Wv, L0_attn_bv, L0_attn_Wo, L0_attn_bo, L0_attn_lambda_q1, L0_attn_lambda_k1, L0_attn_lambda_q2, L0_attn_lambda_k2, L0_attn_ln_w, L0_attn_ln_b, L0_xattn_Wq, L0_xattn_Wk, L0_xattn_Wv, L0_xattn_gru_wih, L0_xattn_gru_whh, L0_xattn_gru_bih, L0_xattn_gru_bhh, L0_xattn_slot_norm_w, L0_xattn_input_norm_w, L0_ffn_gate_w, L0_ffn_w_up, L0_ffn_w_down, L0_ffn_expert_bias, L1_attn_Wq, L1_attn_bq, L1_attn_Wkv, L1_attn_bkv, L1_attn_Wo, L1_xattn_Wq, L1_xattn_bq, L1_xattn_Wk, L1_xattn_bk, L1_xattn_Wv, L1_xattn_bv, L1_xattn_Wo, L1_xattn_bo, L1_ffn_gate_w, L1_ffn_gate_b, L1_ffn_expert_w, L1_ffn_expert_b):
    import jax
    import jax.numpy as jnp

    def _L0_attn_ref(hidden_states, Wq, bq, Wk, bk, Wv, bv, Wo, bo, lambda_q1, lambda_k1, lambda_q2, lambda_k2, ln_w, ln_b):
        import jax, jax.numpy as jnp
        import numpy as np
        B, S, H = (8, 128, 128)
        HEADS = 8
        HD = H // HEADS
        LAMBDA_INIT = 0.8
        LN_EPS = 1e-05
        b, s, h = hidden_states.shape
        q = hidden_states @ Wq + bq
        k = hidden_states @ Wk + bk
        v = hidden_states @ Wv + bv
        q = q.reshape(b, s, HEADS, HD).transpose(0, 2, 1, 3)
        k = k.reshape(b, s, HEADS, HD).transpose(0, 2, 1, 3)
        v = v.reshape(b, s, HEADS, HD).transpose(0, 2, 1, 3)
        scores = jnp.einsum('bhqd,bhkd->bhqk', q, k) / jnp.sqrt(jnp.float32(HD))
        attn = jax.nn.softmax(scores, axis=-1)
        half = HEADS // 2
        v1 = jnp.concatenate([v[:, :half], v[:, :half]], axis=1)
        v2 = jnp.concatenate([v[:, half:], v[:, half:]], axis=1)
        out1 = jnp.einsum('bhqk,bhkd->bhqd', attn, v1)
        out2 = jnp.einsum('bhqk,bhkd->bhqd', attn, v2)
        lam1 = jnp.exp(jnp.sum(lambda_q1 * lambda_k1))
        lam2 = jnp.exp(jnp.sum(lambda_q2 * lambda_k2))
        lam = lam1 - lam2 + LAMBDA_INIT
        attn_out = out1 - lam * out2
        attn_out = attn_out.transpose(0, 2, 1, 3).reshape(b, s, h)
        mu = jnp.mean(attn_out, axis=-1, keepdims=True)
        var = jnp.var(attn_out, axis=-1, keepdims=True)
        normed = (attn_out - mu) / jnp.sqrt(var + LN_EPS) * ln_w + ln_b
        attn_out = (1.0 - LAMBDA_INIT) * normed
        return attn_out @ Wo + bo

    def _L0_xattn_ref(slots, P, Wq, Wk, Wv, gru_wih, gru_whh, gru_bih, gru_bhh, slot_norm_w, input_norm_w):
        import jax, jax.numpy as jnp
        import numpy as np
        D = 128
        NUM_ITERS = 3
        EPS = 1e-06
        SCALE = D ** (-0.5)

        def rmsnorm(x, w, eps=EPS):
            return x * jax.lax.rsqrt(jnp.mean(x * x, axis=-1, keepdims=True) + eps) * w

        def gru_cell(x, h, wih, whh, bih, bhh):
            gx = x @ wih.T + bih
            gh = h @ whh.T + bhh
            xr, xz, xn = jnp.split(gx, 3, axis=-1)
            hr, hz, hn = jnp.split(gh, 3, axis=-1)
            r = jax.nn.sigmoid(xr + hr)
            z = jax.nn.sigmoid(xz + hz)
            n = jnp.tanh(xn + r * hn)
            return (1.0 - z) * n + z * h
        Pn = rmsnorm(P, input_norm_w)
        k_proj = Pn @ Wk.T
        v_proj = Pn @ Wv.T
        for _ in range(NUM_ITERS):
            sn = rmsnorm(slots, slot_norm_w)
            q_proj = sn @ Wq.T
            scores = jnp.einsum('bkd,bmd->bkm', q_proj, k_proj) * SCALE
            attn = jax.nn.softmax(scores, axis=-2)
            attn = attn / (jnp.sum(attn, axis=-1, keepdims=True) + EPS)
            updates = jnp.einsum('bkm,bmd->bkd', attn, v_proj)
            slots = gru_cell(updates, slots, gru_wih, gru_whh, gru_bih, gru_bhh)
        return slots

    def _L0_ffn_ref(x, gate_w, w_up, w_down, expert_bias):
        import jax, jax.numpy as jnp
        import numpy as np
        DIM = 128
        NUM_EXPERTS = 8
        TOP_K = 2
        HIDDEN = 4 * DIM // TOP_K
        BS, SLEN = (1, 256)

        def _moe(x, gate_w, w_up, w_down, expert_bias):
            bs, slen, dim = x.shape
            xf = x.reshape(-1, dim)
            scores = jax.nn.sigmoid(xf @ gate_w.T)
            biased = scores + expert_bias
            _, sel = jax.lax.top_k(biased, TOP_K)
            top_scores = jnp.take_along_axis(scores, sel, axis=-1)

            def body(acc, ew):
                e, wu, wd = ew
                w_t = jnp.sum(jnp.where(sel == e, top_scores, 0.0), axis=-1)
                xe = xf * w_t[:, None]
                h = jnp.square(jax.nn.relu(xe @ wu.T))
                return (acc + h @ wd.T, None)
            out0 = jnp.zeros_like(xf)
            out, _ = jax.lax.scan(body, out0, (jnp.arange(NUM_EXPERTS), w_up, w_down))
            return out.reshape(bs, slen, dim)
        return _moe(x, gate_w, w_up, w_down, expert_bias)

    def _L1_attn_ref(x, Wq, bq, Wkv, bkv, Wo):
        import jax, jax.numpy as jnp
        import numpy as np
        import math
        NUM_HEADS = 8
        EMB = 128
        HEAD_DIM = 128
        B, T = (1, 512)

        def sinusoidal_pe(T, d, dtype=jnp.float32):
            pos = jnp.arange(T, dtype=dtype)[:, None]
            inv_freq = jnp.exp(-math.log(10000.0) * jnp.arange(0, d, 2, dtype=dtype) / d)
            ang = pos * inv_freq[None, :]
            pe = jnp.zeros((T, d), dtype=dtype)
            pe = pe.at[:, 0::2].set(jnp.sin(ang))
            pe = pe.at[:, 1::2].set(jnp.cos(ang))
            return pe
        Bsz, Tlen, E = x.shape
        q = (x @ Wq + bq).reshape(Bsz, Tlen, NUM_HEADS, HEAD_DIM)
        kv = x @ Wkv + bkv
        k, v = (kv[..., :HEAD_DIM], kv[..., HEAD_DIM:])
        q = jnp.transpose(q, (0, 2, 1, 3))
        pe = sinusoidal_pe(Tlen, HEAD_DIM, x.dtype)
        q = q + pe[None, None, :, :]
        k = k + pe[None, :, :]
        scale = 1.0 / math.sqrt(HEAD_DIM)
        scores = jnp.einsum('bhqd,bkd->bhqk', q, k) * scale
        causal = jnp.tril(jnp.ones((Tlen, Tlen), dtype=bool))
        scores = jnp.where(causal[None, None, :, :], scores, jnp.finfo(scores.dtype).min)
        probs = jax.nn.softmax(scores, axis=-1)
        attn = jnp.einsum('bhqk,bkd->bhqd', probs, v)
        out = jnp.transpose(attn, (0, 2, 1, 3)).reshape(Bsz, Tlen, NUM_HEADS * HEAD_DIM)
        return out @ Wo

    def _L1_xattn_ref(decoder_input, encoder_output, Wq, bq, Wk, bk, Wv, bv, Wo, bo):
        import jax, jax.numpy as jnp
        import numpy as np
        D_MODEL = 128
        NUM_HEADS = 16
        STRIDE_LIST = [1, 2, 4, 8, 1, 2, 4, 8, 1, 2, 4, 8, 1, 2, 4, 8]
        HEAD_DIM = D_MODEL // NUM_HEADS
        B, T, _ = decoder_input.shape
        S = encoder_output.shape[1]
        Q = decoder_input @ Wq.T + bq
        K = encoder_output @ Wk.T + bk
        V = encoder_output @ Wv.T + bv
        Q = Q.reshape(B, T, NUM_HEADS, HEAD_DIM).transpose(0, 2, 1, 3)
        K = K.reshape(B, S, NUM_HEADS, HEAD_DIM).transpose(0, 2, 1, 3)
        V = V.reshape(B, S, NUM_HEADS, HEAD_DIM).transpose(0, 2, 1, 3)
        scale = 1.0 / HEAD_DIM ** 0.5
        head_outs = []
        for h in range(NUM_HEADS):
            s = STRIDE_LIST[h]
            K_h = K[:, h, ::s, :]
            V_h = V[:, h, ::s, :]
            scores = jnp.einsum('btd,bsd->bts', Q[:, h], K_h) * scale
            attn = jax.nn.softmax(scores, axis=-1)
            head_outs.append(jnp.einsum('bts,bsd->btd', attn, V_h))
        out = jnp.stack(head_outs, axis=2).reshape(B, T, D_MODEL)
        return out @ Wo.T + bo

    def _L1_ffn_ref(inputs, gate_w, gate_b, expert_w, expert_b):
        import jax, jax.numpy as jnp
        import numpy as np
        THRESHOLD = 0.1
        d = inputs.shape[-1]
        x = inputs.reshape(-1, d)
        gate_logits = jax.nn.softmax(x @ gate_w + gate_b, axis=-1)
        selected = (gate_logits >= THRESHOLD).astype(x.dtype)
        weights = gate_logits * selected
        wsum = jnp.sum(weights, axis=-1, keepdims=True)
        weights = weights / jnp.where(wsum == 0, jnp.ones_like(wsum), wsum)
        E = expert_w.shape[0]
        out = jnp.zeros((x.shape[0], expert_w.shape[-1]), dtype=x.dtype)
        for e in range(E):
            out = out + weights[:, e:e + 1] * (x @ expert_w[e] + expert_b[e])
        return out.reshape(*inputs.shape[:-1], out.shape[-1])
    x = x + _L0_attn_ref(_layernorm(x, axis=-1), L0_attn_Wq, L0_attn_bq, L0_attn_Wk, L0_attn_bk, L0_attn_Wv, L0_attn_bv, L0_attn_Wo, L0_attn_bo, L0_attn_lambda_q1, L0_attn_lambda_k1, L0_attn_lambda_q2, L0_attn_lambda_k2, L0_attn_ln_w, L0_attn_ln_b)
    x = x + _L0_xattn_ref(_layernorm(x, axis=-1), ctx_1024, L0_xattn_Wq, L0_xattn_Wk, L0_xattn_Wv, L0_xattn_gru_wih, L0_xattn_gru_whh, L0_xattn_gru_bih, L0_xattn_gru_bhh, L0_xattn_slot_norm_w, L0_xattn_input_norm_w)
    x = x + _L0_ffn_ref(_layernorm(x, axis=-1), L0_ffn_gate_w, L0_ffn_w_up, L0_ffn_w_down, L0_ffn_expert_bias)
    x = x + _L1_attn_ref(_layernorm(x, axis=-1), L1_attn_Wq, L1_attn_bq, L1_attn_Wkv, L1_attn_bkv, L1_attn_Wo)
    x = x + _L1_xattn_ref(_layernorm(x, axis=-1), ctx_1024, L1_xattn_Wq, L1_xattn_bq, L1_xattn_Wk, L1_xattn_bk, L1_xattn_Wv, L1_xattn_bv, L1_xattn_Wo, L1_xattn_bo)
    x = x + _L1_ffn_ref(_layernorm(x, axis=-1), L1_ffn_gate_w, L1_ffn_gate_b, L1_ffn_expert_w, L1_ffn_expert_b)
    return x

_drawn_inputs = setup_inputs


def setup_inputs(seed=0):
    import zlib

    import numpy as np

    out = dict(_drawn_inputs(seed))
    spreads = {'L0_attn_bq': (0.0, 0.451),
     'L0_attn_bk': (0.0, 2.0),
     'L0_attn_bv': (0.0, 0.1),
     'L0_attn_bo': (0.0, 0.1),
     'L0_attn_ln_w': (1.0, 0.2),
     'L0_attn_ln_b': (0.0, 0.386),
     'L0_xattn_gru_bih': (0.0, 0.1),
     'L0_xattn_gru_bhh': (0.0, 0.1),
     'L0_xattn_slot_norm_w': (1.0, 0.6),
     'L0_xattn_input_norm_w': (1.0, 0.2),
     'L0_ffn_expert_bias': (0.0, 0.8),
     'L1_xattn_bq': (0.0, 2.0),
     'L1_xattn_bk': (0.0, 2.0),
     'L1_xattn_bv': (0.0, 2.0),
     'L1_xattn_bo': (0.0, 0.491),
     'L1_ffn_gate_b': (0.0, 2.0),
     'L1_ffn_expert_b': (0.0, 1.069)}
    factors = {'L0_attn_lambda_q1': 26.807,
     'L0_attn_lambda_k1': 8.0,
     'L0_attn_lambda_q2': 8.0,
     'L0_attn_lambda_k2': 8.0,
     'L0_ffn_gate_w': 8.0,
     'L0_ffn_w_up': 8.0,
     'L0_ffn_w_down': 8.0,
     'L1_attn_bq': 12.562,
     'L1_xattn_Wq': 32.308,
     'L1_xattn_Wk': 30.11,
     'L1_xattn_Wv': 7.649,
     'L1_attn_bkv': 3.532,
     'L1_ffn_gate_w': 5.891,
     'L1_ffn_expert_w': 3.47}
    for name, (base, spread) in spreads.items():
        noise = np.random.default_rng([zlib.crc32(name.encode()), seed]).standard_normal(out[name].shape)
        drawn = base * np.exp(spread * noise) if base else spread * noise
        out[name] = jnp.asarray(drawn.astype(out[name].dtype))
    for name, factor in factors.items():
        out[name] = (out[name] * factor).astype(out[name].dtype)
    return out
```

```python
from contextlib import ExitStack

import concourse.bass as bass
from concourse import mybir

ALU = mybir.AluOpType
ACT = mybir.ActivationFunctionType
AX = mybir.AxisListType
F32 = mybir.dt.float32
BF16 = mybir.dt.bfloat16
U32 = mybir.dt.uint32

NS, T, D, MC = 64, 128, 128, 77
GB = 4
NG = NS // GB
GT = GB * T
GM = GB * MC
NE, HID = 8, 256
NCH = NE * HID // 128
H0, HD0 = 8, 16
H1 = 8
HX, HDX = 16, 8
NCLS = 4
NK = [-(-MC // (1 << c)) for c in range(NCLS)]
OFF = [4 * sum(NK[:c]) for c in range(NCLS + 1)]
JX = OFF[NCLS]
JT = [(i, min(128, JX - i)) for i in range(0, JX, 128)]
LN_EPS, RMS_EPS, LAMBDA_INIT = 1e-5, 1e-6, 0.8

(V_BQ, V_BK, V_BIH, V_BHH, V_WS, V_WIN, V_LNW, V_LNB, V_BQ1, V_BK1, V_BV1, V_XBQ, V_XBK, V_XBV) = (
    0, 1, 2, 5, 8, 9, 10, 11, 12, 20, 21, 22, 23, 24)
NV = 25
STEPS = (46, 93)


def build(nc, a, out):
    with ExitStack() as ctx:
        def sb(name, shape, dt=F32):
            return ctx.enter_context(nc.sbuf_tensor(name, shape, dt))

        def sem(name):
            return ctx.enter_context(nc.semaphore(name))

        ident = sb("ident", [128, 128])
        ident16 = sb("ident16", [128, 128], BF16)
        cmask16 = sb("cmask16", [128, 512], BF16)
        peT = sb("peT", [128, 128])
        sel = sb("sel", [MC, JX])
        vmask = sb("vmask", [128, len(JT), 128])
        kmask = sb("kmask", [128, NCLS, 4])
        hmask = sb("hmask", [128, H0])
        iota8 = sb("iota8", [128, NE])
        mhalf = sb("mhalf", [128, GB])
        held = sb("held", [1, 1])
        vrow = sb("vrow", [NV, 128])
        vcol = sb("vcol", [128, NV])
        rzb = sb("rzb", [128, 2])
        wq0 = sb("wq0", [128, 128])
        wk0 = sb("wk0", [128, 128])
        wv0 = sb("wv0", [128, 128])
        wvc = sb("wvc", [128, 64])
        woe = sb("woe", [128, 128])
        bvc = sb("bvc", [128, 64])
        cb1 = sb("cb1", [128, 128])
        lam_in = sb("lam_in", [128, 4, HD0])
        lam_pr = sb("lam_pr", [128, 2, HD0])
        lam_s = sb("lam_s", [128, 2])
        lam_e = sb("lam_e", [128, 2])
        nlam = sb("nlam", [128, 1])
        whh = sb("whh", [128, 384])
        wqk = sb("wqk", [128, 128])
        wvi = sb("wvi", [128, 384])
        mgate = sb("mgate", [128, NE])
        ebias = sb("ebias", [128, NE])
        wup = sb("wup", [128, NE * HID])
        wdn = sb("wdn", [128, NCH, 128])
        wq1 = sb("wq1", [128, H1 * 128])
        wkv1 = sb("wkv1", [128, 256])
        wo1 = sb("wo1", [128, H1, 128])
        ywq = sb("ywq", [128, 128])
        ywk = sb("ywk", [128, 128])
        ywv = sb("ywv", [128, 128])
        ywo = sb("ywo", [128, 128])
        ybo = sb("ybo", [128, 128])
        fgate = sb("fgate", [128, NE])
        fgb = sb("fgb", [128, NE])
        fw = sb("fw", [128, NE, 128])
        fb = sb("fb", [NE, 128])

        xin = sb("xin", [128, GB, D])
        cin = sb("cin", [MC, GB, D])
        xc = sb("xc", [128, GB, D])
        x1 = sb("x1", [128, GB, D])
        x2 = sb("x2", [128, GB, D])
        a_st = sb("a_st", [128, GB, 6])
        a_mv = sb("a_mv", [128, GB, 2])
        a_ve = sb("a_ve", [128, GB])
        a_rstd = sb("a_rstd", [128, GB])
        a_xn = sb("a_xn", [128, GB, D])
        a_xnT = sb("a_xnT", [128, GB, T])
        css = sb("css", [MC, GB])
        cve = sb("cve", [MC, GB])
        crs = sb("crs", [MC, GB])
        cnT = sb("cnT", [128, GM])
        kq = sb("kq", [128, GB, MC])
        vw = sb("vw", [MC, GB, 384])
        qT = sb("qT", [128, GB, T])
        kT = sb("kT", [128, GB, T])
        a_kbd = sb("a_kbd", [128, 2, H0, T])
        vaug = sb("vaug", [128, GB, 4, HD0 + 1])
        a_mx = sb("a_mx", [128, H0])
        a_ss = sb("a_ss", [128, H0, T])
        a_p = sb("a_p", [128, H0, T])
        a_pt = sb("a_pt", [128, H0, T])
        cmask = a_p[:, 0:4, :].rearrange("p h t -> p (h t)")
        wo0, lnb, bv0, xwq = (a_ss[:, i, :] for i in range(4))
        xwk, xwv = a_ss[:, 4, :], a_ss[:, 5, :]
        wih = a_pt[:, 0:3, :].rearrange("p h t -> p (h t)")
        a_rd = sb("a_rd", [128, 2 * H0])
        a_o = sb("a_o", [128, GB, D])
        hT = sb("hT", [128, GT])
        s_sq = sb("s_sq", [128, GB])
        s_ve = sb("s_ve", [128, GB])
        s_rs = sb("s_rs", [128, GB])
        sn = sb("sn", [128, GB, D])
        snT = sb("snT", [128, GB, T])
        s_mx = sb("s_mx", [MC, GB])
        s_ex = sb("s_ex", [MC, GB, T])
        s_e = sb("s_e", [MC, GB, T])
        s_sum = sb("s_sum", [MC, GB])
        s_rsum = sb("s_rsum", [MC, GB])
        s_at = sb("s_at", [MC, GB, T])
        s_row = sb("s_row", [128, GB])
        s_rowe = sb("s_rowe", [128, GB])
        s_rrow = sb("s_rrow", [128, GB])
        s_an = sb("s_an", [128, GB, MC])
        s_anT = sb("s_anT", [MC, GB, T])
        g_tr = sb("g_tr", [128, GT])
        g_tz = sb("g_tz", [128, GT])
        g_q = sb("g_q", [128, GT])
        g_n = sb("g_n", [128, GT])
        g_d = sb("g_d", [128, GT])
        a_junk = g_d[:].rearrange("p (b t) -> p b t", b=GB)
        cn = sn[0:MC, :, :]

        cT = sb("cT", [128, GB, MC])
        b_st = sb("b_st", [128, GB, 6])
        b_mv = sb("b_mv", [128, GB, 2])
        b_ve = sb("b_ve", [128, GB])
        b_rstd = sb("b_rstd", [128, GB])
        b_xn = sb("b_xn", [128, GB, D])
        b_xnT = sb("b_xnT", [128, GB, T])
        m_t = sb("m_t", [128, GB, NE])
        m_s = sb("m_s", [128, GB, NE])
        m_b = sb("m_b", [128, GB, NE])
        m_top = sb("m_top", [128, GB, 8])
        m_ix = sb("m_ix", [128, GB, 8], U32)
        m_ixf = sb("m_ixf", [128, GB, 8])
        m_1 = sb("m_1", [128, GB, NE])
        m_2 = sb("m_2", [128, GB, NE])
        m_w = sb("m_w", [128, GB, NE])
        m_w2 = sb("m_w2", [128, GB, NE])
        b_sp = sb("b_sp", [128, 2, H1, T])
        m_r = b_sp[:].rearrange("p k h t -> p (k h t)").rearrange("p (c t) -> p c t", c=4)
        m_h = sb("m_h", [128, NCH, GT])
        x3 = sb("x3", [128, GB, D])
        x4 = sb("x4", [128, GB, D])
        x4b = sb("x4b", [128, GB, D])
        x5 = sb("x5", [128, GB, D])
        y = sb("y", [128, GB, D])
        m_flat = m_h[:].rearrange("p c t -> p (c t)")
        q1 = m_flat[:, 0:H1 * GT].rearrange("p (h t) -> p h t", h=H1)
        kbd = m_flat[:, 0:GB * JX].rearrange("p (b j) -> p b j", b=GB)
        vbd = m_flat[:, H1 * GT:H1 * GT + len(JT) * GT].rearrange("p (i b d) -> p i b d", i=len(JT), b=GB)
        k1 = sb("k1", [128, GB, T])
        v1 = sb("v1", [128, GB, D])
        b_mx = sb("b_mx", [128, H1])
        b_ss, b_p = b_sp[:, 0, :, :], b_sp[:, 1, :, :]
        b_sum = sb("b_sum", [128, H1])
        b_rs = sb("b_rs", [128, H1])
        b_pn = sb("b_pn", [128, H1, T])
        b_pt = sb("b_pt", [128, H1, T])
        b_ot = sb("b_ot", [128, H1, T])
        qx = sb("qx", [128, GB, T])
        kx = sb("kx", [128, GB, MC])
        vx = sb("vx", [MC, GB, D])
        x_mx = sb("x_mx", [128, HX])
        x_ss = b_ss.rearrange("p h t -> p (h t)")[:, 0:JX]
        x_p = b_p.rearrange("p h t -> p (h t)")[:, 0:JX]
        x_sum = sb("x_sum", [128, HX])
        x_rs = sb("x_rs", [128, HX])
        x_pn = b_pn[:].rearrange("p h t -> p (h t)")[:, 0:JX]
        x_pt = b_pt[:, 0:len(JT), :]
        x_oT = sb("x_oT", [128, GB, T])
        f_l = sb("f_l", [128, GB, NE])
        f_mx = sb("f_mx", [128, GB])
        f_s = sb("f_s", [128, GB, NE])
        f_e = sb("f_e", [128, GB, NE])
        f_sum = sb("f_sum", [128, GB])
        f_r = sb("f_r", [128, GB])
        f_g = sb("f_g", [128, GB, NE])
        f_w0 = sb("f_w0", [128, GB, NE])
        f_ws = sb("f_ws", [128, GB])
        f_z = sb("f_z", [128, GB])
        f_wd = sb("f_wd", [128, GB])
        f_wr = sb("f_wr", [128, GB])
        f_w = sb("f_w", [128, GB, NE])
        f_wT = sb("f_wT", [NE, GB, T])

        PA = ctx.enter_context(nc.psum_tensor("PA", [128, 4, 512], F32))
        PB = ctx.enter_context(nc.psum_tensor("PB", [128, 4, 512], F32))

        w_loaded = sem("w_loaded")
        set_vec = sem("set_vec")
        set_pe = sem("set_pe")
        set_act = sem("set_act")
        x_loaded, c_loaded, cT_loaded, out_done = (sem(n) for n in ("x_loaded", "c_loaded", "cT_loaded", "out_done"))
        x2_ready = sem("x2_ready")
        names_a = ("a_step css_r cve_r crs_r cn_r cnT_ps cnT_r kq_ps kq_r vw_ps vw_r xc_r var_r rstd_r xn_r "
                   "xnT_ps xnT_r qk_ps qT_r kT_r kbd_r v_ps v_r s_ps ss_r p_r pt_ps pt_r pv_ps o_r y_ps sq_r sve_r srs_r "
                   "sn_r snT_ps snT_r sc_ps ex_r e_r at_r at_ps an_r anT_ps anT_r g_ps tr_r tz_r pre_r n_r h_r hp_ps")
        A = {n: sem("a_" + n) for n in names_a.split()}
        names_b = ("b_step var_r rstd_r xn_r xnT_ps xnT_r mg_ps mt_r up_ps relu_r sqv_r sqp_r dn_ps x3_r "
                   "q_ps q_r k_ps k_r v_ps v_r s_ps ss_r p_r rs_r pn_r pt_ps pt_r ot_ps ot_r wo_ps x4_r "
                   "xq_ps xk_ps xv_ps xq_r xk_r xv_r kbd_r vbd_ps vbd_r xs_ps xss_r xp_r xrs_r xpn_r xpt_ps xpt_r "
                   "xo_ps xo_r xy_ps x4b_r fg_ps fs_r fe_r fw_r fwT_ps fwT_r fb_ps ff_ps y_r")
        B = {n: sem("b_" + n) for n in names_b.split()}

        ones_row = lambda ap, n: ap.rearrange("(o d) -> o d", o=1).to_broadcast([n, ap.shape[0]])
        loads = [
            (ident[:], a["c_ident"]), (cmask, a["c_cmask"]), (peT[:], a["c_peT"]), (sel[:], a["c_sel"]),
            (vmask[:], a["c_vmask"]), (kmask[:], a["c_kmask"]), (iota8[:], a["c_iota8"]),
            (hmask[:], a["c_hmask"]),
            (vrow[V_BIH:V_BIH + 3, :], a["L0_xattn_gru_bih"].rearrange("(r c) -> r c", r=3)),
            (vrow[V_BHH:V_BHH + 3, :], a["L0_xattn_gru_bhh"].rearrange("(r c) -> r c", r=3)),
            (vrow[V_WS:V_WS + 1, :], ones_row(a["L0_xattn_slot_norm_w"], 1)),
            (vrow[V_WIN:V_WIN + 1, :], ones_row(a["L0_xattn_input_norm_w"], 1)),
            (vrow[V_LNW:V_LNW + 1, :], ones_row(a["L0_attn_ln_w"], 1)),
            (vrow[V_LNB:V_LNB + 1, :], ones_row(a["L0_attn_ln_b"], 1)),
            (vrow[V_BQ1:V_BQ1 + 8, :], a["L1_attn_bq"].rearrange("(r c) -> r c", r=8)),
            (vrow[V_BK1:V_BK1 + 2, :], a["L1_attn_bkv"].rearrange("(r c) -> r c", r=2)),
            (vrow[V_XBQ:V_XBQ + 1, :], ones_row(a["L1_xattn_bq"], 1)),
            (vrow[V_XBK:V_XBK + 1, :], ones_row(a["L1_xattn_bk"], 1)),
            (vrow[V_XBV:V_XBV + 1, :], ones_row(a["L1_xattn_bv"], 1)),
            (vrow[V_BQ:V_BQ + 1, :], ones_row(a["L0_attn_bq"], 1)),
            (vrow[V_BK:V_BK + 1, :], ones_row(a["L0_attn_bk"], 1)),
            (wq0[:], a["L0_attn_Wq"]), (wk0[:], a["L0_attn_Wk"]), (wv0[:], a["L0_attn_Wv"]), (wo0, a["L0_attn_Wo"]),
            (bv0, ones_row(a["L0_attn_bv"], 128)), (cb1[:], ones_row(a["L0_attn_bo"], 128)),
            (xwq, a["L0_xattn_Wq"]), (xwk, a["L0_xattn_Wk"]), (xwv, a["L0_xattn_Wv"]),
            (wih, a["L0_xattn_gru_wih"]), (whh[:], a["L0_xattn_gru_whh"]),
            (mgate[:], a["L0_ffn_gate_w"]), (ebias[:], ones_row(a["L0_ffn_expert_bias"], 128)),
            (wup[:], a["L0_ffn_w_up"]), (wdn[:], a["L0_ffn_w_down"]),
            (wq1[:], a["L1_attn_Wq"]), (wkv1[:], a["L1_attn_Wkv"]), (wo1[:], a["L1_attn_Wo"]),
            (ywq[:], a["L1_xattn_Wq"]), (ywk[:], a["L1_xattn_Wk"]), (ywv[:], a["L1_xattn_Wv"]),
            (ywo[:], a["L1_xattn_Wo"]), (ybo[:], ones_row(a["L1_xattn_bo"], 128)),
            (fgate[:], a["L1_ffn_gate_w"]), (fgb[:], ones_row(a["L1_ffn_gate_b"], 128)),
            (fw[:], a["L1_ffn_expert_w"]), (fb[:], a["L1_ffn_expert_b"]),
        ] + [(lam_in[:, i, :], ones_row(a["L0_attn_lambda_" + n], 128)) for i, n in enumerate(("q1", "k1", "q2", "k2"))]
        N_LOADS = 16 * len(loads)

        block = ctx.enter_context(nc.Block())

        @block.sync
        def _(sp):
            for dst, src in loads:
                if dst is loads[8][0]:
                    sp.wait_ge(set_vec, 1)
                sp.dma_start(dst, src).then_inc(w_loaded, 16)

            def load_x(g):
                sp.dma_start(xin[:], a["x"][:, bass.ds(g * GB, GB), :]).then_inc(x_loaded, 16)
                sp.dma_start(cin[:], a["ctx_tok"][:, bass.ds(g * GB, GB), :]).then_inc(c_loaded, 16)

            def load_cT(g):
                sp.dma_start(cT[:], a["ctx_feat"][:, bass.ds(g * GB, GB), :]).then_inc(cT_loaded, 16)

            def store(g):
                sp.wait_ge(B["y_r"], 8 * g + 8)
                sp.dma_start(out[:, bass.ds(g * GB, GB), :], y[:]).then_inc(out_done, 16)

            sp.sem_inc(out_done, 16)
            load_x(0)
            load_cT(0)
            with sp.Fori(1, NG) as g:
                sp.wait_ge(A["xn_r"], 12 * g - 8)
                sp.wait_ge(A["xc_r"], g)
                sp.wait_ge(A["cn_r"], g)
                load_x(g)
                sp.wait_ge(B["xv_ps"], g)
                load_cT(g)
                store(g - 1)
            store(NG - 1)
            sp.wait_ge(out_done, 16 * NG + 16)

        @block.tensor
        def _(pe):
            mm, tp = nc.tensor.matmul, nc.tensor.transpose

            pe.wait_ge(w_loaded, N_LOADS)
            tp(PA[:, 0, 0:NV], vrow[:], ident[0:NV, 0:NV]).then_inc(set_pe, 1)
            mm(PA[:, 1, 0:128], xwk, xwq, start=True, stop=True).then_inc(set_pe, 1)
            mm(PA[:, 2, 0:384], xwv, wih, start=True, stop=True).then_inc(set_pe, 1)
            pe.wait_ge(set_vec, 12)
            mm(PA[:, 3, 0:128], lnb, wo0, start=True, stop=True).then_inc(set_pe, 1)
            pe.wait_ge(set_vec, 17)

            def a_ctx(g):
                pe.wait_ge(A["cn_r"], g + 1)
                for b in range(GB):
                    last = tp(PA[:, 1, b * MC:b * MC + MC], cn[:, b, :], ident[0:MC, 0:MC])
                last.then_inc(A["cnT_ps"], 1)
                pe.wait_ge(A["cnT_r"], g + 1)
                mm(PA[:, 2, 0:GM], wqk[:], cnT[:], start=True, stop=True).then_inc(A["kq_ps"], 1)
                for b, bank in enumerate((3, 0, 1, 2)):
                    if b == 3:
                        pe.wait_ge(A["kq_r"], g + 1)
                    mm(PA[0:MC, bank, 0:384], cnT[:, b * MC:b * MC + MC], wvi[:], start=True,
                       stop=True).then_inc(A["vw_ps"], 1)

            def a_norm_T(g, u, bank):
                for b in range(GB):
                    pe.wait_ge(A["xn_r"], 12 * g + 4 * u + b + 1)
                    last = tp(PA[:, bank, b * T:b * T + T], a_xn[:, b, :], ident[:])
                last.then_inc(A["xnT_ps"], 1)

            def a_qkv(g):
                pe.wait_ge(A["vw_r"], 4 * g + 4)
                a_norm_T(g, 0, 0)
                pe.wait_ge(A["xnT_r"], 3 * g + 1)
                for w, bank in ((wq0, 1), (wk0, 2)):
                    mm(PA[:, bank, :], w[:], a_xnT[:].rearrange("p b t -> p (b t)"), start=True,
                       stop=True).then_inc(A["qk_ps"], 1)
                for b in range(GB):
                    last = mm(PA[:, 3, b * 64:b * 64 + 64], a_xnT[:, b, :], wvc[:], start=True, stop=True)
                last.then_inc(A["v_ps"], 1)

            def a_scores(g, b):
                if b == 0:
                    pe.wait_ge(A["qT_r"], g + 1)
                else:
                    pe.wait_ge(A["ss_r"], 4 * g + b)
                pe.wait_ge(A["kbd_r"], 4 * g + b + 1)
                for t in range(2):
                    last = mm(PA[:, t, :], qT[:, b, :],
                              a_kbd[:, b % 2, 4 * t:4 * t + 4, :].rearrange("p h t -> p (h t)"), start=True, stop=True)
                last.then_inc(A["s_ps"], 1)

            def a_pv(g, b):
                pe.wait_ge(A["p_r"], 4 * g + b + 1)
                for f in range(2):
                    if f == 1 or b > 0:
                        pe.wait_ge(A["pt_r"], 8 * g + 2 * b + f)
                    for h in range(4 * f, 4 * f + 4):
                        last = tp(PA[:, 2, (h % 4) * T:(h % 4) * T + T], a_p[:, h, :], ident[:])
                    last.then_inc(A["pt_ps"], 1)
                pe.wait_ge(A["pt_r"], 8 * g + 2 * b + 2)
                if b == 0:
                    pe.wait_ge(A["v_r"], g + 1)
                if b == 2:
                    pe.wait_ge(A["o_r"], 2 * g + 1)
                for h in range(H0):
                    c = (b % 2) * H0 * 17 + h * 17
                    last = mm(PA[:, 3, c:c + 17], a_pt[:, h, :], vaug[:, b, h % 4, :], start=True, stop=True)
                last.then_inc(A["pv_ps"], 1)

            def a_proj(g):
                a_norm_T(g, 1, 2)
                pe.wait_ge(A["xnT_r"], 3 * g + 2)
                for b in range(GB):
                    last = mm(PA[:, 0, b * T:b * T + T], a_xnT[:, b, :], woe[:], start=True, stop=True)
                last.then_inc(A["y_ps"], 1)
                a_norm_T(g, 2, 1)
                pe.wait_ge(A["xnT_r"], 3 * g + 3)

            def a_slot(g, t):
                u = 3 * g + t
                pe.wait_ge(A["sn_r"], u + 1)
                for b in range(GB):
                    last = tp(PA[:, 1, b * T:b * T + T], sn[:, b, :], ident[:])
                last.then_inc(A["snT_ps"], 1)
                mm(PA[:, 0, :], whh[:, 0:128], hT[:], start=True, stop=False, skip_group_check=True)
                pe.wait_ge(A["snT_r"], u + 1)
                for b in range(GB):
                    last = mm(PA[0:MC, 2, b * T:b * T + T], kq[:, b, :], snT[:, b, :], start=True, stop=True)
                last.then_inc(A["sc_ps"], 1)
                pe.wait_ge(A["at_r"], u + 1)
                for b in range(GB):
                    last = tp(PA[:, 3, b * MC:b * MC + MC], s_at[:, b, :], ident[0:MC, 0:MC])
                last.then_inc(A["at_ps"], 1)
                mm(PA[:, 2, :], whh[:, 128:256], hT[:], start=True, stop=False, skip_group_check=True)
                pe.wait_ge(A["an_r"], u + 1)
                for b in range(GB):
                    last = tp(PA[0:MC, 1, b * T:b * T + T], s_an[:, b, :], ident[:])
                last.then_inc(A["anT_ps"], 1)
                mm(PA[:, 3, :], whh[:, 256:384], hT[:], start=True, stop=True).then_inc(A["g_ps"], 1)
                pe.wait_ge(A["anT_r"], u + 1)
                for k, bank in ((0, 0), (1, 2), (2, 1)):
                    for b in range(GB):
                        last = mm(PA[:, bank, b * T:b * T + T], vw[:, b, 128 * k:128 * k + 128], s_anT[:, b, :],
                                  start=(k == 2), stop=True, skip_group_check=True)
                    last.then_inc(A["g_ps"], 1)
                pe.wait_ge(A["h_r"], u + 1)
                for b in range(GB):
                    last = tp(PA[:, 0, b * T:b * T + T], hT[:, b * T:b * T + T], ident[:])
                last.then_inc(A["hp_ps"], 1)

            def thread_a(g):
                a_ctx(g)
                a_qkv(g)
                a_scores(g, 0)
                for b in range(GB):
                    if b + 1 < GB:
                        a_scores(g, b + 1)
                    a_pv(g, b)
                a_proj(g)
                for t in range(3):
                    a_slot(g, t)

            def b_norm_T(g, u):
                for b in range(GB):
                    pe.wait_ge(B["xn_r"], 16 * g + 4 * u + b + 1)
                    last = tp(PB[:, 0, b * T:b * T + T], b_xn[:, b, :], ident[:])
                last.then_inc(B["xnT_ps"], 1)
                pe.wait_ge(B["xnT_r"], 4 * g + u + 1)

            xnT_all = b_xnT[:].rearrange("p b t -> p (b t)")

            def b_moe_up(g):
                b_norm_T(g, 0)
                for b in range(GB):
                    last = mm(PB[:, 1, b * NE:b * NE + NE], b_xnT[:, b, :], mgate[:], start=True, stop=True)
                last.then_inc(B["mg_ps"], 1)
                for c in range(NCH):
                    if c >= 2:
                        pe.wait_ge(B["relu_r"], NCH * g + c - 1)
                    mm(PB[:, 2 + c % 2, :], wup[:, 128 * c:128 * c + 128], xnT_all, start=True,
                       stop=True).then_inc(B["up_ps"], 1)

            def b_moe_down(g, b):
                if b == 0:
                    pe.wait_ge(B["sqv_r"], 8 * g + 8)
                    pe.wait_ge(B["sqp_r"], 8 * g + 8)
                    pe.wait_ge(B["mt_r"], g + 1)
                for f in range(2):
                    if b > 0:
                        pe.wait_ge(B["x3_r"], 8 * g + 2 * b - 1 + f)
                    for e in range(4 * f, 4 * f + 4):
                        for k in range(2):
                            last = mm(PB[:, f, (e % 4) * 128:(e % 4) * 128 + 128],
                                      m_h[:, 2 * e + k, b * T:b * T + T], wdn[:, 2 * e + k, :],
                                      start=(k == 0), stop=(k == 1))
                    last.then_inc(B["dn_ps"], 1)

            def b_qkv(g):
                b_norm_T(g, 1)
                mm(PB[:, 3, :], wkv1[:, 0:128], xnT_all, start=True, stop=True).then_inc(B["k_ps"], 1)
                for b in range(GB):
                    last = mm(PB[:, 0, b * T:b * T + T], b_xnT[:, b, :], wkv1[:, 128:256], start=True, stop=True)
                last.then_inc(B["v_ps"], 1)
                for h in range(H1):
                    if h >= 2:
                        pe.wait_ge(B["q_r"], 8 * g + h - 1)
                    mm(PB[:, 1 + h % 2, :], wq1[:, 128 * h:128 * h + 128], xnT_all, start=True,
                       stop=True).then_inc(B["q_ps"], 1)

            def b_scores(g, b):
                if b == 0:
                    pe.wait_ge(B["q_r"], 8 * g + 8)
                    pe.wait_ge(B["k_r"], g + 1)
                    pe.wait_ge(B["v_r"], g + 1)
                else:
                    pe.wait_ge(B["ss_r"], 4 * g + b)
                for f in range(2):
                    mm(PB[:, f, :], ident16[:], cmask16[:], start=True, stop=False, skip_group_check=True)
                    for h in range(4 * f, 4 * f + 4):
                        last = mm(PB[:, f, (h % 4) * T:(h % 4) * T + T], q1[:, h, b * T:b * T + T], k1[:, b, :],
                                  start=False, stop=True, skip_group_check=True)
                last.then_inc(B["s_ps"], 1)

            def b_pv(g, b):
                pe.wait_ge(B["pn_r"], 4 * g + b + 1)
                if b > 0:
                    pe.wait_ge(B["x4_r"], 4 * g + b)
                for f in range(2):
                    for h in range(4 * f, 4 * f + 4):
                        last = tp(PB[:, 2 + f, (h % 4) * T:(h % 4) * T + T], b_pn[:, h, :], ident[:])
                    last.then_inc(B["pt_ps"], 1)
                for f in range(2):
                    pe.wait_ge(B["pt_r"], 8 * g + 2 * b + f + 1)
                    mm(PB[:, 2 + f, :], v1[:, b, :], b_pt[:, 4 * f:4 * f + 4, :].rearrange("p h t -> p (h t)"),
                       start=True, stop=True).then_inc(B["ot_ps"], 1)
                pe.wait_ge(B["ot_r"], 8 * g + 2 * b + 2)
                for h in range(H1):
                    last = mm(PB[:, 2, 0:128], b_ot[:, h, :], wo1[:, h, :], start=(h == 0), stop=(h == H1 - 1))
                last.then_inc(B["wo_ps"], 1)

            def b_xqkv(g):
                b_norm_T(g, 2)
                mm(PB[:, 1, :], ywq[:], xnT_all, start=True, stop=True).then_inc(B["xq_ps"], 1)
                pe.wait_ge(cT_loaded, 16 * g + 16)
                mm(PB[:, 2, 0:GM], ywk[:], cT[:].rearrange("p b m -> p (b m)"), start=True,
                   stop=True).then_inc(B["xk_ps"], 1)
                for b in range(GB):
                    last = mm(PB[0:MC, 3, b * D:b * D + D], cT[:, b, :], ywv[:], start=True, stop=True)
                last.then_inc(B["xv_ps"], 1)
                pe.wait_ge(B["xk_r"], g + 1)
                pe.wait_ge(B["xv_r"], g + 1)
                for i, (j, w) in enumerate(JT):
                    if i >= 2:
                        pe.wait_ge(B["vbd_r"], 5 * g + i - 1)
                    mm(PB[0:w, 2 + i % 2, :], sel[:, j:j + w], vx[:].rearrange("p b d -> p (b d)"),
                       start=True, stop=True).then_inc(B["vbd_ps"], 1)

            def b_xscores(g, b):
                if b == 0:
                    pe.wait_ge(B["xq_r"], g + 1)
                    pe.wait_ge(B["kbd_r"], g + 1)
                else:
                    pe.wait_ge(B["xss_r"], 4 * g + b)
                mm(PB[:, 0, 0:OFF[1]], qx[:, b, :], kbd[:, b, 0:OFF[1]], start=True, stop=True)
                mm(PB[:, 1, 0:JX - OFF[1]], qx[:, b, :], kbd[:, b, OFF[1]:JX], start=True,
                   stop=True).then_inc(B["xs_ps"], 1)

            def b_xpv(g, b):
                if b == 0:
                    pe.wait_ge(B["vbd_r"], 5 * g + 5)
                else:
                    pe.wait_ge(B["xo_r"], 4 * g + b)
                pe.wait_ge(B["xpn_r"], 4 * g + b + 1)
                for i, (j, w) in enumerate(JT):
                    dst = PB[0:w, 2, i * T:i * T + T] if i < 4 else PB[0:w, 3, 0:T]
                    last = tp(dst, x_pn[:, j:j + w], ident[:])
                last.then_inc(B["xpt_ps"], 1)
                pe.wait_ge(B["xpt_r"], 4 * g + b + 1)
                for i, (j, w) in enumerate(JT):
                    last = mm(PB[:, 3, T:2 * T], vbd[0:w, i, b, :], x_pt[0:w, i, :], start=(i == 0),
                              stop=(i == len(JT) - 1))
                last.then_inc(B["xo_ps"], 1)

            def b_xout(g):
                pe.wait_ge(B["xo_r"], 4 * g + 4)
                for b in range(GB):
                    last = mm(PB[:, 0, b * T:b * T + T], x_oT[:, b, :], ywo[:], start=True, stop=True)
                last.then_inc(B["xy_ps"], 1)

            def b_ffn(g):
                b_norm_T(g, 3)
                for b in range(GB):
                    last = mm(PB[:, 1, b * NE:b * NE + NE], b_xnT[:, b, :], fgate[:], start=True, stop=True)
                last.then_inc(B["fg_ps"], 1)
                pe.wait_ge(B["fw_r"], g + 1)
                for b in range(GB):
                    last = tp(PB[0:NE, 1, b * T:b * T + T], f_w[:, b, :], ident[:])
                last.then_inc(B["fwT_ps"], 1)
                pe.wait_ge(B["fwT_r"], g + 1)
                for b in range(GB):
                    last = mm(PB[:, 0, b * T:b * T + T], f_wT[:, b, :], fb[:], start=True, stop=True)
                last.then_inc(B["fb_ps"], 1)
                for b in range(GB):
                    for f in range(2):
                        if b > 0:
                            pe.wait_ge(B["y_r"], 8 * g + 2 * b - 1 + f)
                        mm(PB[:, 2 + f, :], b_xnT[:, b, :], fw[:, 4 * f:4 * f + 4, :].rearrange("p e d -> p (e d)"),
                           start=True, stop=True).then_inc(B["ff_ps"], 1)

            def thread_b(g):
                b_moe_up(g)
                for b in range(GB):
                    b_moe_down(g, b)
                b_qkv(g)
                b_scores(g, 0)
                for b in range(GB):
                    if b + 1 < GB:
                        b_scores(g, b + 1)
                    b_pv(g, b)
                b_xqkv(g)
                b_xscores(g, 0)
                for b in range(GB):
                    if b + 1 < GB:
                        b_xscores(g, b + 1)
                    b_xpv(g, b)
                b_xout(g)
                b_ffn(g)

            thread_a(0)
            with pe.Fori(0, NG - 1) as g:
                thread_b(g)
                thread_a(g + 1)
            thread_b(NG - 1)

        @block.scalar
        def _(act):
            f = nc.scalar.activation

            act.wait_ge(set_vec, 3)
            f(lam_e[:], lam_s[:], ACT.Exp).then_inc(set_act, 1)
            act.wait_ge(set_vec, 17)

            def a_ctx(g):
                act.wait_ge(c_loaded, 16 * g + 16)
                for b in range(GB):
                    last = f(a_junk[0:MC, b, :], cin[:, b, :], ACT.Square, accum_out=css[:, b:b + 1])
                last.then_inc(A["css_r"], 1)
                act.wait_ge(A["cnT_ps"], g + 1)
                f(cnT[:], PA[:, 1, 0:GM], ACT.Copy).then_inc(A["cnT_r"], 1)
                for b, bank in enumerate((3, 0, 1, 2)):
                    act.wait_ge(A["vw_ps"], 4 * g + b + 1)
                    f(vw[:, b, :], PA[0:MC, bank, 0:384], ACT.Copy).then_inc(A["vw_r"], 1)

            def a_xnT_out(g, u, bank, dst):
                act.wait_ge(A["xnT_ps"], 3 * g + u + 1)
                f(dst, PA[:, bank, :], ACT.Copy).then_inc(A["xnT_r"], 1)

            def a_q(g):
                a_xnT_out(g, 0, 0, a_xnT[:].rearrange("p b t -> p (b t)"))
                act.wait_ge(A["qk_ps"], 2 * g + 1)
                f(qT[:].rearrange("p b t -> p (b t)"), PA[:, 1, :], ACT.Identity,
                  bias=vcol[:, V_BQ:V_BQ + 1]).then_inc(A["qT_r"], 1)

            def a_exp(g, b):
                act.wait_ge(A["ss_r"], 4 * g + b + 1)
                if b > 0:
                    act.wait_ge(A["pt_ps"], 8 * g + 2 * b)
                f(a_p[:], a_ss[:], ACT.Exp, scale=HD0 ** -0.5).then_inc(A["p_r"], 1)

            def a_pt_out(g, b):
                for h in range(2):
                    act.wait_ge(A["pt_ps"], 8 * g + 2 * b + h + 1)
                    if b > 0 and h == 0:
                        act.wait_ge(A["pv_ps"], 4 * g + b)
                    f(a_pt[:, 4 * h:4 * h + 4, :].rearrange("p h t -> p (h t)"), PA[:, 2, :],
                      ACT.Copy).then_inc(A["pt_r"], 1)

            def a_slot(g, t):
                u = 3 * g + t
                if t > 0:
                    act.wait_ge(A["hp_ps"], u)
                for b in range(GB):
                    src = a_xn[:, b, :] if t == 0 else PA[:, 0, b * T:b * T + T]
                    last = f(a_junk[:, b, :], src, ACT.Square, accum_out=s_sq[:, b:b + 1])
                last.then_inc(A["sq_r"], 1)
                act.wait_ge(A["snT_ps"], u + 1)
                f(snT[:].rearrange("p b t -> p (b t)"), PA[:, 1, :], ACT.Copy).then_inc(A["snT_r"], 1)
                act.wait_ge(A["ex_r"], u + 1)
                f(s_e[:], s_ex[:], ACT.Exp, scale=D ** -0.5).then_inc(A["e_r"], 1)
                act.wait_ge(A["anT_ps"], u + 1)
                f(s_anT[:].rearrange("p b t -> p (b t)"), PA[0:MC, 1, :], ACT.Copy).then_inc(A["anT_r"], 1)
                act.wait_ge(A["g_ps"], 4 * u + 2)
                f(g_tr[:], PA[:, 0, :], ACT.Tanh, scale=0.5, bias=rzb[:, 0:1]).then_inc(A["tr_r"], 1)
                act.wait_ge(A["g_ps"], 4 * u + 3)
                f(g_tz[:], PA[:, 2, :], ACT.Tanh, scale=0.5, bias=rzb[:, 1:2]).then_inc(A["tz_r"], 1)
                act.wait_ge(A["pre_r"], u + 1)
                f(g_n[:], g_q[:], ACT.Tanh, bias=vcol[:, V_BIH + 2:V_BIH + 3]).then_inc(A["n_r"], 1)

            def thread_a(g):
                a_ctx(g)
                a_q(g)
                a_exp(g, 0)
                for b in range(GB):
                    a_pt_out(g, b)
                    if b + 1 < GB:
                        a_exp(g, b + 1)
                a_xnT_out(g, 1, 2, a_xnT[:].rearrange("p b t -> p (b t)"))
                a_xnT_out(g, 2, 1, hT[:])
                for t in range(3):
                    a_slot(g, t)

            def b_xnT_out(g, u):
                act.wait_ge(B["xnT_ps"], 4 * g + u + 1)
                f(b_xnT[:].rearrange("p b t -> p (b t)"), PB[:, 0, :], ACT.Copy).then_inc(B["xnT_r"], 1)

            def b_moe(g):
                b_xnT_out(g, 0)
                act.wait_ge(B["mg_ps"], g + 1)
                f(m_t[:].rearrange("p b e -> p (b e)"), PB[:, 1, 0:GB * NE], ACT.Tanh,
                  scale=0.5).then_inc(B["mt_r"], 1)
                for c in range(NCH):
                    act.wait_ge(B["up_ps"], NCH * g + c + 1)
                    if c >= 4:
                        act.wait_ge(B["sqp_r" if c % 2 else "sqv_r"], 8 * g + c // 2 - 1)
                    f(m_r[:, c % 4, :], PB[:, 2 + c % 2, :], ACT.Relu).then_inc(B["relu_r"], 1)

            def b_v(g):
                b_xnT_out(g, 1)
                act.wait_ge(B["v_ps"], g + 1)
                f(v1[:].rearrange("p b d -> p (b d)"), PB[:, 0, :], ACT.Copy).then_inc(B["v_r"], 1)

            def b_exp(g, b):
                act.wait_ge(B["ss_r"], 4 * g + b + 1)
                if b > 0:
                    act.wait_ge(B["pn_r"], 4 * g + b)
                f(b_p, b_ss, ACT.Exp, scale=D ** -0.5).then_inc(B["p_r"], 1)

            def b_pt_out(g, b):
                for h in range(2):
                    act.wait_ge(B["pt_ps"], 8 * g + 2 * b + h + 1)
                    f(b_pt[:, 4 * h:4 * h + 4, :].rearrange("p h t -> p (h t)"), PB[:, 2 + h, :],
                      ACT.Copy).then_inc(B["pt_r"], 1)
                for h in range(2):
                    act.wait_ge(B["ot_ps"], 8 * g + 2 * b + h + 1)
                    f(b_ot[:, 4 * h:4 * h + 4, :].rearrange("p h t -> p (h t)"), PB[:, 2 + h, :], ACT.Identity,
                      bias=vcol[:, V_BV1:V_BV1 + 1]).then_inc(B["ot_r"], 1)

            def b_xqkv(g):
                b_xnT_out(g, 2)
                act.wait_ge(B["xq_ps"], g + 1)
                f(qx[:].rearrange("p b t -> p (b t)"), PB[:, 1, :], ACT.Identity,
                  bias=vcol[:, V_XBQ:V_XBQ + 1]).then_inc(B["xq_r"], 1)
                act.wait_ge(B["xk_ps"], g + 1)
                f(kx[:].rearrange("p b m -> p (b m)"), PB[:, 2, 0:GM], ACT.Identity,
                  bias=vcol[:, V_XBK:V_XBK + 1]).then_inc(B["xk_r"], 1)
                act.wait_ge(B["xv_ps"], g + 1)
                f(vx[:].rearrange("p b d -> p (b d)"), PB[0:MC, 3, :], ACT.Copy).then_inc(B["xv_r"], 1)

            def b_xexp(g, b):
                act.wait_ge(B["xss_r"], 4 * g + b + 1)
                if b > 0:
                    act.wait_ge(B["xpn_r"], 4 * g + b)
                f(x_p, x_ss, ACT.Exp, scale=HDX ** -0.5).then_inc(B["xp_r"], 1)

            def b_xpt_out(g, b):
                act.wait_ge(B["xpt_ps"], 4 * g + b + 1)
                f(x_pt[:, 0:4, :].rearrange("p j t -> p (j t)"), PB[:, 2, :], ACT.Copy)
                f(x_pt[0:JT[4][1], 4, :], PB[0:JT[4][1], 3, 0:T], ACT.Copy).then_inc(B["xpt_r"], 1)
                act.wait_ge(B["xo_ps"], 4 * g + b + 1)
                f(x_oT[:, b, :], PB[:, 3, T:2 * T], ACT.Identity,
                  bias=vcol[:, V_XBV:V_XBV + 1]).then_inc(B["xo_r"], 1)

            def b_ffn(g):
                b_xnT_out(g, 3)
                act.wait_ge(B["fs_r"], g + 1)
                f(f_e[:], f_s[:], ACT.Exp).then_inc(B["fe_r"], 1)
                act.wait_ge(B["fwT_ps"], g + 1)
                f(f_wT[:].rearrange("p b t -> p (b t)"), PB[0:NE, 1, :], ACT.Copy).then_inc(B["fwT_r"], 1)

            def thread_b(g):
                b_moe(g)
                b_v(g)
                b_exp(g, 0)
                for b in range(GB):
                    if b + 1 < GB:
                        b_exp(g, b + 1)
                    b_pt_out(g, b)
                b_xqkv(g)
                b_xexp(g, 0)
                for b in range(GB):
                    if b + 1 < GB:
                        b_xexp(g, b + 1)
                    b_xpt_out(g, b)
                b_ffn(g)

            thread_a(0)
            with act.Fori(0, NG - 1) as g:
                thread_b(g)
                thread_a(g + 1)
            thread_b(NG - 1)

        @block.gpsimd
        def _(pool):
            tt = nc.gpsimd.tensor_tensor
            pool.wait_ge(set_vec, 17)

            def a_ctx(g):
                pool.wait_ge(A["cve_r"], g + 1)
                tt(crs[:], cve[:], mhalf[0:MC, :], ALU.pow).then_inc(A["crs_r"], 1)
                pool.wait_ge(x_loaded, 16 * g + 16)
                tt(xc[:], xin[:], cb1[:].unsqueeze(1).to_broadcast([128, GB, D]), ALU.add).then_inc(A["xc_r"], 1)

            def a_rstd_(g, u):
                pool.wait_ge(A["var_r"], 3 * g + u + 1)
                tt(a_rstd[:], a_ve[:], mhalf[:], ALU.pow).then_inc(A["rstd_r"], 1)

            def a_keys(g, b):
                if b == 0:
                    pool.wait_ge(A["kT_r"], g + 1)
                if b >= 2:
                    pool.wait_ge(A["s_ps"], 4 * g + b - 1)
                tt(a_kbd[:, b % 2, :, :], kT[:, b, :].unsqueeze(1).to_broadcast([128, H0, T]),
                   hmask[:].unsqueeze(2).to_broadcast([128, H0, T]), ALU.mult).then_inc(A["kbd_r"], 1)

            def a_slot(g, t):
                pool.wait_ge(A["sve_r"], 3 * g + t + 1)
                tt(s_rs[:], s_ve[:], mhalf[:], ALU.pow).then_inc(A["srs_r"], 1)

            def thread_a(g):
                a_ctx(g)
                a_rstd_(g, 0)
                for b in range(GB):
                    a_keys(g, b)
                a_rstd_(g, 1)
                a_rstd_(g, 2)
                for t in range(3):
                    a_slot(g, t)

            def b_rstd_(g, u):
                pool.wait_ge(B["var_r"], 4 * g + u + 1)
                tt(b_rstd[:], b_ve[:], mhalf[:], ALU.pow).then_inc(B["rstd_r"], 1)

            def b_squares(g):
                for c in range(1, NCH, 2):
                    pool.wait_ge(B["relu_r"], NCH * g + c + 1)
                    tt(m_h[:, c, :], m_r[:, c % 4, :], m_r[:, c % 4, :], ALU.mult).then_inc(B["sqp_r"], 1)

            def b_probs(g, b):
                pool.wait_ge(B["rs_r"], 4 * g + b + 1)
                if b > 0:
                    pool.wait_ge(B["pt_ps"], 8 * g + 2 * b)
                tt(b_pn[:], b_p, b_rs[:].unsqueeze(2).to_broadcast([128, H1, T]), ALU.mult).then_inc(B["pn_r"], 1)

            def b_xprobs(g, b):
                pool.wait_ge(B["xrs_r"], 4 * g + b + 1)
                if b > 0:
                    pool.wait_ge(B["xpt_ps"], 4 * g + b)
                for c in range(NCLS):
                    v = lambda ap: ap[:, OFF[c]:OFF[c + 1]].rearrange("p (h k) -> p h k", h=4)
                    last = tt(v(x_pn), v(x_p), x_rs[:, 4 * c:4 * c + 4].unsqueeze(2).to_broadcast([128, 4, NK[c]]),
                              ALU.mult)
                last.then_inc(B["xpn_r"], 1)

            def thread_b(g):
                b_rstd_(g, 0)
                b_squares(g)
                b_rstd_(g, 1)
                for b in range(GB):
                    b_probs(g, b)
                b_rstd_(g, 2)
                tt(x4b[:], x4[:], ybo[:].unsqueeze(1).to_broadcast([128, GB, D]), ALU.add).then_inc(B["x4b_r"], 1)
                for b in range(GB):
                    b_xprobs(g, b)
                b_rstd_(g, 3)

            thread_a(0)
            with pool.Fori(0, NG - 1) as g:
                thread_b(g)
                thread_a(g + 1)
            thread_b(NG - 1)

        STEPS_A, STEPS_B = STEPS

        @block.vector
        def _(dve):
            v = nc.vector
            bc = lambda ap, n: ap.unsqueeze(2).to_broadcast([*ap.shape, n])

            class Steps:

                def __init__(self, s, per_group):
                    self.s, self.per_group = s, per_group

                def begin(self, g):
                    self.base, self.n = g * self.per_group, 0

                def then(self, ins):
                    ins.then_inc(self.s, 1)
                    self.n += 1
                    dve.wait_ge(self.s, self.base + self.n)

            sa, sbx = Steps(A["a_step"], STEPS_A), Steps(B["b_step"], STEPS_B)

            count = [0]

            def setup(ins):
                ins.then_inc(set_vec, 1)
                count[0] += 1
                dve.wait_ge(set_vec, count[0])

            v.memset(vaug[:], 1.0)
            v.memset(mhalf[:], -0.5)
            setup(v.memset(vrow[:], 0.0))
            dve.wait_ge(w_loaded, N_LOADS)
            setup(v.tensor_tensor(lam_pr[:], lam_in[:, 0::2, :], lam_in[:, 1::2, :], ALU.mult))
            setup(v.tensor_reduce(lam_s[:], lam_pr[:], AX.X, ALU.add))
            setup(v.tensor_copy(ident16[:], ident[:]))
            setup(v.tensor_copy(cmask16[:], cmask))
            dve.wait_ge(set_act, 1)
            setup(v.tensor_tensor(nlam[:], lam_e[:, 1:2], lam_e[:, 0:1], ALU.subtract))
            setup(v.tensor_scalar(nlam[:], nlam[:], LAMBDA_INIT, None, ALU.subtract))
            dve.wait_ge(set_pe, 1)
            setup(v.tensor_copy(vcol[:], PA[:, 0, 0:NV]))
            setup(v.scalar_tensor_tensor(wvc[:], wv0[:, 64:128], nlam[:, 0:1], wv0[:, 0:64], ALU.mult, ALU.add))
            setup(v.scalar_tensor_tensor(bvc[:], bv0[:, 64:128], nlam[:, 0:1], bv0[:, 0:64], ALU.mult, ALU.add))
            setup(v.tensor_scalar(woe[:], wo0, vcol[:, V_LNW:V_LNW + 1], 1.0 - LAMBDA_INIT, ALU.mult, ALU.mult))
            setup(v.tensor_scalar(lnb, vcol[:, V_LNB:V_LNB + 1].to_broadcast([128, 128]), 1.0 - LAMBDA_INIT, None,
                                  ALU.mult))
            dve.wait_ge(set_pe, 2)
            setup(v.tensor_scalar(wqk[:], PA[:, 1, 0:128], vcol[:, V_WIN:V_WIN + 1], None, ALU.mult))
            dve.wait_ge(set_pe, 3)
            setup(v.tensor_scalar(wvi[:], PA[:, 2, 0:384], vcol[:, V_WIN:V_WIN + 1], None, ALU.mult))
            dve.wait_ge(set_pe, 4)
            setup(v.tensor_tensor(cb1[:], PA[:, 3, 0:128], cb1[:], ALU.add))
            setup(v.tensor_tensor(rzb[:], vcol[:, V_BIH:V_BIH + 2], vcol[:, V_BHH:V_BHH + 2], ALU.add))
            setup(v.tensor_scalar(rzb[:], rzb[:], 0.5, None, ALU.mult))

            def hold():
                v.memset(held[:], 0.0)

            def norm(st, S, src, dst, stt, mv, ve, rstd, uses, u, g):
                for b in range(GB):
                    last = v.bn_stats(stt[:, b, :], src[:, b, :])
                st.then(last)
                hold()
                for b in range(GB):
                    last = v.bn_aggr(mv[:, b, :], stt[:, b, :])
                st.then(last)
                v.tensor_scalar(ve[:], mv[:, :, 1], LN_EPS, None, ALU.add).then_inc(S["var_r"], 1)
                dve.wait_ge(S["rstd_r"], uses * g + u + 1)
                for b in range(GB):
                    v.tensor_scalar(dst[:, b, :], src[:, b, :], mv[:, b, 0:1], rstd[:, b:b + 1], ALU.subtract,
                                    ALU.mult).then_inc(S["xn_r"], 1)

            def a_norm(g, u, src):
                norm(sa, A, src, a_xn, a_st, a_mv, a_ve, a_rstd, 3, u, g)

            def b_norm(g, u, src):
                norm(sbx, B, src, b_xn, b_st, b_mv, b_ve, b_rstd, 4, u, g)

            def a_ctx(g):
                dve.wait_ge(A["css_r"], g + 1)
                v.tensor_scalar(cve[:], css[:], 1.0 / D, RMS_EPS, ALU.mult, ALU.add).then_inc(A["cve_r"], 1)
                dve.wait_ge(A["crs_r"], g + 1)
                for b in range(GB):
                    last = v.tensor_scalar(cn[:, b, :], cin[:, b, :], crs[:, b:b + 1], None, ALU.mult)
                last.then_inc(A["cn_r"], 1)
                dve.wait_ge(A["kq_ps"], g + 1)
                v.tensor_scalar(kq[:].rearrange("p b m -> p (b m)"), PA[:, 2, 0:GM], vcol[:, V_WS:V_WS + 1], None,
                                ALU.mult).then_inc(A["kq_r"], 1)

            def a_kv(g):
                dve.wait_ge(A["qk_ps"], 2 * g + 2)
                v.tensor_scalar(kT[:].rearrange("p b t -> p (b t)"), PA[:, 2, :],
                                vcol[:, V_BK:V_BK + 1], None, ALU.add).then_inc(A["kT_r"], 1)
                dve.wait_ge(A["v_ps"], g + 1)
                v.tensor_tensor(vaug[:, :, :, 0:HD0], PA[:, 3, 0:256].rearrange("p (b j d) -> p b j d", b=GB, d=HD0),
                                bvc[:].rearrange("p (j d) -> p j d", d=HD0).unsqueeze(1).to_broadcast([128, GB, 4, HD0]),
                                ALU.add).then_inc(A["v_r"], 1)

            def a_soft(g, b):
                dve.wait_ge(A["s_ps"], 4 * g + b + 1)
                s = PA[:, 0:2, :].rearrange("p k (h t) -> p (k h) t", h=4)
                sa.then(v.tensor_reduce(a_mx[:], s, AX.X, ALU.max))
                if b > 0:
                    dve.wait_ge(A["p_r"], 4 * g + b)
                v.tensor_tensor(a_ss[:], s, bc(a_mx[:], T), ALU.subtract).then_inc(A["ss_r"], 1)

            def a_heads(g, p):
                dve.wait_ge(A["pv_ps"], 4 * g + 2 * p + 2)
                s = PA[:, 3, 0:2 * H0 * 17].rearrange("p (n d) -> p n d", d=17)
                sa.then(v.reciprocal(a_rd[:], s[:, :, 16]))
                v.tensor_tensor(a_o[:, 2 * p:2 * p + 2, :].rearrange("p b (h d) -> p (b h) d", d=HD0),
                                s[:, :, 0:HD0], bc(a_rd[:], HD0), ALU.mult).then_inc(A["o_r"], 1)

            def a_slot(g, t):
                u = 3 * g + t
                dve.wait_ge(A["sq_r"], u + 1)
                v.tensor_scalar(s_ve[:], s_sq[:], 1.0 / D, RMS_EPS, ALU.mult, ALU.add).then_inc(A["sve_r"], 1)
                dve.wait_ge(A["srs_r"], u + 1)
                for b in range(GB):
                    src = a_xn[:, b, :] if t == 0 else PA[:, 0, b * T:b * T + T]
                    last = v.tensor_scalar(sn[:, b, :], src, s_rs[:, b:b + 1], None, ALU.mult)
                last.then_inc(A["sn_r"], 1)
                dve.wait_ge(A["sc_ps"], u + 1)
                s = PA[0:MC, 2, :].rearrange("p (b t) -> p b t", b=GB)
                sa.then(v.tensor_reduce(s_mx[:], s, AX.X, ALU.max))
                v.tensor_tensor(s_ex[:], s, bc(s_mx[:], T), ALU.subtract).then_inc(A["ex_r"], 1)
                dve.wait_ge(A["e_r"], u + 1)
                sa.then(v.tensor_reduce(s_sum[:], s_e[:], AX.X, ALU.add))
                sa.then(v.reciprocal(s_rsum[:], s_sum[:]))
                v.tensor_tensor(s_at[:], s_e[:], bc(s_rsum[:], T), ALU.mult).then_inc(A["at_r"], 1)
                dve.wait_ge(A["at_ps"], u + 1)
                s = PA[:, 3, 0:GM].rearrange("p (b m) -> p b m", b=GB)
                sa.then(v.tensor_reduce(s_row[:], s, AX.X, ALU.add))
                sa.then(v.tensor_scalar(s_rowe[:], s_row[:], RMS_EPS, None, ALU.add))
                sa.then(v.reciprocal(s_rrow[:], s_rowe[:]))
                v.tensor_tensor(s_an[:], s, bc(s_rrow[:], MC), ALU.mult).then_inc(A["an_r"], 1)
                dve.wait_ge(A["tr_r"], u + 1)
                sa.then(v.tensor_scalar(g_tr[:], g_tr[:], 0.5, 0.5, ALU.mult, ALU.add))
                dve.wait_ge(A["g_ps"], 4 * u + 1)
                sa.then(v.scalar_tensor_tensor(g_q[:], PA[:, 3, :], vcol[:, V_BHH + 2:V_BHH + 3], g_tr[:], ALU.add,
                                               ALU.mult))
                dve.wait_ge(A["g_ps"], 4 * u + 4)
                v.tensor_tensor(g_q[:], PA[:, 1, :], g_q[:], ALU.add).then_inc(A["pre_r"], 1)
                dve.wait_ge(A["tz_r"], u + 1)
                sa.then(v.tensor_scalar(g_tz[:], g_tz[:], 0.5, 0.5, ALU.mult, ALU.add))
                dve.wait_ge(A["n_r"], u + 1)
                sa.then(v.tensor_tensor(g_d[:], hT[:], g_n[:], ALU.subtract))
                sa.then(v.tensor_tensor(g_d[:], g_d[:], g_tz[:], ALU.mult))
                v.tensor_tensor(hT[:], g_n[:], g_d[:], ALU.add).then_inc(A["h_r"], 1)

            def thread_a(g):
                sa.begin(g)
                a_ctx(g)
                dve.wait_ge(x_loaded, 16 * g + 16)
                a_norm(g, 0, xin)
                a_kv(g)
                a_soft(g, 0)
                for b in range(GB):
                    if b + 1 < GB:
                        a_soft(g, b + 1)
                    if b % 2:
                        a_heads(g, b // 2)
                dve.wait_ge(A["o_r"], 2 * g + 2)
                a_norm(g, 1, a_o)
                dve.wait_ge(A["y_ps"], g + 1)
                dve.wait_ge(A["xc_r"], g + 1)
                sa.then(v.tensor_tensor(x1[:].rearrange("p b d -> p (b d)"), PA[:, 0, :],
                                        xc[:].rearrange("p b d -> p (b d)"), ALU.add))
                a_norm(g, 2, x1)
                for t in range(3):
                    a_slot(g, t)
                dve.wait_ge(A["hp_ps"], 3 * g + 3)
                v.tensor_tensor(x2[:].rearrange("p b d -> p (b d)"), PA[:, 0, :],
                                x1[:].rearrange("p b d -> p (b d)"), ALU.add).then_inc(x2_ready, 1)
                assert sa.n == STEPS_A, sa.n

            def b_route(g):
                dve.wait_ge(B["mt_r"], g + 1)
                st = sbx
                st.then(v.tensor_scalar(m_s[:], m_t[:], 0.5, 0.5, ALU.mult, ALU.add))
                st.then(v.tensor_tensor(m_b[:], m_s[:], ebias[:].unsqueeze(1).to_broadcast([128, GB, NE]), ALU.add))
                hold()
                for b in range(GB):
                    last = v.max(m_top[:, b, :], m_b[:, b, :])
                st.then(last)
                hold()
                for b in range(GB):
                    last = v.max_index(m_ix[:, b, :], m_top[:, b, :], m_b[:, b, :])
                st.then(last)
                st.then(v.tensor_copy(m_ixf[:], m_ix[:]))
                io = iota8[:].unsqueeze(1).to_broadcast([128, GB, NE])
                v.tensor_tensor(m_1[:], io, m_ixf[:, :, 0:1].to_broadcast([128, GB, NE]), ALU.is_equal)
                st.then(v.tensor_tensor(m_2[:], io, m_ixf[:, :, 1:2].to_broadcast([128, GB, NE]), ALU.is_equal))
                st.then(v.tensor_tensor(m_1[:], m_1[:], m_2[:], ALU.add))
                st.then(v.tensor_tensor(m_w[:], m_1[:], m_s[:], ALU.mult))
                st.then(v.tensor_tensor(m_w2[:], m_w[:], m_w[:], ALU.mult))

            def b_squares(g):
                for c in range(0, NCH, 2):
                    dve.wait_ge(B["relu_r"], NCH * g + c + 1)
                    v.tensor_tensor(m_h[:, c, :], m_r[:, c % 4, :], m_r[:, c % 4, :], ALU.mult).then_inc(B["sqv_r"], 1)

            def b_combine(g, b):
                for f in range(2):
                    dve.wait_ge(B["dn_ps"], 8 * g + 2 * b + f + 1)
                    for e in range(4 * f, 4 * f + 4):
                        ins = v.scalar_tensor_tensor(x3[:, b, :], PB[:, f, (e % 4) * 128:(e % 4) * 128 + 128],
                                                     m_w2[:, b, e:e + 1], x2[:, b, :] if e == 0 else x3[:, b, :],
                                                     ALU.mult, ALU.add)
                        if e % 4 < 3:
                            sbx.then(ins)
                    ins.then_inc(B["x3_r"], 1)
                    dve.wait_ge(B["x3_r"], 8 * g + 2 * b + f + 1)

            def b_qk(g):
                pe4 = peT[:].unsqueeze(1).to_broadcast([128, GB, T])
                dve.wait_ge(B["k_ps"], g + 1)
                v.scalar_tensor_tensor(k1[:], PB[:, 3, :].rearrange("p (b t) -> p b t", b=GB),
                                       vcol[:, V_BK1:V_BK1 + 1], pe4, ALU.add, ALU.add).then_inc(B["k_r"], 1)
                for h in range(H1):
                    dve.wait_ge(B["q_ps"], 8 * g + h + 1)
                    v.scalar_tensor_tensor(q1[:, h, :].rearrange("p (b t) -> p b t", b=GB),
                                           PB[:, 1 + h % 2, :].rearrange("p (b t) -> p b t", b=GB),
                                           vcol[:, V_BQ1 + h:V_BQ1 + h + 1], pe4, ALU.add, ALU.add).then_inc(B["q_r"], 1)

            def b_soft(g, b):
                dve.wait_ge(B["s_ps"], 4 * g + b + 1)
                s = PB[:, 0:2, :].rearrange("p k (h t) -> p (k h) t", h=4)
                sbx.then(v.tensor_reduce(b_mx[:], s, AX.X, ALU.max))
                if b > 0:
                    dve.wait_ge(B["p_r"], 4 * g + b)
                v.tensor_tensor(b_ss, s, bc(b_mx[:], T), ALU.subtract).then_inc(B["ss_r"], 1)

            def b_sums(g, b):
                dve.wait_ge(B["p_r"], 4 * g + b + 1)
                sbx.then(v.tensor_reduce(b_sum[:], b_p, AX.X, ALU.add))
                if b > 0:
                    dve.wait_ge(B["pn_r"], 4 * g + b)
                v.reciprocal(b_rs[:], b_sum[:]).then_inc(B["rs_r"], 1)

            def b_res(g, b):
                dve.wait_ge(B["wo_ps"], 4 * g + b + 1)
                v.tensor_tensor(x4[:, b, :], PB[:, 2, 0:128], x3[:, b, :], ALU.add).then_inc(B["x4_r"], 1)

            def cls(ap, c):
                return ap[:, OFF[c]:OFF[c + 1]].rearrange("p (h k) -> p h k", h=4)

            def b_xbd(g):
                dve.wait_ge(B["xk_r"], g + 1)
                for c in range(NCLS):
                    for b in range(GB):
                        last = v.tensor_tensor(cls(kbd[:, b, :], c),
                                               kx[:, b, ::1 << c].unsqueeze(1).to_broadcast([128, 4, NK[c]]),
                                               bc(kmask[:, c, :], NK[c]), ALU.mult)
                last.then_inc(B["kbd_r"], 1)
                for i, (j, w) in enumerate(JT):
                    dve.wait_ge(B["vbd_ps"], 5 * g + i + 1)
                    v.tensor_tensor(vbd[0:w, i, :, :], PB[0:w, 2 + i % 2, :].rearrange("p (b d) -> p b d", b=GB),
                                    vmask[0:w, i, :].unsqueeze(1).to_broadcast([w, GB, D]),
                                    ALU.mult).then_inc(B["vbd_r"], 1)

            def xps(c):
                if c == 0:
                    return PB[:, 0, 0:OFF[1]].rearrange("p (h k) -> p h k", h=4)
                return PB[:, 1, OFF[c] - OFF[1]:OFF[c + 1] - OFF[1]].rearrange("p (h k) -> p h k", h=4)

            def b_xsoft(g, b):
                dve.wait_ge(B["xs_ps"], 4 * g + b + 1)
                for c in range(NCLS):
                    last = v.tensor_reduce(x_mx[:, 4 * c:4 * c + 4], xps(c), AX.X, ALU.max)
                sbx.then(last)
                if b > 0:
                    dve.wait_ge(B["xp_r"], 4 * g + b)
                for c in range(NCLS):
                    last = v.tensor_tensor(cls(x_ss, c), xps(c), bc(x_mx[:, 4 * c:4 * c + 4], NK[c]), ALU.subtract)
                last.then_inc(B["xss_r"], 1)

            def b_xsums(g, b):
                dve.wait_ge(B["xp_r"], 4 * g + b + 1)
                for c in range(NCLS):
                    last = v.tensor_reduce(x_sum[:, 4 * c:4 * c + 4], cls(x_p, c), AX.X, ALU.add)
                sbx.then(last)
                if b > 0:
                    dve.wait_ge(B["xpn_r"], 4 * g + b)
                v.reciprocal(x_rs[:], x_sum[:]).then_inc(B["xrs_r"], 1)

            def b_mix(g):
                st = sbx
                dve.wait_ge(B["fg_ps"], g + 1)
                st.then(v.tensor_tensor(f_l[:], PB[:, 1, 0:GB * NE].rearrange("p (b e) -> p b e", b=GB),
                                        fgb[:].unsqueeze(1).to_broadcast([128, GB, NE]), ALU.add))
                st.then(v.tensor_reduce(f_mx[:], f_l[:], AX.X, ALU.max))
                v.tensor_tensor(f_s[:], f_l[:], bc(f_mx[:], NE), ALU.subtract).then_inc(B["fs_r"], 1)
                dve.wait_ge(B["fe_r"], g + 1)
                st.then(v.tensor_reduce(f_sum[:], f_e[:], AX.X, ALU.add))
                st.then(v.reciprocal(f_r[:], f_sum[:]))
                st.then(v.tensor_tensor(f_g[:], f_e[:], bc(f_r[:], NE), ALU.mult))
                st.then(v.scalar_tensor_tensor(f_w0[:], f_g[:], 0.1, f_g[:], ALU.is_ge, ALU.mult))
                st.then(v.tensor_reduce(f_ws[:], f_w0[:], AX.X, ALU.add))
                st.then(v.tensor_scalar(f_z[:], f_ws[:], 0.0, None, ALU.is_equal))
                st.then(v.tensor_tensor(f_wd[:], f_ws[:], f_z[:], ALU.add))
                st.then(v.reciprocal(f_wr[:], f_wd[:]))
                v.tensor_tensor(f_w[:], f_w0[:], bc(f_wr[:], NE), ALU.mult).then_inc(B["fw_r"], 1)
                dve.wait_ge(B["fb_ps"], g + 1)
                dve.wait_ge(out_done, 16 * g + 16)
                st.then(v.tensor_tensor(y[:].rearrange("p b d -> p (b d)"), PB[:, 0, :],
                                        x5[:].rearrange("p b d -> p (b d)"), ALU.add))
                for b in range(GB):
                    for f in range(2):
                        dve.wait_ge(B["ff_ps"], 8 * g + 2 * b + f + 1)
                        for e in range(4 * f, 4 * f + 4):
                            ins = v.scalar_tensor_tensor(y[:, b, :], PB[:, 2 + f, (e % 4) * 128:(e % 4) * 128 + 128],
                                                         f_w[:, b, e:e + 1], y[:, b, :], ALU.mult, ALU.add)
                            if e % 4 < 3:
                                st.then(ins)
                        ins.then_inc(B["y_r"], 1)
                        dve.wait_ge(B["y_r"], 8 * g + 2 * b + f + 1)

            def thread_b(g):
                sbx.begin(g)
                dve.wait_ge(x2_ready, g + 1)
                b_norm(g, 0, x2)
                b_route(g)
                b_squares(g)
                for b in range(GB):
                    b_combine(g, b)
                b_norm(g, 1, x3)
                b_qk(g)
                b_soft(g, 0)
                for b in range(GB):
                    if b + 1 < GB:
                        b_sums(g, b)
                        b_soft(g, b + 1)
                    else:
                        b_sums(g, b)
                    b_res(g, b)
                dve.wait_ge(B["x4_r"], 4 * g + 4)
                b_norm(g, 2, x4)
                b_xbd(g)
                b_xsoft(g, 0)
                for b in range(GB):
                    b_xsums(g, b)
                    if b + 1 < GB:
                        b_xsoft(g, b + 1)
                dve.wait_ge(B["xy_ps"], g + 1)
                dve.wait_ge(B["x4b_r"], g + 1)
                sbx.then(v.tensor_tensor(x5[:].rearrange("p b d -> p (b d)"), PB[:, 0, :],
                                         x4b[:].rearrange("p b d -> p (b d)"), ALU.add))
                b_norm(g, 3, x5)
                b_mix(g)
                assert sbx.n == STEPS_B, sbx.n

            thread_a(0)
            with dve.Fori(0, NG - 1) as g:
                thread_b(g)
                thread_a(g + 1)
            thread_b(NG - 1)


def _layout(i):
    import numpy as np

    f = np.float32
    t = {k: np.asarray(v) for k, v in i.items()}
    w = {k: v for k, v in t.items() if k not in ("x", "ctx_1024")}
    w["x"] = t["x"].transpose(1, 0, 2)
    w["ctx_tok"] = t["ctx_1024"].transpose(1, 0, 2)
    w["ctx_feat"] = t["ctx_1024"].transpose(2, 0, 1)
    for n in ("L0_xattn_gru_wih", "L0_xattn_gru_whh", "L0_ffn_gate_w", "L1_xattn_Wq", "L1_xattn_Wk", "L1_xattn_Wv",
              "L1_xattn_Wo"):
        w[n] = t[n].T
    w["L0_ffn_w_up"] = t["L0_ffn_w_up"].reshape(NE * HID, D).T
    w["L0_ffn_w_down"] = t["L0_ffn_w_down"].transpose(0, 2, 1).reshape(NCH, 128, D).transpose(1, 0, 2)
    w["L1_attn_Wo"] = t["L1_attn_Wo"].reshape(H1, 128, D).transpose(1, 0, 2)
    w["L1_ffn_expert_w"] = t["L1_ffn_expert_w"].transpose(1, 0, 2)
    p = np.arange(128)
    w["c_ident"] = np.eye(128, dtype=f)
    w["c_cmask"] = np.tile(np.where(p[None, :] > p[:, None], f(-1e30), f(0)), (1, 4)).astype(f)
    ang = p.astype(f)[:, None] * np.exp(f(-np.log(10000.0)) * np.arange(0, D, 2, dtype=f) / f(D))[None, :]
    pe = np.zeros((128, D), f)
    pe[:, 0::2], pe[:, 1::2] = np.sin(ang), np.cos(ang)
    w["c_peT"] = pe.T
    sel, vm, km = np.zeros((MC, JX), f), np.zeros((len(JT) * 128, D), f), np.zeros((128, NCLS, 4), f)
    for c in range(NCLS):
        for n in range(4):
            head = c + 4 * n
            km[head * HDX:(head + 1) * HDX, c, n] = 1
            for k in range(NK[c]):
                j = OFF[c] + n * NK[c] + k
                sel[k << c, j] = 1
                vm[j, head * HDX:(head + 1) * HDX] = 1
    w["c_sel"], w["c_kmask"] = sel, km
    w["c_hmask"] = np.repeat(np.eye(H0, dtype=f), HD0, axis=0)
    w["c_vmask"] = vm.reshape(len(JT), 128, D).transpose(1, 0, 2)
    w["c_iota8"] = np.tile(np.arange(NE, dtype=f), (128, 1))
    return {k: np.ascontiguousarray(v) for k, v in w.items()}


def kernel(**inputs):
    import concourse.bacc as _bacc
    from concourse import mybir as _mybir
    from concourse.bass_utils import run_bass_kernel_spmd as _run

    nc = _bacc.Bacc("TRN2", target_bir_lowering=False, num_devices=1)
    arrays, aps = {}, {}
    for name, arr in _layout(inputs).items():
        arrays[f"in_{name}_dram"] = arr
        aps[name] = nc.dram_tensor(f"in_{name}_dram", arr.shape, _mybir.dt.from_np(arr.dtype),
                                   kind="ExternalInput").ap()
    out = nc.dram_tensor("out_0_dram", (T, NS, D), F32, kind="ExternalOutput").ap()
    build(nc, aps, out)
    r = _run(nc, [arrays], core_ids=[0])
    return r.results[0]["out_0_dram"].transpose(1, 0, 2)
```

```python
from contextlib import ExitStack

import concourse.bass as bass
from concourse import mybir

ALU = mybir.AluOpType
ACT = mybir.ActivationFunctionType
AX = mybir.AxisListType
F32 = mybir.dt.float32
BF16 = mybir.dt.bfloat16
U32 = mybir.dt.uint32

NS, T, D, MC = 64, 128, 128, 77
GB = 4
NG = NS // GB
GT = GB * T
GM = GB * MC
NE, HID = 8, 256
NCH = NE * HID // 128
H0, HD0 = 8, 16
H1 = 8
HX, HDX = 16, 8
NCLS = 4
NK = [-(-MC // (1 << c)) for c in range(NCLS)]
OFF = [4 * sum(NK[:c]) for c in range(NCLS + 1)]
JX = OFF[NCLS]
JT = [(i, min(128, JX - i)) for i in range(0, JX, 128)]
LN_EPS, RMS_EPS, LAMBDA_INIT = 1e-5, 1e-6, 0.8

(V_BQ, V_BK, V_BIH, V_BHH, V_WS, V_WIN, V_LNW, V_LNB, V_BQ1, V_BK1, V_BV1, V_XBQ, V_XBK, V_XBV) = (
    0, 1, 2, 5, 8, 9, 10, 11, 12, 20, 21, 22, 23, 24)
NV = 25
STEPS = (46, 93)


ORDER = {
    "pe": (
        "aaabbbbabbbbbbbbabbbabbababbaaababbbbbabbbbbbbaaaabbbbbbbbbbbbbabaabaababbbbabbababbaabaabbbaabbbaab"
        "aaabbbbbbbaaaabbbabbbababbbababbabbbabbaabbbbbaaabbabbababbbabaaba"),
    "act": (
        "aababbabbbbbbbbbaabbbbbabaaaabbbaaabbbbbbbbabbaaabbbabbabbbbabbbbaababbabbbaabbbaabbabababaaaabaaaaa"
        "aa"),
    "pool": "abbbbababbbbaabababbbabaabbbbaba",
    "dve": (
        "aabbbbbbaababbbbabbabaabbbbbbbabbbbbbbbabbababbbbabbbbaabbbbbbbbaaabbbaabbabbabbbbbbbbbaabbabbbbbaab"
        "abaaaabbaaabbaaaaabaabbbabababbaaaaaab"),
}


def weave(order, a, b):
    threads = {"a": a, "b": b}
    for thread in threads.values():
        next(thread)
    ended = [c for c in order if next(threads[c], "end") == "end"]
    assert sorted(ended) == ["a", "b"], ended


def alone(thread):
    for _ in thread:
        pass


def build(nc, a, out):
    with ExitStack() as ctx:
        def sb(name, shape, dt=F32):
            return ctx.enter_context(nc.sbuf_tensor(name, shape, dt))

        def sem(name):
            return ctx.enter_context(nc.semaphore(name))

        ident = sb("ident", [128, 128])
        ident16 = sb("ident16", [128, 128], BF16)
        cmask16 = sb("cmask16", [128, 512], BF16)
        peT = sb("peT", [128, 128])
        sel = sb("sel", [MC, JX])
        vmask = sb("vmask", [128, len(JT), 128])
        kmask = sb("kmask", [128, NCLS, 4])
        hmask = sb("hmask", [128, H0])
        iota8 = sb("iota8", [128, NE])
        mhalf = sb("mhalf", [128, GB])
        held = sb("held", [1, 2])
        vrow = sb("vrow", [NV, 128])
        vcol = sb("vcol", [128, NV])
        rzb = sb("rzb", [128, 2])
        wq0 = sb("wq0", [128, 128])
        wk0 = sb("wk0", [128, 128])
        wv0 = sb("wv0", [128, 128])
        wvc = sb("wvc", [128, 64])
        woe = sb("woe", [128, 128])
        bvc = sb("bvc", [128, 64])
        cb1 = sb("cb1", [128, 128])
        lam_in = sb("lam_in", [128, 4, HD0])
        lam_pr = sb("lam_pr", [128, 2, HD0])
        lam_s = sb("lam_s", [128, 2])
        lam_e = sb("lam_e", [128, 2])
        nlam = sb("nlam", [128, 1])
        whh = sb("whh", [128, 384])
        wqk = sb("wqk", [128, 128])
        wvi = sb("wvi", [128, 384])
        mgate = sb("mgate", [128, NE])
        ebias = sb("ebias", [128, NE])
        wup = sb("wup", [128, NE * HID])
        wdn = sb("wdn", [128, NCH, 128])
        wq1 = sb("wq1", [128, H1 * 128])
        wkv1 = sb("wkv1", [128, 256])
        wo1 = sb("wo1", [128, H1, 128])
        ywq = sb("ywq", [128, 128])
        ywk = sb("ywk", [128, 128])
        ywv = sb("ywv", [128, 128])
        ywo = sb("ywo", [128, 128])
        ybo = sb("ybo", [128, 128])
        fgate = sb("fgate", [128, NE])
        fgb = sb("fgb", [128, NE])
        fw = sb("fw", [128, NE, 128])
        fb = sb("fb", [NE, 128])

        xin = sb("xin", [128, GB, D])
        cin = sb("cin", [MC, GB, D])
        xc = sb("xc", [128, GB, D])
        x1 = sb("x1", [128, GB, D])
        x2 = sb("x2", [128, GB, D])
        a_st = sb("a_st", [128, GB, 6])
        a_mv = sb("a_mv", [128, GB, 2])
        a_ve = sb("a_ve", [128, GB])
        a_rstd = sb("a_rstd", [128, GB])
        a_xn = sb("a_xn", [128, GB, D])
        a_xnT = sb("a_xnT", [128, GB, T])
        css = sb("css", [MC, GB])
        cve = sb("cve", [MC, GB])
        crs = sb("crs", [MC, GB])
        cnT = sb("cnT", [128, GM])
        kq = sb("kq", [128, GB, MC])
        vw = sb("vw", [MC, GB, 384])
        qT = sb("qT", [128, GB, T])
        kT = sb("kT", [128, GB, T])
        a_kbd = sb("a_kbd", [128, 2, H0, T])
        vaug = sb("vaug", [128, GB, 4, HD0 + 1])
        a_mx = sb("a_mx", [128, H0])
        a_ss = sb("a_ss", [128, H0, T])
        a_p = sb("a_p", [128, H0, T])
        a_pt = sb("a_pt", [128, H0, T])
        cmask = a_p[:, 0:4, :].rearrange("p h t -> p (h t)")
        wo0, lnb, bv0, xwq = (a_ss[:, i, :] for i in range(4))
        xwk, xwv = a_ss[:, 4, :], a_ss[:, 5, :]
        wih = a_pt[:, 0:3, :].rearrange("p h t -> p (h t)")
        a_rd = sb("a_rd", [128, 2 * H0])
        a_o = sb("a_o", [128, GB, D])
        hT = sb("hT", [128, GT])
        s_sq = sb("s_sq", [128, GB])
        s_ve = sb("s_ve", [128, GB])
        s_rs = sb("s_rs", [128, GB])
        sn = sb("sn", [128, GB, D])
        snT = sb("snT", [128, GB, T])
        s_mx = sb("s_mx", [MC, GB])
        s_ex = sb("s_ex", [MC, GB, T])
        s_e = sb("s_e", [MC, GB, T])
        s_sum = sb("s_sum", [MC, GB])
        s_rsum = sb("s_rsum", [MC, GB])
        s_at = sb("s_at", [MC, GB, T])
        s_row = sb("s_row", [128, GB])
        s_rowe = sb("s_rowe", [128, GB])
        s_rrow = sb("s_rrow", [128, GB])
        s_an = sb("s_an", [128, GB, MC])
        s_anT = sb("s_anT", [MC, GB, T])
        g_tr = sb("g_tr", [128, GT])
        g_tz = sb("g_tz", [128, GT])
        g_q = sb("g_q", [128, GT])
        g_n = sb("g_n", [128, GT])
        g_d = sb("g_d", [128, GT])
        a_junk = g_d[:].rearrange("p (b t) -> p b t", b=GB)
        cn = sn[0:MC, :, :]

        cT = sb("cT", [128, GB, MC])
        b_st = sb("b_st", [128, GB, 6])
        b_mv = sb("b_mv", [128, GB, 2])
        b_ve = sb("b_ve", [128, GB])
        b_rstd = sb("b_rstd", [128, GB])
        b_xn = sb("b_xn", [128, GB, D])
        b_xnT = sb("b_xnT", [128, GB, T])
        m_t = sb("m_t", [128, GB, NE])
        m_s = sb("m_s", [128, GB, NE])
        m_b = sb("m_b", [128, GB, NE])
        m_top = sb("m_top", [128, GB, 8])
        m_ix = sb("m_ix", [128, GB, 8], U32)
        m_ixf = sb("m_ixf", [128, GB, 8])
        m_1 = sb("m_1", [128, GB, NE])
        m_2 = sb("m_2", [128, GB, NE])
        m_w = sb("m_w", [128, GB, NE])
        m_w2 = sb("m_w2", [128, GB, NE])
        b_sp = sb("b_sp", [128, 2, H1, T])
        m_r = b_sp[:].rearrange("p k h t -> p (k h t)").rearrange("p (c t) -> p c t", c=4)
        m_h = sb("m_h", [128, NCH, GT])
        x3 = sb("x3", [128, GB, D])
        x4 = sb("x4", [128, GB, D])
        x4b = sb("x4b", [128, GB, D])
        x5 = sb("x5", [128, GB, D])
        y = sb("y", [128, GB, D])
        m_flat = m_h[:].rearrange("p c t -> p (c t)")
        q1 = m_flat[:, 0:H1 * GT].rearrange("p (h t) -> p h t", h=H1)
        kbd = m_flat[:, 0:GB * JX].rearrange("p (b j) -> p b j", b=GB)
        vbd = m_flat[:, H1 * GT:H1 * GT + len(JT) * GT].rearrange("p (i b d) -> p i b d", i=len(JT), b=GB)
        k1 = sb("k1", [128, GB, T])
        v1 = sb("v1", [128, GB, D])
        b_mx = sb("b_mx", [128, H1])
        b_ss, b_p = b_sp[:, 0, :, :], b_sp[:, 1, :, :]
        b_sum = sb("b_sum", [128, H1])
        b_rs = sb("b_rs", [128, H1])
        b_pn = sb("b_pn", [128, H1, T])
        b_pt = sb("b_pt", [128, H1, T])
        b_ot = sb("b_ot", [128, H1, T])
        qx = sb("qx", [128, GB, T])
        kx = sb("kx", [128, GB, MC])
        vx = sb("vx", [MC, GB, D])
        x_mx = sb("x_mx", [128, HX])
        x_ss = b_ss.rearrange("p h t -> p (h t)")[:, 0:JX]
        x_p = b_p.rearrange("p h t -> p (h t)")[:, 0:JX]
        x_sum = sb("x_sum", [128, HX])
        x_rs = sb("x_rs", [128, HX])
        x_pn = b_pn[:].rearrange("p h t -> p (h t)")[:, 0:JX]
        x_pt = b_pt[:, 0:len(JT), :]
        x_oT = sb("x_oT", [128, GB, T])
        f_l = sb("f_l", [128, GB, NE])
        f_mx = sb("f_mx", [128, GB])
        f_s = sb("f_s", [128, GB, NE])
        f_e = sb("f_e", [128, GB, NE])
        f_sum = sb("f_sum", [128, GB])
        f_r = sb("f_r", [128, GB])
        f_g = sb("f_g", [128, GB, NE])
        f_w0 = sb("f_w0", [128, GB, NE])
        f_ws = sb("f_ws", [128, GB])
        f_z = sb("f_z", [128, GB])
        f_wd = sb("f_wd", [128, GB])
        f_wr = sb("f_wr", [128, GB])
        f_w = sb("f_w", [128, GB, NE])
        f_wT = sb("f_wT", [NE, GB, T])

        PA = ctx.enter_context(nc.psum_tensor("PA", [128, 4, 512], F32))
        PB = ctx.enter_context(nc.psum_tensor("PB", [128, 4, 512], F32))

        w_loaded = sem("w_loaded")
        set_vec = sem("set_vec")
        set_pe = sem("set_pe")
        set_act = sem("set_act")
        x_loaded, c_loaded, cT_loaded, out_done = (sem(n) for n in ("x_loaded", "c_loaded", "cT_loaded", "out_done"))
        x2_ready = sem("x2_ready")
        names_a = ("a_step css_r cve_r crs_r cn_r cnT_ps cnT_r kq_ps kq_r vw_ps vw_r xc_r var_r rstd_r xn_r "
                   "xnT_ps xnT_r qk_ps qT_r kT_r kbd_r v_ps v_r s_ps ss_r p_r pt_ps pt_r pv_ps o_r y_ps sq_r sve_r srs_r "
                   "sn_r snT_ps snT_r sc_ps ex_r e_r at_r at_ps an_r anT_ps anT_r g_ps tr_r tz_r pre_r n_r h_r hp_ps")
        A = {n: sem("a_" + n) for n in names_a.split()}
        names_b = ("b_step var_r rstd_r xn_r xnT_ps xnT_r mg_ps mt_r up_ps relu_r sqv_r sqp_r dn_ps x3_r "
                   "q_ps q_r k_ps k_r v_ps v_r s_ps ss_r p_r rs_r pn_r pt_ps pt_r ot_ps ot_r wo_ps x4_r "
                   "xq_ps xk_ps xv_ps xq_r xk_r xv_r kbd_r vbd_ps vbd_r xs_ps xss_r xp_r xrs_r xpn_r xpt_ps xpt_r "
                   "xo_ps xo_r xy_ps x4b_r fg_ps fs_r fe_r fw_r fwT_ps fwT_r fb_ps ff_ps y_r")
        B = {n: sem("b_" + n) for n in names_b.split()}

        ones_row = lambda ap, n: ap.rearrange("(o d) -> o d", o=1).to_broadcast([n, ap.shape[0]])
        loads = [
            (ident[:], a["c_ident"]), (cmask, a["c_cmask"]), (peT[:], a["c_peT"]), (sel[:], a["c_sel"]),
            (vmask[:], a["c_vmask"]), (kmask[:], a["c_kmask"]), (iota8[:], a["c_iota8"]),
            (hmask[:], a["c_hmask"]),
            (vrow[V_BIH:V_BIH + 3, :], a["L0_xattn_gru_bih"].rearrange("(r c) -> r c", r=3)),
            (vrow[V_BHH:V_BHH + 3, :], a["L0_xattn_gru_bhh"].rearrange("(r c) -> r c", r=3)),
            (vrow[V_WS:V_WS + 1, :], ones_row(a["L0_xattn_slot_norm_w"], 1)),
            (vrow[V_WIN:V_WIN + 1, :], ones_row(a["L0_xattn_input_norm_w"], 1)),
            (vrow[V_LNW:V_LNW + 1, :], ones_row(a["L0_attn_ln_w"], 1)),
            (vrow[V_LNB:V_LNB + 1, :], ones_row(a["L0_attn_ln_b"], 1)),
            (vrow[V_BQ1:V_BQ1 + 8, :], a["L1_attn_bq"].rearrange("(r c) -> r c", r=8)),
            (vrow[V_BK1:V_BK1 + 2, :], a["L1_attn_bkv"].rearrange("(r c) -> r c", r=2)),
            (vrow[V_XBQ:V_XBQ + 1, :], ones_row(a["L1_xattn_bq"], 1)),
            (vrow[V_XBK:V_XBK + 1, :], ones_row(a["L1_xattn_bk"], 1)),
            (vrow[V_XBV:V_XBV + 1, :], ones_row(a["L1_xattn_bv"], 1)),
            (vrow[V_BQ:V_BQ + 1, :], ones_row(a["L0_attn_bq"], 1)),
            (vrow[V_BK:V_BK + 1, :], ones_row(a["L0_attn_bk"], 1)),
            (wq0[:], a["L0_attn_Wq"]), (wk0[:], a["L0_attn_Wk"]), (wv0[:], a["L0_attn_Wv"]), (wo0, a["L0_attn_Wo"]),
            (bv0, ones_row(a["L0_attn_bv"], 128)), (cb1[:], ones_row(a["L0_attn_bo"], 128)),
            (xwq, a["L0_xattn_Wq"]), (xwk, a["L0_xattn_Wk"]), (xwv, a["L0_xattn_Wv"]),
            (wih, a["L0_xattn_gru_wih"]), (whh[:], a["L0_xattn_gru_whh"]),
            (mgate[:], a["L0_ffn_gate_w"]), (ebias[:], ones_row(a["L0_ffn_expert_bias"], 128)),
            (wup[:], a["L0_ffn_w_up"]), (wdn[:], a["L0_ffn_w_down"]),
            (wq1[:], a["L1_attn_Wq"]), (wkv1[:], a["L1_attn_Wkv"]), (wo1[:], a["L1_attn_Wo"]),
            (ywq[:], a["L1_xattn_Wq"]), (ywk[:], a["L1_xattn_Wk"]), (ywv[:], a["L1_xattn_Wv"]),
            (ywo[:], a["L1_xattn_Wo"]), (ybo[:], ones_row(a["L1_xattn_bo"], 128)),
            (fgate[:], a["L1_ffn_gate_w"]), (fgb[:], ones_row(a["L1_ffn_gate_b"], 128)),
            (fw[:], a["L1_ffn_expert_w"]), (fb[:], a["L1_ffn_expert_b"]),
        ] + [(lam_in[:, i, :], ones_row(a["L0_attn_lambda_" + n], 128)) for i, n in enumerate(("q1", "k1", "q2", "k2"))]
        N_LOADS = 16 * len(loads)

        block = ctx.enter_context(nc.Block())

        @block.sync
        def _(sp):
            for dst, src in loads:
                if dst is loads[8][0]:
                    sp.wait_ge(set_vec, 1)
                sp.dma_start(dst, src).then_inc(w_loaded, 16)

            def load_x(g):
                sp.dma_start(xin[:], a["x"][:, bass.ds(g * GB, GB), :]).then_inc(x_loaded, 16)
                sp.dma_start(cin[:], a["ctx_tok"][:, bass.ds(g * GB, GB), :]).then_inc(c_loaded, 16)

            def load_cT(g):
                sp.dma_start(cT[:], a["ctx_feat"][:, bass.ds(g * GB, GB), :]).then_inc(cT_loaded, 16)

            def store(g):
                sp.wait_ge(B["y_r"], 8 * g + 8)
                sp.dma_start(out[:, bass.ds(g * GB, GB), :], y[:]).then_inc(out_done, 16)

            sp.sem_inc(out_done, 16)
            load_x(0)
            load_cT(0)
            with sp.Fori(1, NG) as g:
                sp.wait_ge(A["xn_r"], 12 * g - 8)
                sp.wait_ge(A["xc_r"], g)
                sp.wait_ge(A["cn_r"], g)
                load_x(g)
                sp.wait_ge(B["xv_ps"], g)
                load_cT(g)
                store(g - 1)
            store(NG - 1)
            sp.wait_ge(out_done, 16 * NG + 16)

        @block.tensor
        def _(pe):
            mm, tp = nc.tensor.matmul, nc.tensor.transpose

            pe.wait_ge(w_loaded, N_LOADS)
            tp(PA[:, 0, 0:NV], vrow[:], ident[0:NV, 0:NV]).then_inc(set_pe, 1)
            mm(PA[:, 1, 0:128], xwk, xwq, start=True, stop=True).then_inc(set_pe, 1)
            mm(PA[:, 2, 0:384], xwv, wih, start=True, stop=True).then_inc(set_pe, 1)
            pe.wait_ge(set_vec, 12)
            mm(PA[:, 3, 0:128], lnb, wo0, start=True, stop=True).then_inc(set_pe, 1)
            pe.wait_ge(set_vec, 17)

            def a_ctx(g):
                yield
                pe.wait_ge(A["cn_r"], g + 1)
                for b in range(GB):
                    last = tp(PA[:, 1, b * MC:b * MC + MC], cn[:, b, :], ident[0:MC, 0:MC])
                last.then_inc(A["cnT_ps"], 1)
                yield
                pe.wait_ge(A["cnT_r"], g + 1)
                mm(PA[:, 2, 0:GM], wqk[:], cnT[:], start=True, stop=True).then_inc(A["kq_ps"], 1)
                for b, bank in enumerate((3, 0, 1, 2)):
                    yield
                    if b == 3:
                        pe.wait_ge(A["kq_r"], g + 1)
                    mm(PA[0:MC, bank, 0:384], cnT[:, b * MC:b * MC + MC], wvi[:], start=True,
                       stop=True).then_inc(A["vw_ps"], 1)

            def a_norm_T(g, u, bank):
                for b in range(GB):
                    yield
                    pe.wait_ge(A["xn_r"], 12 * g + 4 * u + b + 1)
                    last = tp(PA[:, bank, b * T:b * T + T], a_xn[:, b, :], ident[:])
                last.then_inc(A["xnT_ps"], 1)

            def a_qkv(g):
                yield
                pe.wait_ge(A["vw_r"], 4 * g + 4)
                yield from a_norm_T(g, 0, 0)
                yield
                pe.wait_ge(A["xnT_r"], 3 * g + 1)
                for w, bank in ((wq0, 1), (wk0, 2)):
                    mm(PA[:, bank, :], w[:], a_xnT[:].rearrange("p b t -> p (b t)"), start=True,
                       stop=True).then_inc(A["qk_ps"], 1)
                for b in range(GB):
                    last = mm(PA[:, 3, b * 64:b * 64 + 64], a_xnT[:, b, :], wvc[:], start=True, stop=True)
                last.then_inc(A["v_ps"], 1)

            def a_scores(g, b):
                yield
                if b == 0:
                    pe.wait_ge(A["qT_r"], g + 1)
                else:
                    pe.wait_ge(A["ss_r"], 4 * g + b)
                pe.wait_ge(A["kbd_r"], 4 * g + b + 1)
                for t in range(2):
                    last = mm(PA[:, t, :], qT[:, b, :],
                              a_kbd[:, b % 2, 4 * t:4 * t + 4, :].rearrange("p h t -> p (h t)"), start=True, stop=True)
                last.then_inc(A["s_ps"], 1)

            def a_pv(g, b):
                yield
                pe.wait_ge(A["p_r"], 4 * g + b + 1)
                for f in range(2):
                    yield
                    if f == 1 or b > 0:
                        pe.wait_ge(A["pt_r"], 8 * g + 2 * b + f)
                    for h in range(4 * f, 4 * f + 4):
                        last = tp(PA[:, 2, (h % 4) * T:(h % 4) * T + T], a_p[:, h, :], ident[:])
                    last.then_inc(A["pt_ps"], 1)
                yield
                pe.wait_ge(A["pt_r"], 8 * g + 2 * b + 2)
                if b == 0:
                    pe.wait_ge(A["v_r"], g + 1)
                if b == 2:
                    pe.wait_ge(A["o_r"], 2 * g + 1)
                for h in range(H0):
                    c = (b % 2) * H0 * 17 + h * 17
                    last = mm(PA[:, 3, c:c + 17], a_pt[:, h, :], vaug[:, b, h % 4, :], start=True, stop=True)
                last.then_inc(A["pv_ps"], 1)

            def a_proj(g):
                yield from a_norm_T(g, 1, 2)
                yield
                pe.wait_ge(A["xnT_r"], 3 * g + 2)
                for b in range(GB):
                    last = mm(PA[:, 0, b * T:b * T + T], a_xnT[:, b, :], woe[:], start=True, stop=True)
                last.then_inc(A["y_ps"], 1)
                yield from a_norm_T(g, 2, 1)
                yield
                pe.wait_ge(A["xnT_r"], 3 * g + 3)

            def a_slot(g, t):
                u = 3 * g + t
                yield
                pe.wait_ge(A["sn_r"], u + 1)
                for b in range(GB):
                    last = tp(PA[:, 1, b * T:b * T + T], sn[:, b, :], ident[:])
                last.then_inc(A["snT_ps"], 1)
                mm(PA[:, 0, :], whh[:, 0:128], hT[:], start=True, stop=False, skip_group_check=True)
                yield
                pe.wait_ge(A["snT_r"], u + 1)
                for b in range(GB):
                    last = mm(PA[0:MC, 2, b * T:b * T + T], kq[:, b, :], snT[:, b, :], start=True, stop=True)
                last.then_inc(A["sc_ps"], 1)
                yield
                pe.wait_ge(A["at_r"], u + 1)
                for b in range(GB):
                    last = tp(PA[:, 3, b * MC:b * MC + MC], s_at[:, b, :], ident[0:MC, 0:MC])
                last.then_inc(A["at_ps"], 1)
                mm(PA[:, 2, :], whh[:, 128:256], hT[:], start=True, stop=False, skip_group_check=True)
                yield
                pe.wait_ge(A["an_r"], u + 1)
                for b in range(GB):
                    last = tp(PA[0:MC, 1, b * T:b * T + T], s_an[:, b, :], ident[:])
                last.then_inc(A["anT_ps"], 1)
                mm(PA[:, 3, :], whh[:, 256:384], hT[:], start=True, stop=True).then_inc(A["g_ps"], 1)
                yield
                pe.wait_ge(A["anT_r"], u + 1)
                for k, bank in ((0, 0), (1, 2), (2, 1)):
                    for b in range(GB):
                        last = mm(PA[:, bank, b * T:b * T + T], vw[:, b, 128 * k:128 * k + 128], s_anT[:, b, :],
                                  start=(k == 2), stop=True, skip_group_check=True)
                    last.then_inc(A["g_ps"], 1)
                yield
                pe.wait_ge(A["h_r"], u + 1)
                for b in range(GB):
                    last = tp(PA[:, 0, b * T:b * T + T], hT[:, b * T:b * T + T], ident[:])
                last.then_inc(A["hp_ps"], 1)

            def thread_a(g):
                yield from a_ctx(g)
                yield from a_qkv(g)
                yield from a_scores(g, 0)
                for b in range(GB):
                    if b + 1 < GB:
                        yield from a_scores(g, b + 1)
                    yield from a_pv(g, b)
                yield from a_proj(g)
                for t in range(3):
                    yield from a_slot(g, t)

            def b_norm_T(g, u):
                for b in range(GB):
                    yield
                    pe.wait_ge(B["xn_r"], 16 * g + 4 * u + b + 1)
                    last = tp(PB[:, 0, b * T:b * T + T], b_xn[:, b, :], ident[:])
                last.then_inc(B["xnT_ps"], 1)
                yield
                pe.wait_ge(B["xnT_r"], 4 * g + u + 1)

            xnT_all = b_xnT[:].rearrange("p b t -> p (b t)")

            def b_moe_up(g):
                yield from b_norm_T(g, 0)
                for b in range(GB):
                    last = mm(PB[:, 1, b * NE:b * NE + NE], b_xnT[:, b, :], mgate[:], start=True, stop=True)
                last.then_inc(B["mg_ps"], 1)
                for c in range(NCH):
                    yield
                    if c >= 2:
                        pe.wait_ge(B["relu_r"], NCH * g + c - 1)
                    mm(PB[:, 2 + c % 2, :], wup[:, 128 * c:128 * c + 128], xnT_all, start=True,
                       stop=True).then_inc(B["up_ps"], 1)

            def b_moe_down(g, b):
                yield
                if b == 0:
                    pe.wait_ge(B["sqv_r"], 8 * g + 8)
                    pe.wait_ge(B["sqp_r"], 8 * g + 8)
                    pe.wait_ge(B["mt_r"], g + 1)
                for f in range(2):
                    yield
                    if b > 0:
                        pe.wait_ge(B["x3_r"], 8 * g + 2 * b - 1 + f)
                    for e in range(4 * f, 4 * f + 4):
                        for k in range(2):
                            last = mm(PB[:, f, (e % 4) * 128:(e % 4) * 128 + 128],
                                      m_h[:, 2 * e + k, b * T:b * T + T], wdn[:, 2 * e + k, :],
                                      start=(k == 0), stop=(k == 1))
                    last.then_inc(B["dn_ps"], 1)

            def b_qkv(g):
                yield from b_norm_T(g, 1)
                mm(PB[:, 3, :], wkv1[:, 0:128], xnT_all, start=True, stop=True).then_inc(B["k_ps"], 1)
                for b in range(GB):
                    last = mm(PB[:, 0, b * T:b * T + T], b_xnT[:, b, :], wkv1[:, 128:256], start=True, stop=True)
                last.then_inc(B["v_ps"], 1)
                for h in range(H1):
                    yield
                    if h >= 2:
                        pe.wait_ge(B["q_r"], 8 * g + h - 1)
                    mm(PB[:, 1 + h % 2, :], wq1[:, 128 * h:128 * h + 128], xnT_all, start=True,
                       stop=True).then_inc(B["q_ps"], 1)

            def b_scores(g, b):
                yield
                if b == 0:
                    pe.wait_ge(B["q_r"], 8 * g + 8)
                    pe.wait_ge(B["k_r"], g + 1)
                    pe.wait_ge(B["v_r"], g + 1)
                else:
                    pe.wait_ge(B["ss_r"], 4 * g + b)
                for f in range(2):
                    mm(PB[:, f, :], ident16[:], cmask16[:], start=True, stop=False, skip_group_check=True)
                    for h in range(4 * f, 4 * f + 4):
                        last = mm(PB[:, f, (h % 4) * T:(h % 4) * T + T], q1[:, h, b * T:b * T + T], k1[:, b, :],
                                  start=False, stop=True, skip_group_check=True)
                last.then_inc(B["s_ps"], 1)

            def b_pv(g, b):
                yield
                pe.wait_ge(B["pn_r"], 4 * g + b + 1)
                if b > 0:
                    pe.wait_ge(B["x4_r"], 4 * g + b)
                for f in range(2):
                    for h in range(4 * f, 4 * f + 4):
                        last = tp(PB[:, 2 + f, (h % 4) * T:(h % 4) * T + T], b_pn[:, h, :], ident[:])
                    last.then_inc(B["pt_ps"], 1)
                for f in range(2):
                    yield
                    pe.wait_ge(B["pt_r"], 8 * g + 2 * b + f + 1)
                    mm(PB[:, 2 + f, :], v1[:, b, :], b_pt[:, 4 * f:4 * f + 4, :].rearrange("p h t -> p (h t)"),
                       start=True, stop=True).then_inc(B["ot_ps"], 1)
                yield
                pe.wait_ge(B["ot_r"], 8 * g + 2 * b + 2)
                for h in range(H1):
                    last = mm(PB[:, 2, 0:128], b_ot[:, h, :], wo1[:, h, :], start=(h == 0), stop=(h == H1 - 1))
                last.then_inc(B["wo_ps"], 1)

            def b_xqkv(g):
                yield from b_norm_T(g, 2)
                mm(PB[:, 1, :], ywq[:], xnT_all, start=True, stop=True).then_inc(B["xq_ps"], 1)
                yield
                pe.wait_ge(cT_loaded, 16 * g + 16)
                mm(PB[:, 2, 0:GM], ywk[:], cT[:].rearrange("p b m -> p (b m)"), start=True,
                   stop=True).then_inc(B["xk_ps"], 1)
                for b in range(GB):
                    last = mm(PB[0:MC, 3, b * D:b * D + D], cT[:, b, :], ywv[:], start=True, stop=True)
                last.then_inc(B["xv_ps"], 1)
                yield
                pe.wait_ge(B["xk_r"], g + 1)
                pe.wait_ge(B["xv_r"], g + 1)
                for i, (j, w) in enumerate(JT):
                    yield
                    if i >= 2:
                        pe.wait_ge(B["vbd_r"], 5 * g + i - 1)
                    mm(PB[0:w, 2 + i % 2, :], sel[:, j:j + w], vx[:].rearrange("p b d -> p (b d)"),
                       start=True, stop=True).then_inc(B["vbd_ps"], 1)

            def b_xscores(g, b):
                yield
                if b == 0:
                    pe.wait_ge(B["xq_r"], g + 1)
                    pe.wait_ge(B["kbd_r"], g + 1)
                else:
                    pe.wait_ge(B["xss_r"], 4 * g + b)
                mm(PB[:, 0, 0:OFF[1]], qx[:, b, :], kbd[:, b, 0:OFF[1]], start=True, stop=True)
                mm(PB[:, 1, 0:JX - OFF[1]], qx[:, b, :], kbd[:, b, OFF[1]:JX], start=True,
                   stop=True).then_inc(B["xs_ps"], 1)

            def b_xpv(g, b):
                yield
                if b == 0:
                    pe.wait_ge(B["vbd_r"], 5 * g + 5)
                else:
                    pe.wait_ge(B["xo_r"], 4 * g + b)
                pe.wait_ge(B["xpn_r"], 4 * g + b + 1)
                for i, (j, w) in enumerate(JT):
                    dst = PB[0:w, 2, i * T:i * T + T] if i < 4 else PB[0:w, 3, 0:T]
                    last = tp(dst, x_pn[:, j:j + w], ident[:])
                last.then_inc(B["xpt_ps"], 1)
                yield
                pe.wait_ge(B["xpt_r"], 4 * g + b + 1)
                for i, (j, w) in enumerate(JT):
                    last = mm(PB[:, 3, T:2 * T], vbd[0:w, i, b, :], x_pt[0:w, i, :], start=(i == 0),
                              stop=(i == len(JT) - 1))
                last.then_inc(B["xo_ps"], 1)

            def b_xout(g):
                yield
                pe.wait_ge(B["xo_r"], 4 * g + 4)
                for b in range(GB):
                    last = mm(PB[:, 0, b * T:b * T + T], x_oT[:, b, :], ywo[:], start=True, stop=True)
                last.then_inc(B["xy_ps"], 1)

            def b_ffn(g):
                yield from b_norm_T(g, 3)
                for b in range(GB):
                    last = mm(PB[:, 1, b * NE:b * NE + NE], b_xnT[:, b, :], fgate[:], start=True, stop=True)
                last.then_inc(B["fg_ps"], 1)
                yield
                pe.wait_ge(B["fw_r"], g + 1)
                for b in range(GB):
                    last = tp(PB[0:NE, 1, b * T:b * T + T], f_w[:, b, :], ident[:])
                last.then_inc(B["fwT_ps"], 1)
                yield
                pe.wait_ge(B["fwT_r"], g + 1)
                for b in range(GB):
                    last = mm(PB[:, 0, b * T:b * T + T], f_wT[:, b, :], fb[:], start=True, stop=True)
                last.then_inc(B["fb_ps"], 1)
                for b in range(GB):
                    for f in range(2):
                        yield
                        if b > 0:
                            pe.wait_ge(B["y_r"], 8 * g + 2 * b - 1 + f)
                        mm(PB[:, 2 + f, :], b_xnT[:, b, :], fw[:, 4 * f:4 * f + 4, :].rearrange("p e d -> p (e d)"),
                           start=True, stop=True).then_inc(B["ff_ps"], 1)

            def thread_b(g):
                yield from b_moe_up(g)
                for b in range(GB):
                    yield from b_moe_down(g, b)
                yield from b_qkv(g)
                yield from b_scores(g, 0)
                for b in range(GB):
                    if b + 1 < GB:
                        yield from b_scores(g, b + 1)
                    yield from b_pv(g, b)
                yield from b_xqkv(g)
                yield from b_xscores(g, 0)
                for b in range(GB):
                    if b + 1 < GB:
                        yield from b_xscores(g, b + 1)
                    yield from b_xpv(g, b)
                yield from b_xout(g)
                yield from b_ffn(g)

            alone(thread_a(0))
            with pe.Fori(0, NG - 1) as g:
                weave(ORDER["pe"], thread_a(g + 1), thread_b(g))
            alone(thread_b(NG - 1))

        @block.scalar
        def _(act):
            f = nc.scalar.activation

            act.wait_ge(set_vec, 3)
            f(lam_e[:], lam_s[:], ACT.Exp).then_inc(set_act, 1)
            act.wait_ge(set_vec, 17)

            def a_ctx(g, first):
                yield
                if not first:
                    act.wait_ge(x2_ready, g)
                act.wait_ge(c_loaded, 16 * g + 16)
                for b in range(GB):
                    last = f(a_junk[0:MC, b, :], cin[:, b, :], ACT.Square, accum_out=css[:, b:b + 1])
                last.then_inc(A["css_r"], 1)
                yield
                act.wait_ge(A["cnT_ps"], g + 1)
                f(cnT[:], PA[:, 1, 0:GM], ACT.Copy).then_inc(A["cnT_r"], 1)
                for b, bank in enumerate((3, 0, 1, 2)):
                    yield
                    act.wait_ge(A["vw_ps"], 4 * g + b + 1)
                    f(vw[:, b, :], PA[0:MC, bank, 0:384], ACT.Copy).then_inc(A["vw_r"], 1)

            def a_xnT_out(g, u, bank, dst):
                yield
                act.wait_ge(A["xnT_ps"], 3 * g + u + 1)
                f(dst, PA[:, bank, :], ACT.Copy).then_inc(A["xnT_r"], 1)

            def a_q(g):
                yield from a_xnT_out(g, 0, 0, a_xnT[:].rearrange("p b t -> p (b t)"))
                yield
                act.wait_ge(A["qk_ps"], 2 * g + 1)
                f(qT[:].rearrange("p b t -> p (b t)"), PA[:, 1, :], ACT.Identity,
                  bias=vcol[:, V_BQ:V_BQ + 1]).then_inc(A["qT_r"], 1)

            def a_exp(g, b):
                yield
                act.wait_ge(A["ss_r"], 4 * g + b + 1)
                if b > 0:
                    act.wait_ge(A["pt_ps"], 8 * g + 2 * b)
                f(a_p[:], a_ss[:], ACT.Exp, scale=HD0 ** -0.5).then_inc(A["p_r"], 1)

            def a_pt_out(g, b):
                for h in range(2):
                    yield
                    act.wait_ge(A["pt_ps"], 8 * g + 2 * b + h + 1)
                    if b > 0 and h == 0:
                        act.wait_ge(A["pv_ps"], 4 * g + b)
                    f(a_pt[:, 4 * h:4 * h + 4, :].rearrange("p h t -> p (h t)"), PA[:, 2, :],
                      ACT.Copy).then_inc(A["pt_r"], 1)

            def a_slot(g, t):
                u = 3 * g + t
                yield
                if t > 0:
                    act.wait_ge(A["hp_ps"], u)
                for b in range(GB):
                    src = a_xn[:, b, :] if t == 0 else PA[:, 0, b * T:b * T + T]
                    last = f(a_junk[:, b, :], src, ACT.Square, accum_out=s_sq[:, b:b + 1])
                last.then_inc(A["sq_r"], 1)
                yield
                act.wait_ge(A["snT_ps"], u + 1)
                f(snT[:].rearrange("p b t -> p (b t)"), PA[:, 1, :], ACT.Copy).then_inc(A["snT_r"], 1)
                yield
                act.wait_ge(A["ex_r"], u + 1)
                f(s_e[:], s_ex[:], ACT.Exp, scale=D ** -0.5).then_inc(A["e_r"], 1)
                yield
                act.wait_ge(A["anT_ps"], u + 1)
                f(s_anT[:].rearrange("p b t -> p (b t)"), PA[0:MC, 1, :], ACT.Copy).then_inc(A["anT_r"], 1)
                yield
                act.wait_ge(A["g_ps"], 4 * u + 2)
                f(g_tr[:], PA[:, 0, :], ACT.Tanh, scale=0.5, bias=rzb[:, 0:1]).then_inc(A["tr_r"], 1)
                yield
                act.wait_ge(A["g_ps"], 4 * u + 3)
                f(g_tz[:], PA[:, 2, :], ACT.Tanh, scale=0.5, bias=rzb[:, 1:2]).then_inc(A["tz_r"], 1)
                yield
                act.wait_ge(A["pre_r"], u + 1)
                f(g_n[:], g_q[:], ACT.Tanh, bias=vcol[:, V_BIH + 2:V_BIH + 3]).then_inc(A["n_r"], 1)

            def thread_a(g, first=False):
                yield from a_ctx(g, first)
                yield from a_q(g)
                yield from a_exp(g, 0)
                for b in range(GB):
                    yield from a_pt_out(g, b)
                    if b + 1 < GB:
                        yield from a_exp(g, b + 1)
                yield from a_xnT_out(g, 1, 2, a_xnT[:].rearrange("p b t -> p (b t)"))
                yield from a_xnT_out(g, 2, 1, hT[:])
                for t in range(3):
                    yield from a_slot(g, t)

            def b_xnT_out(g, u):
                yield
                act.wait_ge(B["xnT_ps"], 4 * g + u + 1)
                f(b_xnT[:].rearrange("p b t -> p (b t)"), PB[:, 0, :], ACT.Copy).then_inc(B["xnT_r"], 1)

            def b_moe(g):
                yield from b_xnT_out(g, 0)
                yield
                act.wait_ge(B["mg_ps"], g + 1)
                f(m_t[:].rearrange("p b e -> p (b e)"), PB[:, 1, 0:GB * NE], ACT.Tanh,
                  scale=0.5).then_inc(B["mt_r"], 1)
                for c in range(NCH):
                    yield
                    act.wait_ge(B["up_ps"], NCH * g + c + 1)
                    if c >= 4:
                        act.wait_ge(B["sqp_r" if c % 2 else "sqv_r"], 8 * g + c // 2 - 1)
                    f(m_r[:, c % 4, :], PB[:, 2 + c % 2, :], ACT.Relu).then_inc(B["relu_r"], 1)

            def b_v(g):
                yield from b_xnT_out(g, 1)
                yield
                act.wait_ge(B["v_ps"], g + 1)
                f(v1[:].rearrange("p b d -> p (b d)"), PB[:, 0, :], ACT.Copy).then_inc(B["v_r"], 1)

            def b_exp(g, b):
                yield
                act.wait_ge(B["ss_r"], 4 * g + b + 1)
                if b > 0:
                    act.wait_ge(B["pn_r"], 4 * g + b)
                f(b_p, b_ss, ACT.Exp, scale=D ** -0.5).then_inc(B["p_r"], 1)

            def b_pt_out(g, b):
                for h in range(2):
                    yield
                    act.wait_ge(B["pt_ps"], 8 * g + 2 * b + h + 1)
                    f(b_pt[:, 4 * h:4 * h + 4, :].rearrange("p h t -> p (h t)"), PB[:, 2 + h, :],
                      ACT.Copy).then_inc(B["pt_r"], 1)
                for h in range(2):
                    yield
                    act.wait_ge(B["ot_ps"], 8 * g + 2 * b + h + 1)
                    f(b_ot[:, 4 * h:4 * h + 4, :].rearrange("p h t -> p (h t)"), PB[:, 2 + h, :], ACT.Identity,
                      bias=vcol[:, V_BV1:V_BV1 + 1]).then_inc(B["ot_r"], 1)

            def b_xqkv(g):
                yield from b_xnT_out(g, 2)
                yield
                act.wait_ge(B["xq_ps"], g + 1)
                f(qx[:].rearrange("p b t -> p (b t)"), PB[:, 1, :], ACT.Identity,
                  bias=vcol[:, V_XBQ:V_XBQ + 1]).then_inc(B["xq_r"], 1)
                yield
                act.wait_ge(B["xk_ps"], g + 1)
                f(kx[:].rearrange("p b m -> p (b m)"), PB[:, 2, 0:GM], ACT.Identity,
                  bias=vcol[:, V_XBK:V_XBK + 1]).then_inc(B["xk_r"], 1)
                yield
                act.wait_ge(B["xv_ps"], g + 1)
                f(vx[:].rearrange("p b d -> p (b d)"), PB[0:MC, 3, :], ACT.Copy).then_inc(B["xv_r"], 1)

            def b_xexp(g, b):
                yield
                act.wait_ge(B["xss_r"], 4 * g + b + 1)
                if b > 0:
                    act.wait_ge(B["xpn_r"], 4 * g + b)
                f(x_p, x_ss, ACT.Exp, scale=HDX ** -0.5).then_inc(B["xp_r"], 1)

            def b_xpt_out(g, b):
                yield
                act.wait_ge(B["xpt_ps"], 4 * g + b + 1)
                f(x_pt[:, 0:4, :].rearrange("p j t -> p (j t)"), PB[:, 2, :], ACT.Copy)
                f(x_pt[0:JT[4][1], 4, :], PB[0:JT[4][1], 3, 0:T], ACT.Copy).then_inc(B["xpt_r"], 1)
                yield
                act.wait_ge(B["xo_ps"], 4 * g + b + 1)
                f(x_oT[:, b, :], PB[:, 3, T:2 * T], ACT.Identity,
                  bias=vcol[:, V_XBV:V_XBV + 1]).then_inc(B["xo_r"], 1)

            def b_ffn(g):
                yield from b_xnT_out(g, 3)
                yield
                act.wait_ge(B["fs_r"], g + 1)
                f(f_e[:], f_s[:], ACT.Exp).then_inc(B["fe_r"], 1)
                yield
                act.wait_ge(B["fwT_ps"], g + 1)
                f(f_wT[:].rearrange("p b t -> p (b t)"), PB[0:NE, 1, :], ACT.Copy).then_inc(B["fwT_r"], 1)

            def thread_b(g):
                yield from b_moe(g)
                yield from b_v(g)
                yield from b_exp(g, 0)
                for b in range(GB):
                    if b + 1 < GB:
                        yield from b_exp(g, b + 1)
                    yield from b_pt_out(g, b)
                yield from b_xqkv(g)
                yield from b_xexp(g, 0)
                for b in range(GB):
                    if b + 1 < GB:
                        yield from b_xexp(g, b + 1)
                    yield from b_xpt_out(g, b)
                yield from b_ffn(g)

            alone(thread_a(0, first=True))
            with act.Fori(0, NG - 1) as g:
                weave(ORDER["act"], thread_a(g + 1), thread_b(g))
            alone(thread_b(NG - 1))

        @block.gpsimd
        def _(pool):
            tt = nc.gpsimd.tensor_tensor
            pool.wait_ge(set_vec, 17)

            def a_ctx(g):
                yield
                pool.wait_ge(A["cve_r"], g + 1)
                tt(crs[:], cve[:], mhalf[0:MC, :], ALU.pow).then_inc(A["crs_r"], 1)
                yield
                pool.wait_ge(x_loaded, 16 * g + 16)
                tt(xc[:], xin[:], cb1[:].unsqueeze(1).to_broadcast([128, GB, D]), ALU.add).then_inc(A["xc_r"], 1)

            def a_rstd_(g, u):
                yield
                pool.wait_ge(A["var_r"], 3 * g + u + 1)
                tt(a_rstd[:], a_ve[:], mhalf[:], ALU.pow).then_inc(A["rstd_r"], 1)

            def a_keys(g, b):
                yield
                if b == 0:
                    pool.wait_ge(A["kT_r"], g + 1)
                if b >= 2:
                    pool.wait_ge(A["s_ps"], 4 * g + b - 1)
                tt(a_kbd[:, b % 2, :, :], kT[:, b, :].unsqueeze(1).to_broadcast([128, H0, T]),
                   hmask[:].unsqueeze(2).to_broadcast([128, H0, T]), ALU.mult).then_inc(A["kbd_r"], 1)

            def a_slot(g, t):
                yield
                pool.wait_ge(A["sve_r"], 3 * g + t + 1)
                tt(s_rs[:], s_ve[:], mhalf[:], ALU.pow).then_inc(A["srs_r"], 1)

            def thread_a(g):
                yield from a_ctx(g)
                yield from a_rstd_(g, 0)
                for b in range(GB):
                    yield from a_keys(g, b)
                yield from a_rstd_(g, 1)
                yield from a_rstd_(g, 2)
                for t in range(3):
                    yield from a_slot(g, t)

            def b_rstd_(g, u):
                yield
                pool.wait_ge(B["var_r"], 4 * g + u + 1)
                tt(b_rstd[:], b_ve[:], mhalf[:], ALU.pow).then_inc(B["rstd_r"], 1)

            def b_squares(g):
                for c in range(1, NCH, 2):
                    yield
                    pool.wait_ge(B["relu_r"], NCH * g + c + 1)
                    tt(m_h[:, c, :], m_r[:, c % 4, :], m_r[:, c % 4, :], ALU.mult).then_inc(B["sqp_r"], 1)

            def b_probs(g, b):
                yield
                pool.wait_ge(B["rs_r"], 4 * g + b + 1)
                if b > 0:
                    pool.wait_ge(B["pt_ps"], 8 * g + 2 * b)
                tt(b_pn[:], b_p, b_rs[:].unsqueeze(2).to_broadcast([128, H1, T]), ALU.mult).then_inc(B["pn_r"], 1)

            def b_xprobs(g, b):
                yield
                pool.wait_ge(B["xrs_r"], 4 * g + b + 1)
                if b > 0:
                    pool.wait_ge(B["xpt_ps"], 4 * g + b)
                for c in range(NCLS):
                    v = lambda ap: ap[:, OFF[c]:OFF[c + 1]].rearrange("p (h k) -> p h k", h=4)
                    last = tt(v(x_pn), v(x_p), x_rs[:, 4 * c:4 * c + 4].unsqueeze(2).to_broadcast([128, 4, NK[c]]),
                              ALU.mult)
                last.then_inc(B["xpn_r"], 1)

            def thread_b(g):
                yield from b_rstd_(g, 0)
                yield from b_squares(g)
                yield from b_rstd_(g, 1)
                for b in range(GB):
                    yield from b_probs(g, b)
                yield from b_rstd_(g, 2)
                tt(x4b[:], x4[:], ybo[:].unsqueeze(1).to_broadcast([128, GB, D]), ALU.add).then_inc(B["x4b_r"], 1)
                for b in range(GB):
                    yield from b_xprobs(g, b)
                yield from b_rstd_(g, 3)

            alone(thread_a(0))
            with pool.Fori(0, NG - 1) as g:
                weave(ORDER["pool"], thread_a(g + 1), thread_b(g))
            alone(thread_b(NG - 1))

        STEPS_A, STEPS_B = STEPS

        @block.vector
        def _(dve):
            v = nc.vector
            bc = lambda ap, n: ap.unsqueeze(2).to_broadcast([*ap.shape, n])

            class Steps:

                def __init__(self, s, per_group):
                    self.s, self.per_group = s, per_group

                def begin(self, g):
                    self.base, self.n = g * self.per_group, 0

                def then(self, ins):
                    ins.then_inc(self.s, 1)
                    self.n += 1
                    dve.wait_ge(self.s, self.base + self.n)

            sa, sbx = Steps(A["a_step"], STEPS_A), Steps(B["b_step"], STEPS_B)

            count = [0]

            def setup(ins):
                ins.then_inc(set_vec, 1)
                count[0] += 1
                dve.wait_ge(set_vec, count[0])

            v.memset(vaug[:], 1.0)
            v.memset(mhalf[:], -0.5)
            setup(v.memset(vrow[:], 0.0))
            dve.wait_ge(w_loaded, N_LOADS)
            setup(v.tensor_tensor(lam_pr[:], lam_in[:, 0::2, :], lam_in[:, 1::2, :], ALU.mult))
            setup(v.tensor_reduce(lam_s[:], lam_pr[:], AX.X, ALU.add))
            setup(v.tensor_copy(ident16[:], ident[:]))
            setup(v.tensor_copy(cmask16[:], cmask))
            dve.wait_ge(set_act, 1)
            setup(v.tensor_tensor(nlam[:], lam_e[:, 1:2], lam_e[:, 0:1], ALU.subtract))
            setup(v.tensor_scalar(nlam[:], nlam[:], LAMBDA_INIT, None, ALU.subtract))
            dve.wait_ge(set_pe, 1)
            setup(v.tensor_copy(vcol[:], PA[:, 0, 0:NV]))
            setup(v.scalar_tensor_tensor(wvc[:], wv0[:, 64:128], nlam[:, 0:1], wv0[:, 0:64], ALU.mult, ALU.add))
            setup(v.scalar_tensor_tensor(bvc[:], bv0[:, 64:128], nlam[:, 0:1], bv0[:, 0:64], ALU.mult, ALU.add))
            setup(v.tensor_scalar(woe[:], wo0, vcol[:, V_LNW:V_LNW + 1], 1.0 - LAMBDA_INIT, ALU.mult, ALU.mult))
            setup(v.tensor_scalar(lnb, vcol[:, V_LNB:V_LNB + 1].to_broadcast([128, 128]), 1.0 - LAMBDA_INIT, None,
                                  ALU.mult))
            dve.wait_ge(set_pe, 2)
            setup(v.tensor_scalar(wqk[:], PA[:, 1, 0:128], vcol[:, V_WIN:V_WIN + 1], None, ALU.mult))
            dve.wait_ge(set_pe, 3)
            setup(v.tensor_scalar(wvi[:], PA[:, 2, 0:384], vcol[:, V_WIN:V_WIN + 1], None, ALU.mult))
            dve.wait_ge(set_pe, 4)
            setup(v.tensor_tensor(cb1[:], PA[:, 3, 0:128], cb1[:], ALU.add))
            setup(v.tensor_tensor(rzb[:], vcol[:, V_BIH:V_BIH + 2], vcol[:, V_BHH:V_BHH + 2], ALU.add))
            setup(v.tensor_scalar(rzb[:], rzb[:], 0.5, None, ALU.mult))

            def hold(st):
                v.memset(held[:, 0:1] if st is sa else held[:, 1:2], 0.0)

            def norm(st, S, src, dst, stt, mv, ve, rstd, uses, u, g):
                for b in range(GB):
                    last = v.bn_stats(stt[:, b, :], src[:, b, :])
                st.then(last)
                hold(st)
                for b in range(GB):
                    last = v.bn_aggr(mv[:, b, :], stt[:, b, :])
                st.then(last)
                v.tensor_scalar(ve[:], mv[:, :, 1], LN_EPS, None, ALU.add).then_inc(S["var_r"], 1)
                yield
                dve.wait_ge(S["rstd_r"], uses * g + u + 1)
                for b in range(GB):
                    v.tensor_scalar(dst[:, b, :], src[:, b, :], mv[:, b, 0:1], rstd[:, b:b + 1], ALU.subtract,
                                    ALU.mult).then_inc(S["xn_r"], 1)

            def a_norm(g, u, src):
                yield from norm(sa, A, src, a_xn, a_st, a_mv, a_ve, a_rstd, 3, u, g)

            def b_norm(g, u, src):
                yield from norm(sbx, B, src, b_xn, b_st, b_mv, b_ve, b_rstd, 4, u, g)

            def a_ctx(g):
                yield
                dve.wait_ge(A["css_r"], g + 1)
                v.tensor_scalar(cve[:], css[:], 1.0 / D, RMS_EPS, ALU.mult, ALU.add).then_inc(A["cve_r"], 1)
                yield
                dve.wait_ge(A["crs_r"], g + 1)
                for b in range(GB):
                    last = v.tensor_scalar(cn[:, b, :], cin[:, b, :], crs[:, b:b + 1], None, ALU.mult)
                last.then_inc(A["cn_r"], 1)
                yield
                dve.wait_ge(A["kq_ps"], g + 1)
                v.tensor_scalar(kq[:].rearrange("p b m -> p (b m)"), PA[:, 2, 0:GM], vcol[:, V_WS:V_WS + 1], None,
                                ALU.mult).then_inc(A["kq_r"], 1)

            def a_kv(g):
                yield
                dve.wait_ge(A["qk_ps"], 2 * g + 2)
                v.tensor_scalar(kT[:].rearrange("p b t -> p (b t)"), PA[:, 2, :],
                                vcol[:, V_BK:V_BK + 1], None, ALU.add).then_inc(A["kT_r"], 1)
                yield
                dve.wait_ge(A["v_ps"], g + 1)
                v.tensor_tensor(vaug[:, :, :, 0:HD0], PA[:, 3, 0:256].rearrange("p (b j d) -> p b j d", b=GB, d=HD0),
                                bvc[:].rearrange("p (j d) -> p j d", d=HD0).unsqueeze(1).to_broadcast([128, GB, 4, HD0]),
                                ALU.add).then_inc(A["v_r"], 1)

            def a_soft(g, b):
                yield
                dve.wait_ge(A["s_ps"], 4 * g + b + 1)
                s = PA[:, 0:2, :].rearrange("p k (h t) -> p (k h) t", h=4)
                sa.then(v.tensor_reduce(a_mx[:], s, AX.X, ALU.max))
                yield
                if b > 0:
                    dve.wait_ge(A["p_r"], 4 * g + b)
                v.tensor_tensor(a_ss[:], s, bc(a_mx[:], T), ALU.subtract).then_inc(A["ss_r"], 1)

            def a_heads(g, p):
                yield
                dve.wait_ge(A["pv_ps"], 4 * g + 2 * p + 2)
                s = PA[:, 3, 0:2 * H0 * 17].rearrange("p (n d) -> p n d", d=17)
                sa.then(v.reciprocal(a_rd[:], s[:, :, 16]))
                v.tensor_tensor(a_o[:, 2 * p:2 * p + 2, :].rearrange("p b (h d) -> p (b h) d", d=HD0),
                                s[:, :, 0:HD0], bc(a_rd[:], HD0), ALU.mult).then_inc(A["o_r"], 1)

            def a_slot(g, t):
                u = 3 * g + t
                yield
                dve.wait_ge(A["sq_r"], u + 1)
                v.tensor_scalar(s_ve[:], s_sq[:], 1.0 / D, RMS_EPS, ALU.mult, ALU.add).then_inc(A["sve_r"], 1)
                yield
                dve.wait_ge(A["srs_r"], u + 1)
                for b in range(GB):
                    src = a_xn[:, b, :] if t == 0 else PA[:, 0, b * T:b * T + T]
                    last = v.tensor_scalar(sn[:, b, :], src, s_rs[:, b:b + 1], None, ALU.mult)
                last.then_inc(A["sn_r"], 1)
                yield
                dve.wait_ge(A["sc_ps"], u + 1)
                s = PA[0:MC, 2, :].rearrange("p (b t) -> p b t", b=GB)
                sa.then(v.tensor_reduce(s_mx[:], s, AX.X, ALU.max))
                v.tensor_tensor(s_ex[:], s, bc(s_mx[:], T), ALU.subtract).then_inc(A["ex_r"], 1)
                yield
                dve.wait_ge(A["e_r"], u + 1)
                sa.then(v.tensor_reduce(s_sum[:], s_e[:], AX.X, ALU.add))
                sa.then(v.reciprocal(s_rsum[:], s_sum[:]))
                v.tensor_tensor(s_at[:], s_e[:], bc(s_rsum[:], T), ALU.mult).then_inc(A["at_r"], 1)
                yield
                dve.wait_ge(A["at_ps"], u + 1)
                s = PA[:, 3, 0:GM].rearrange("p (b m) -> p b m", b=GB)
                sa.then(v.tensor_reduce(s_row[:], s, AX.X, ALU.add))
                sa.then(v.tensor_scalar(s_rowe[:], s_row[:], RMS_EPS, None, ALU.add))
                sa.then(v.reciprocal(s_rrow[:], s_rowe[:]))
                v.tensor_tensor(s_an[:], s, bc(s_rrow[:], MC), ALU.mult).then_inc(A["an_r"], 1)
                yield
                dve.wait_ge(A["tr_r"], u + 1)
                sa.then(v.tensor_scalar(g_tr[:], g_tr[:], 0.5, 0.5, ALU.mult, ALU.add))
                yield
                dve.wait_ge(A["g_ps"], 4 * u + 1)
                sa.then(v.scalar_tensor_tensor(g_q[:], PA[:, 3, :], vcol[:, V_BHH + 2:V_BHH + 3], g_tr[:], ALU.add,
                                               ALU.mult))
                yield
                dve.wait_ge(A["g_ps"], 4 * u + 4)
                v.tensor_tensor(g_q[:], PA[:, 1, :], g_q[:], ALU.add).then_inc(A["pre_r"], 1)
                yield
                dve.wait_ge(A["tz_r"], u + 1)
                sa.then(v.tensor_scalar(g_tz[:], g_tz[:], 0.5, 0.5, ALU.mult, ALU.add))
                yield
                dve.wait_ge(A["n_r"], u + 1)
                sa.then(v.tensor_tensor(g_d[:], hT[:], g_n[:], ALU.subtract))
                sa.then(v.tensor_tensor(g_d[:], g_d[:], g_tz[:], ALU.mult))
                v.tensor_tensor(hT[:], g_n[:], g_d[:], ALU.add).then_inc(A["h_r"], 1)

            def thread_a(g, first=False):
                sa.begin(g)
                yield from a_ctx(g)
                yield
                dve.wait_ge(x_loaded, 16 * g + 16)
                yield from a_norm(g, 0, xin)
                yield from a_kv(g)
                yield from a_soft(g, 0)
                for b in range(GB):
                    if b + 1 < GB:
                        yield from a_soft(g, b + 1)
                    if b % 2:
                        yield from a_heads(g, b // 2)
                yield
                dve.wait_ge(A["o_r"], 2 * g + 2)
                yield from a_norm(g, 1, a_o)
                yield
                dve.wait_ge(A["y_ps"], g + 1)
                dve.wait_ge(A["xc_r"], g + 1)
                sa.then(v.tensor_tensor(x1[:].rearrange("p b d -> p (b d)"), PA[:, 0, :],
                                        xc[:].rearrange("p b d -> p (b d)"), ALU.add))
                yield from a_norm(g, 2, x1)
                for t in range(3):
                    yield from a_slot(g, t)
                yield
                dve.wait_ge(A["hp_ps"], 3 * g + 3)
                if not first:
                    dve.wait_ge(B["x3_r"], 8 * g)
                v.tensor_tensor(x2[:].rearrange("p b d -> p (b d)"), PA[:, 0, :],
                                x1[:].rearrange("p b d -> p (b d)"), ALU.add).then_inc(x2_ready, 1)
                assert sa.n == STEPS_A, sa.n

            def b_route(g):
                yield
                dve.wait_ge(B["mt_r"], g + 1)
                st = sbx
                st.then(v.tensor_scalar(m_s[:], m_t[:], 0.5, 0.5, ALU.mult, ALU.add))
                st.then(v.tensor_tensor(m_b[:], m_s[:], ebias[:].unsqueeze(1).to_broadcast([128, GB, NE]), ALU.add))
                hold(st)
                for b in range(GB):
                    last = v.max(m_top[:, b, :], m_b[:, b, :])
                st.then(last)
                hold(st)
                for b in range(GB):
                    last = v.max_index(m_ix[:, b, :], m_top[:, b, :], m_b[:, b, :])
                st.then(last)
                st.then(v.tensor_copy(m_ixf[:], m_ix[:]))
                io = iota8[:].unsqueeze(1).to_broadcast([128, GB, NE])
                v.tensor_tensor(m_1[:], io, m_ixf[:, :, 0:1].to_broadcast([128, GB, NE]), ALU.is_equal)
                st.then(v.tensor_tensor(m_2[:], io, m_ixf[:, :, 1:2].to_broadcast([128, GB, NE]), ALU.is_equal))
                st.then(v.tensor_tensor(m_1[:], m_1[:], m_2[:], ALU.add))
                st.then(v.tensor_tensor(m_w[:], m_1[:], m_s[:], ALU.mult))
                st.then(v.tensor_tensor(m_w2[:], m_w[:], m_w[:], ALU.mult))

            def b_squares(g):
                for c in range(0, NCH, 2):
                    yield
                    dve.wait_ge(B["relu_r"], NCH * g + c + 1)
                    v.tensor_tensor(m_h[:, c, :], m_r[:, c % 4, :], m_r[:, c % 4, :], ALU.mult).then_inc(B["sqv_r"], 1)

            def b_combine(g, b):
                for f in range(2):
                    yield
                    dve.wait_ge(B["dn_ps"], 8 * g + 2 * b + f + 1)
                    for e in range(4 * f, 4 * f + 4):
                        ins = v.scalar_tensor_tensor(x3[:, b, :], PB[:, f, (e % 4) * 128:(e % 4) * 128 + 128],
                                                     m_w2[:, b, e:e + 1], x2[:, b, :] if e == 0 else x3[:, b, :],
                                                     ALU.mult, ALU.add)
                        if e % 4 < 3:
                            sbx.then(ins)
                    ins.then_inc(B["x3_r"], 1)
                    dve.wait_ge(B["x3_r"], 8 * g + 2 * b + f + 1)

            def b_qk(g):
                pe4 = peT[:].unsqueeze(1).to_broadcast([128, GB, T])
                yield
                dve.wait_ge(B["k_ps"], g + 1)
                v.scalar_tensor_tensor(k1[:], PB[:, 3, :].rearrange("p (b t) -> p b t", b=GB),
                                       vcol[:, V_BK1:V_BK1 + 1], pe4, ALU.add, ALU.add).then_inc(B["k_r"], 1)
                for h in range(H1):
                    yield
                    dve.wait_ge(B["q_ps"], 8 * g + h + 1)
                    v.scalar_tensor_tensor(q1[:, h, :].rearrange("p (b t) -> p b t", b=GB),
                                           PB[:, 1 + h % 2, :].rearrange("p (b t) -> p b t", b=GB),
                                           vcol[:, V_BQ1 + h:V_BQ1 + h + 1], pe4, ALU.add, ALU.add).then_inc(B["q_r"], 1)

            def b_soft(g, b):
                yield
                dve.wait_ge(B["s_ps"], 4 * g + b + 1)
                s = PB[:, 0:2, :].rearrange("p k (h t) -> p (k h) t", h=4)
                sbx.then(v.tensor_reduce(b_mx[:], s, AX.X, ALU.max))
                yield
                if b > 0:
                    dve.wait_ge(B["p_r"], 4 * g + b)
                v.tensor_tensor(b_ss, s, bc(b_mx[:], T), ALU.subtract).then_inc(B["ss_r"], 1)

            def b_sums(g, b):
                yield
                dve.wait_ge(B["p_r"], 4 * g + b + 1)
                sbx.then(v.tensor_reduce(b_sum[:], b_p, AX.X, ALU.add))
                yield
                if b > 0:
                    dve.wait_ge(B["pn_r"], 4 * g + b)
                v.reciprocal(b_rs[:], b_sum[:]).then_inc(B["rs_r"], 1)

            def b_res(g, b):
                yield
                dve.wait_ge(B["wo_ps"], 4 * g + b + 1)
                v.tensor_tensor(x4[:, b, :], PB[:, 2, 0:128], x3[:, b, :], ALU.add).then_inc(B["x4_r"], 1)

            def cls(ap, c):
                return ap[:, OFF[c]:OFF[c + 1]].rearrange("p (h k) -> p h k", h=4)

            def b_xbd(g):
                yield
                dve.wait_ge(B["xk_r"], g + 1)
                for c in range(NCLS):
                    for b in range(GB):
                        last = v.tensor_tensor(cls(kbd[:, b, :], c),
                                               kx[:, b, ::1 << c].unsqueeze(1).to_broadcast([128, 4, NK[c]]),
                                               bc(kmask[:, c, :], NK[c]), ALU.mult)
                last.then_inc(B["kbd_r"], 1)
                for i, (j, w) in enumerate(JT):
                    yield
                    dve.wait_ge(B["vbd_ps"], 5 * g + i + 1)
                    v.tensor_tensor(vbd[0:w, i, :, :], PB[0:w, 2 + i % 2, :].rearrange("p (b d) -> p b d", b=GB),
                                    vmask[0:w, i, :].unsqueeze(1).to_broadcast([w, GB, D]),
                                    ALU.mult).then_inc(B["vbd_r"], 1)

            def xps(c):
                if c == 0:
                    return PB[:, 0, 0:OFF[1]].rearrange("p (h k) -> p h k", h=4)
                return PB[:, 1, OFF[c] - OFF[1]:OFF[c + 1] - OFF[1]].rearrange("p (h k) -> p h k", h=4)

            def b_xsoft(g, b):
                yield
                dve.wait_ge(B["xs_ps"], 4 * g + b + 1)
                for c in range(NCLS):
                    last = v.tensor_reduce(x_mx[:, 4 * c:4 * c + 4], xps(c), AX.X, ALU.max)
                sbx.then(last)
                yield
                if b > 0:
                    dve.wait_ge(B["xp_r"], 4 * g + b)
                for c in range(NCLS):
                    last = v.tensor_tensor(cls(x_ss, c), xps(c), bc(x_mx[:, 4 * c:4 * c + 4], NK[c]), ALU.subtract)
                last.then_inc(B["xss_r"], 1)

            def b_xsums(g, b):
                yield
                dve.wait_ge(B["xp_r"], 4 * g + b + 1)
                for c in range(NCLS):
                    last = v.tensor_reduce(x_sum[:, 4 * c:4 * c + 4], cls(x_p, c), AX.X, ALU.add)
                sbx.then(last)
                yield
                if b > 0:
                    dve.wait_ge(B["xpn_r"], 4 * g + b)
                v.reciprocal(x_rs[:], x_sum[:]).then_inc(B["xrs_r"], 1)

            def b_mix(g):
                st = sbx
                yield
                dve.wait_ge(B["fg_ps"], g + 1)
                st.then(v.tensor_tensor(f_l[:], PB[:, 1, 0:GB * NE].rearrange("p (b e) -> p b e", b=GB),
                                        fgb[:].unsqueeze(1).to_broadcast([128, GB, NE]), ALU.add))
                st.then(v.tensor_reduce(f_mx[:], f_l[:], AX.X, ALU.max))
                v.tensor_tensor(f_s[:], f_l[:], bc(f_mx[:], NE), ALU.subtract).then_inc(B["fs_r"], 1)
                yield
                dve.wait_ge(B["fe_r"], g + 1)
                st.then(v.tensor_reduce(f_sum[:], f_e[:], AX.X, ALU.add))
                st.then(v.reciprocal(f_r[:], f_sum[:]))
                st.then(v.tensor_tensor(f_g[:], f_e[:], bc(f_r[:], NE), ALU.mult))
                st.then(v.scalar_tensor_tensor(f_w0[:], f_g[:], 0.1, f_g[:], ALU.is_ge, ALU.mult))
                st.then(v.tensor_reduce(f_ws[:], f_w0[:], AX.X, ALU.add))
                st.then(v.tensor_scalar(f_z[:], f_ws[:], 0.0, None, ALU.is_equal))
                st.then(v.tensor_tensor(f_wd[:], f_ws[:], f_z[:], ALU.add))
                st.then(v.reciprocal(f_wr[:], f_wd[:]))
                v.tensor_tensor(f_w[:], f_w0[:], bc(f_wr[:], NE), ALU.mult).then_inc(B["fw_r"], 1)
                yield
                dve.wait_ge(B["fb_ps"], g + 1)
                dve.wait_ge(out_done, 16 * g + 16)
                st.then(v.tensor_tensor(y[:].rearrange("p b d -> p (b d)"), PB[:, 0, :],
                                        x5[:].rearrange("p b d -> p (b d)"), ALU.add))
                for b in range(GB):
                    for f in range(2):
                        yield
                        dve.wait_ge(B["ff_ps"], 8 * g + 2 * b + f + 1)
                        for e in range(4 * f, 4 * f + 4):
                            ins = v.scalar_tensor_tensor(y[:, b, :], PB[:, 2 + f, (e % 4) * 128:(e % 4) * 128 + 128],
                                                         f_w[:, b, e:e + 1], y[:, b, :], ALU.mult, ALU.add)
                            if e % 4 < 3:
                                st.then(ins)
                        ins.then_inc(B["y_r"], 1)
                        if 2 * b + f < 2 * GB - 1:
                            dve.wait_ge(B["y_r"], 8 * g + 2 * b + f + 1)

            def thread_b(g):
                sbx.begin(g)
                yield
                dve.wait_ge(x2_ready, g + 1)
                yield from b_norm(g, 0, x2)
                yield from b_route(g)
                yield from b_squares(g)
                for b in range(GB):
                    yield from b_combine(g, b)
                yield from b_norm(g, 1, x3)
                yield from b_qk(g)
                yield from b_soft(g, 0)
                for b in range(GB):
                    if b + 1 < GB:
                        yield from b_sums(g, b)
                        yield from b_soft(g, b + 1)
                    else:
                        yield from b_sums(g, b)
                    yield from b_res(g, b)
                yield
                dve.wait_ge(B["x4_r"], 4 * g + 4)
                yield from b_norm(g, 2, x4)
                yield from b_xbd(g)
                yield from b_xsoft(g, 0)
                for b in range(GB):
                    yield from b_xsums(g, b)
                    if b + 1 < GB:
                        yield from b_xsoft(g, b + 1)
                yield
                dve.wait_ge(B["xy_ps"], g + 1)
                dve.wait_ge(B["x4b_r"], g + 1)
                sbx.then(v.tensor_tensor(x5[:].rearrange("p b d -> p (b d)"), PB[:, 0, :],
                                         x4b[:].rearrange("p b d -> p (b d)"), ALU.add))
                yield from b_norm(g, 3, x5)
                yield from b_mix(g)
                assert sbx.n == STEPS_B, sbx.n

            alone(thread_a(0, first=True))
            with dve.Fori(0, NG - 1) as g:
                weave(ORDER["dve"], thread_a(g + 1), thread_b(g))
            alone(thread_b(NG - 1))


def _layout(i):
    import numpy as np

    f = np.float32
    t = {k: np.asarray(v) for k, v in i.items()}
    w = {k: v for k, v in t.items() if k not in ("x", "ctx_1024")}
    w["x"] = t["x"].transpose(1, 0, 2)
    w["ctx_tok"] = t["ctx_1024"].transpose(1, 0, 2)
    w["ctx_feat"] = t["ctx_1024"].transpose(2, 0, 1)
    for n in ("L0_xattn_gru_wih", "L0_xattn_gru_whh", "L0_ffn_gate_w", "L1_xattn_Wq", "L1_xattn_Wk", "L1_xattn_Wv",
              "L1_xattn_Wo"):
        w[n] = t[n].T
    w["L0_ffn_w_up"] = t["L0_ffn_w_up"].reshape(NE * HID, D).T
    w["L0_ffn_w_down"] = t["L0_ffn_w_down"].transpose(0, 2, 1).reshape(NCH, 128, D).transpose(1, 0, 2)
    w["L1_attn_Wo"] = t["L1_attn_Wo"].reshape(H1, 128, D).transpose(1, 0, 2)
    w["L1_ffn_expert_w"] = t["L1_ffn_expert_w"].transpose(1, 0, 2)
    p = np.arange(128)
    w["c_ident"] = np.eye(128, dtype=f)
    w["c_cmask"] = np.tile(np.where(p[None, :] > p[:, None], f(-1e30), f(0)), (1, 4)).astype(f)
    ang = p.astype(f)[:, None] * np.exp(f(-np.log(10000.0)) * np.arange(0, D, 2, dtype=f) / f(D))[None, :]
    pe = np.zeros((128, D), f)
    pe[:, 0::2], pe[:, 1::2] = np.sin(ang), np.cos(ang)
    w["c_peT"] = pe.T
    sel, vm, km = np.zeros((MC, JX), f), np.zeros((len(JT) * 128, D), f), np.zeros((128, NCLS, 4), f)
    for c in range(NCLS):
        for n in range(4):
            head = c + 4 * n
            km[head * HDX:(head + 1) * HDX, c, n] = 1
            for k in range(NK[c]):
                j = OFF[c] + n * NK[c] + k
                sel[k << c, j] = 1
                vm[j, head * HDX:(head + 1) * HDX] = 1
    w["c_sel"], w["c_kmask"] = sel, km
    w["c_hmask"] = np.repeat(np.eye(H0, dtype=f), HD0, axis=0)
    w["c_vmask"] = vm.reshape(len(JT), 128, D).transpose(1, 0, 2)
    w["c_iota8"] = np.tile(np.arange(NE, dtype=f), (128, 1))
    return {k: np.ascontiguousarray(v) for k, v in w.items()}


def kernel(**inputs):
    import concourse.bacc as _bacc
    from concourse import mybir as _mybir
    from concourse.bass_utils import run_bass_kernel_spmd as _run

    nc = _bacc.Bacc("TRN2", target_bir_lowering=False, num_devices=1)
    arrays, aps = {}, {}
    for name, arr in _layout(inputs).items():
        arrays[f"in_{name}_dram"] = arr
        aps[name] = nc.dram_tensor(f"in_{name}_dram", arr.shape, _mybir.dt.from_np(arr.dtype),
                                   kind="ExternalInput").ap()
    out = nc.dram_tensor("out_0_dram", (T, NS, D), F32, kind="ExternalOutput").ap()
    build(nc, aps, out)
    r = _run(nc, [arrays], core_ids=[0])
    return r.results[0]["out_0_dram"].transpose(1, 0, 2)
```

```python
from contextlib import ExitStack

import concourse.bass as bass
from concourse import mybir

ALU = mybir.AluOpType
ACT = mybir.ActivationFunctionType
AX = mybir.AxisListType
F32 = mybir.dt.float32
F32R = mybir.dt.float32r
BF16 = mybir.dt.bfloat16
U32 = mybir.dt.uint32

NS, T, D, MC = 64, 128, 128, 77
GB = 4
NG = NS // GB
GT = GB * T
GM = GB * MC
NE, HID = 8, 256
NCH = NE * HID // 128
H0, HD0 = 8, 16
H1 = 8
HX, HDX = 16, 8
NCLS = 4
NK = [-(-MC // (1 << c)) for c in range(NCLS)]
OFF = [4 * sum(NK[:c]) for c in range(NCLS + 1)]
JX = OFF[NCLS]
JT = [(i, min(128, JX - i)) for i in range(0, JX, 128)]
LN_EPS, RMS_EPS, LAMBDA_INIT = 1e-5, 1e-6, 0.8

(V_BQ, V_BK, V_BIH, V_BHH, V_WS, V_WIN, V_LNW, V_LNB, V_BQ1, V_BK1, V_BV1, V_XBQ, V_XBK, V_XBV) = (
    0, 1, 2, 5, 8, 9, 10, 11, 12, 20, 21, 22, 23, 24)
NV = 25
STEPS = (23, 24, 53, 47)


ORDER = {
    "pe": (
        "bbabbbbbsbbcaaaacsccbabccbasacabbsabsbascsbcabbcabcbcsabcbasbasbcabcacbabsabcaacscbbbbsbsbbsbbcbbcbb"
        "cbabbabbsbcbbcbcsabsabacbcccabcsaababsbcsbcbcbcssbaacbaabasbcbbbcacaaababacabcbbabaaa"),
    "act": (
        "sbsbbbsbbacsbaccbbcabsababssbsbsbbaabbsscsaacscacaccssabsacbccssbcbbbbsbcabcsbsabbbscaababcscsbbsbsb"
        "sabbabbaabbbaaaa"),
    "pool": "bscabbabbbabbbscacabccscaaa",
    "dve": (
        "bbbccbscabaabcbabbbbbbbbssbassbassssbaaaabccbasacssbcasascscbcbsabbabbbccbbbcbcaabbbbbbsbbasbabbbbbb"
        "absasccbbbcbcbbssbabasbsbbbbbbbbaabcbcbcsscbbsbbbbbbsccaasccsaasbbccbcbbcbaasbcsbbbaassbbccssssccaac"
        "acacbacccccabbbbbabccbscccbbcccasccscccsbcscsbbbbscbabacbacccabbcaccccacccbcacbbbbccbcbccccbccaccb"),
}


def weave(order, **threads):
    for thread in threads.values():
        next(thread)
    ended = [c for c in order if c in threads and next(threads[c], "end") == "end"]
    assert sorted(ended) == sorted(threads), ended


def build(nc, a, out):
    with ExitStack() as ctx:
        def sb(name, shape, dt=F32):
            return ctx.enter_context(nc.sbuf_tensor(name, shape, dt))

        def sem(name):
            return ctx.enter_context(nc.semaphore(name))

        ident = sb("ident", [128, 128])
        ident16 = sb("ident16", [128, 128], BF16)
        cmask16 = sb("cmask16", [128, 512], BF16)
        peT = sb("peT", [128, 128])
        sel = sb("sel", [MC, JX], F32R)
        vmask = sb("vmask", [128, len(JT), 128])
        kmask = sb("kmask", [128, NCLS, 4])
        hmask = sb("hmask", [128, H0])
        iota8 = sb("iota8", [128, NE])
        mhalf = sb("mhalf", [128, GB])
        warm = sb("warm", [128, 1])
        held = sb("held", [1, 3])
        vrow = sb("vrow", [NV, 128])
        vcol = sb("vcol", [128, NV])
        rzb = sb("rzb", [128, 3])
        wq0 = sb("wq0", [128, 128])
        wk0 = sb("wk0", [128, 128])
        wv0 = sb("wv0", [128, 128])
        wvc = sb("wvc", [128, 64])
        woe = sb("woe", [128, 128])
        bvc = sb("bvc", [128, 64])
        cb1 = sb("cb1", [128, 128])
        lam_in = sb("lam_in", [128, 4, HD0])
        lam_pr = sb("lam_pr", [128, 2, HD0])
        lam_s = sb("lam_s", [128, 2])
        lam_e = sb("lam_e", [128, 2])
        nlam = sb("nlam", [128, 1])
        whh = sb("whh", [128, 384])
        wqk = sb("wqk", [128, 128])
        wvi = sb("wvi", [128, 384])
        mgate = sb("mgate", [128, NE])
        mgate_h, mgate_l = sb("mgate_h", [128, NE], F32R), sb("mgate_l", [128, NE], F32R)
        ebias = sb("ebias", [128, NE])
        wup_h, wup_l = sb("wup_h", [128, NE * HID], F32R), sb("wup_l", [128, NE * HID], F32R)
        wdn = sb("wdn", [128, NCH, 128])
        wq1_h, wq1_l = sb("wq1_h", [128, H1 * 128], F32R), sb("wq1_l", [128, H1 * 128], F32R)
        wkv1_h, wkv1_l = sb("wkv1_h", [128, 256], F32R), sb("wkv1_l", [128, 256], F32R)
        wo1 = sb("wo1", [128, H1, 128])
        ywq = sb("ywq", [128, 128])
        ywk = sb("ywk", [128, 128])
        ywv = sb("ywv", [128, 128])
        ywo = sb("ywo", [128, 128])
        ybo = sb("ybo", [128, 128])
        fgate = sb("fgate", [128, NE])
        fgb = sb("fgb", [128, NE])
        fw = sb("fw", [128, NE, 128])
        fb = sb("fb", [NE, 128])

        xin = sb("xin", [128, GB, D])
        cin = sb("cin", [MC, GB, D])
        xc = sb("xc", [128, GB, D])
        x1 = sb("x1", [128, GB, D])
        x2 = sb("x2", [128, GB, D])
        a_st = sb("a_st", [128, GB, 6])
        a_mv = sb("a_mv", [128, GB, 2])
        a_ve = sb("a_ve", [128, GB])
        a_rstd = sb("a_rstd", [128, GB])
        a_xn = sb("a_xn", [128, GB, D])
        a_xnT = sb("a_xnT", [128, GB, T])
        css = sb("css", [MC, GB])
        cve = sb("cve", [MC, GB])
        crs = sb("crs", [MC, GB])
        cnT = sb("cnT", [128, GM])
        kq = sb("kq", [128, GB, MC])
        vw = sb("vw", [MC, GB, 384])
        qT = sb("qT", [128, GB, T])
        kT = sb("kT", [128, GB, T])
        a_kbd = sb("a_kbd", [128, H0, T])
        vaug = sb("vaug", [128, GB, 4, HD0 + 1])
        a_mx = sb("a_mx", [128, H0])
        a_nm = sb("a_nm", [128, H0])
        a_p = sb("a_p", [128, H0, T])
        a_pt = sb("a_pt", [128, H0, T])
        cmask = a_p[:, 0:4, :].rearrange("p h t -> p (h t)")
        wo0, lnb, bv0, xwq = (a_p[:, i, :] for i in range(4, 8))
        xwk, xwv = a_kbd[:, 0, :], a_kbd[:, 1, :]
        wih = a_pt[:, 0:3, :].rearrange("p h t -> p (h t)")
        a_rd = sb("a_rd", [128, H0])
        a_o = a_xn

        hT = sb("hT", [128, GT])
        s_sq = sb("s_sq", [128, GB])
        s_ve = sb("s_ve", [128, GB])
        s_rs = sb("s_rs", [128, GB])
        sn = sb("sn", [128, GB, D])
        s_mx = sb("s_mx", [MC, GB])
        s_nm = sb("s_nm", [MC, GB])
        s_sum = sb("s_sum", [MC, GB])
        s_rsum = sb("s_rsum", [MC, GB])
        s_row = sb("s_row", [128, GB])
        s_rowe = sb("s_rowe", [128, GB])
        s_rrow = sb("s_rrow", [128, GB])
        s_e = sb("s_e", [MC, GB, T])
        snT = sb("snT", [128, GB, T])
        s_an = sb("s_an", [128, GB, MC])
        s_anT = s_e
        g_tr = sb("g_tr", [128, GT])
        g_tz = sb("g_tz", [128, GT])
        g_q = sb("g_q", [128, GT])
        g_d, g_n = g_tr, g_q
        s_junk = g_tz[:].rearrange("p (b t) -> p b t", b=GB)
        cn = s_e

        b_st = sb("b_st", [128, GB, 6])
        b_mv = sb("b_mv", [128, GB, 2])
        b_ve = sb("b_ve", [128, GB])
        b_rstd = sb("b_rstd", [128, GB])
        b_xn = sb("b_xn", [128, GB, D])
        b_xh = sb("b_xh", [128, GB, T], F32R)
        b_xl = sb("b_xl", [128, GB, T], F32R)
        m_t = sb("m_t", [128, GB, NE])
        m_s = sb("m_s", [128, GB, NE])
        m_b = sb("m_b", [128, GB, NE])
        m_top = sb("m_top", [128, GB, 8])
        m_ix = sb("m_ix", [128, GB, 8], U32)
        m_ixf = sb("m_ixf", [128, GB, 8])
        m_1 = sb("m_1", [128, GB, NE])
        m_2 = sb("m_2", [128, GB, NE])
        m_w = sb("m_w", [128, GB, NE])
        m_w2 = sb("m_w2", [128, GB, NE])
        b_sp = sb("b_sp", [128, 16, T])
        m_r = b_sp[:].rearrange("p (c h) t -> p c (h t)", c=4)
        b_p, b_pt = b_sp[:, 0:H1, :], b_sp[:, H1:2 * H1, :]
        m_h = sb("m_h", [128, NCH, GT])
        x3 = sb("x3", [128, GB, D])
        x4 = sb("x4", [128, GB, D])
        m_flat = m_h[:].rearrange("p c t -> p (c t)")
        wup, wq1, wkv1 = m_flat[:, 0:2048], m_flat[:, 2048:3072], m_flat[:, 3072:3328]
        sel_in = m_flat[0:MC, 3328:3328 + JX]
        SPLIT = ((wup_h, wup_l, wup), (wq1_h, wq1_l, wq1), (wkv1_h, wkv1_l, wkv1), (mgate_h, mgate_l, mgate[:]))
        q1 = m_flat[:, 0:H1 * GT].rearrange("p (h t) -> p h t", h=H1)
        vw1 = m_flat[:, H1 * GT:2 * H1 * GT].rearrange("p (b h d) -> p b h d", b=GB, h=H1)
        k1 = sb("k1", [128, GB, T])
        v1T = b_xn
        b_mx = sb("b_mx", [128, H1])
        b_nm = sb("b_nm", [128, H1])
        b_sum = sb("b_sum", [128, H1])
        b_rs = sb("b_rs", [128, H1])

        c_st = sb("c_st", [128, GB, 6])
        c_mv = sb("c_mv", [128, GB, 2])
        c_ve = sb("c_ve", [128, GB])
        c_rstd = sb("c_rstd", [128, GB])
        c_xn = sb("c_xn", [128, GB, D])
        c_xnT = sb("c_xnT", [128, GB, T])
        cT = sb("cT", [128, GB, MC])
        x4b = sb("x4b", [128, GB, D])
        x5 = x4b
        y = sb("y", [128, GB, D])
        kbd = sb("kbd", [128, GB, JX])
        vbd = sb("vbd", [128, len(JT), GB, D])
        qx = c_xnT
        x_mx = sb("x_mx", [128, HX])
        x_p = sb("x_p", [128, JX])
        x_sum = sb("x_sum", [128, HX])
        x_rs = sb("x_rs", [128, HX])
        x_pt = sb("x_pt", [128, len(JT), T])
        kx = x_p[:, 0:GM].rearrange("p (b m) -> p b m", b=GB)
        vx_h = sb("vx_h", [MC, GB, D], F32R)
        vx_l = sb("vx_l", [MC, GB, D], F32R)
        x_oT = c_xn
        f_l = sb("f_l", [128, GB, NE])
        f_mx = sb("f_mx", [128, GB])
        f_s = sb("f_s", [128, GB, NE])
        f_e = sb("f_e", [128, GB, NE])
        f_sum = sb("f_sum", [128, GB])
        f_r = sb("f_r", [128, GB])
        f_g = sb("f_g", [128, GB, NE])
        f_w0 = sb("f_w0", [128, GB, NE])
        f_ws = sb("f_ws", [128, GB])
        f_z = sb("f_z", [128, GB])
        f_wd = sb("f_wd", [128, GB])
        f_wr = sb("f_wr", [128, GB])
        f_w = sb("f_w", [128, GB, NE])
        f_wT = x_pt[0:NE, 0:4, :]

        PA = ctx.enter_context(nc.psum_tensor("PA", [128, 2, 512], F32))
        PS = ctx.enter_context(nc.psum_tensor("PS", [128, 2, 512], F32))
        PB = ctx.enter_context(nc.psum_tensor("PB", [128, 2, 512], F32))
        PC = ctx.enter_context(nc.psum_tensor("PC", [128, 2, 512], F32))

        w_loaded, late_loaded = sem("w_loaded"), sem("late_loaded")
        set_vec = sem("set_vec")
        set_pe = sem("set_pe")
        set_act = sem("set_act")
        hi_made, lo_made = sem("hi_made"), sem("lo_made")
        x_loaded, c_loaded, cT_loaded, out_done = (sem(n) for n in ("x_loaded", "c_loaded", "cT_loaded", "out_done"))
        x2_ready = sem("x2_ready")
        names_a = ("a_step css_r cve_r crs_r cn_r cnT_ps cnT_r kq_ps kq_r vw_ps vw_r xc_r var_r rstd_r xn_r "
                   "xnT_ps xnT_r qk_ps qT_r kT_r kbd_r v_ps v_r s_ps ss_r p_r pt_ps pt_r pv_ps o_r y_ps")
        A = {n: sem("a_" + n) for n in names_a.split()}
        names_s = ("s_step sq_r sve_r srs_r sn_r snT_ps snT_r sc_ps ex_r e_r at_r at_ps an_r anT_ps anT_r g_ps "
                   "tr_r tz_r hn_r pre_r n_r h_r hp_ps")
        S = {n: sem("s_" + n) for n in names_s.split()}
        names_b = ("b_step var_r rstd_r xn_r xnT_ps xnT_r xl_r mg_ps mt_r up_ps relu_r sqv_r sqp_r dn_ps x3_r "
                   "k_ps k_r v_ps v_r q_ps q_r vw_ps vw_r s_ps ss_r p_r pn_r pt_ps pt_r o_ps x4_r")
        B = {n: sem("b_" + n) for n in names_b.split()}
        names_c = ("c_step var_r rstd_r xn_r xnT_ps xnT_r x4b_r xq_ps xk_ps xv_ps xq_r xk_r xv_r kbd_r vbd_ps vbd_r "
                   "xvl_r s_ps ss_r p_r rs_r pn_r pt_ps pt_r o_ps o_r xy_ps fg_ps fs_r fe_r fw_r fwT_ps fwT_r fb_ps y0_r "
                   "ff_ps y_r")
        C = {n: sem("c_" + n) for n in names_c.split()}

        ones_row = lambda ap, n: ap.rearrange("(o d) -> o d", o=1).to_broadcast([n, ap.shape[0]])
        loads = [
            (vrow[:], a["vectors"]), (ident[:], a["c_ident"]),
            (xwk, a["L0_xattn_Wk"]), (xwq, a["L0_xattn_Wq"]), (xwv, a["L0_xattn_Wv"]), (wih, a["L0_xattn_gru_wih"]),
            (cmask, a["c_cmask"]), (hmask[:], a["c_hmask"]),
            (wq0[:], a["L0_attn_Wq"]), (wk0[:], a["L0_attn_Wk"]), (wv0[:], a["L0_attn_Wv"]), (wo0, a["L0_attn_Wo"]),
            (bv0, ones_row(a["L0_attn_bv"], 128)), (cb1[:], ones_row(a["L0_attn_bo"], 128)),
            (whh[:], a["L0_xattn_gru_whh"]),
        ] + [(lam_in[:, i, :], ones_row(a["L0_attn_lambda_" + n], 128)) for i, n in enumerate(("q1", "k1", "q2", "k2"))]
        late_loads = [
            (wup, a["L0_ffn_w_up"]), (wq1, a["L1_attn_Wq"]), (wkv1, a["L1_attn_Wkv"]), (mgate[:], a["L0_ffn_gate_w"]),
            (ebias[:], ones_row(a["L0_ffn_expert_bias"], 128)), (iota8[:], a["c_iota8"]),
            (wdn[:], a["L0_ffn_w_down"]), (wo1[:], a["L1_attn_Wo"]), (peT[:], a["c_peT"]),
            (sel_in, a["c_sel"]), (vmask[:], a["c_vmask"]), (kmask[:], a["c_kmask"]),
            (ywq[:], a["L1_xattn_Wq"]), (ywk[:], a["L1_xattn_Wk"]), (ywv[:], a["L1_xattn_Wv"]),
            (ywo[:], a["L1_xattn_Wo"]), (ybo[:], ones_row(a["L1_xattn_bo"], 128)),
            (fgate[:], a["L1_ffn_gate_w"]), (fgb[:], ones_row(a["L1_ffn_gate_b"], 128)),
            (fw[:], a["L1_ffn_expert_w"]), (fb[:], a["L1_ffn_expert_b"]),
        ]
        N_LOADS, N_LATE = 16 * len(loads), 16 * len(late_loads)

        block = ctx.enter_context(nc.Block())

        def load_weights(eng, which, loaded):
            for dst, src in which:
                eng.dma_start(dst, src).then_inc(loaded, 16)

        @block.sync
        def _(sp):
            load_weights(sp, loads[0::2], w_loaded)

            def load_x(g):
                sp.dma_start(xin[:], a["x"][:, bass.ds(g * GB, GB), :]).then_inc(x_loaded, 16)

            def load_ctx(g):
                sp.dma_start(cin[:], a["ctx_tok"][:, bass.ds(g * GB, GB), :]).then_inc(c_loaded, 16)

            def load_cT(g):
                sp.dma_start(cT[:], a["ctx_feat"][:, bass.ds(g * GB, GB), :]).then_inc(cT_loaded, 16)

            def store(g):
                sp.wait_ge(C["y_r"], 8 * g + 8)
                sp.dma_start(out[:, bass.ds(g * GB, GB), :], y[:]).then_inc(out_done, 16)

            def next_x(g):
                sp.wait_ge(A["xn_r"], 12 * g - 8)
                sp.wait_ge(A["xc_r"], g)
                load_x(g)

            def next_ctx(g):
                sp.wait_ge(A["cn_r"], g)
                load_ctx(g)

            def next_cT(g):
                sp.wait_ge(C["xv_ps"], g)
                load_cT(g)

            sp.sem_inc(out_done, 16)
            load_x(0)
            load_ctx(0)
            load_weights(sp, late_loads, late_loaded)
            load_cT(0)
            for g in range(1, 4):
                next_x(g)
                next_ctx(g)
            with sp.Fori(0, NG - 4) as g:
                next_x(g + 4)
                next_cT(g + 1)
                store(g)
                next_ctx(g + 4)
            for g in range(NG - 4, NG - 1):
                next_cT(g + 1)
                store(g)
            store(NG - 1)
            sp.wait_ge(out_done, 16 * NG + 16)

        @block.tensor
        def _(pe):
            mm, tp = nc.tensor.matmul, nc.tensor.transpose

            pe.wait_ge(w_loaded, N_LOADS)
            tp(PA[:, 0, 0:NV], vrow[:], ident[0:NV, 0:NV]).then_inc(set_pe, 1)
            mm(PA[:, 1, 0:128], xwk, xwq, start=True, stop=True).then_inc(set_pe, 1)
            mm(PS[:, 0, 0:384], xwv, wih, start=True, stop=True).then_inc(set_pe, 1)
            pe.wait_ge(set_vec, 12)
            mm(PS[:, 1, 0:128], lnb, wo0, start=True, stop=True).then_inc(set_pe, 1)
            pe.wait_ge(set_vec, 18)

            def a_norm_T(g, u):
                for b in range(GB):
                    yield
                    pe.wait_ge(A["xn_r"], 12 * g + 4 * u + b + 1)
                    last = tp(PA[:, 0, b * T:b * T + T], (sn if u == 2 else a_xn)[:, b, :], ident[:])
                last.then_inc(A["xnT_ps"], 1)
                yield
                pe.wait_ge(A["xnT_r"], 3 * g + u + 1)

            def a_qkv(g, first):
                yield
                if not first:
                    pe.wait_ge(A["vw_r"], 4 * g)
                yield from a_norm_T(g, 0)
                mm(PA[:, 1, :], wq0[:], a_xnT[:].rearrange("p b t -> p (b t)"), start=True,
                   stop=True).then_inc(A["qk_ps"], 1)
                mm(PA[:, 0, :], wk0[:], a_xnT[:].rearrange("p b t -> p (b t)"), start=True,
                   stop=True).then_inc(A["qk_ps"], 1)
                yield
                pe.wait_ge(A["qT_r"], g + 1)
                for b in range(GB):
                    last = mm(PA[:, 1, b * 64:b * 64 + 64], a_xnT[:, b, :], wvc[:], start=True, stop=True)
                last.then_inc(A["v_ps"], 1)

            def a_scores(g, b, t):
                yield
                if b == 0:
                    pe.wait_ge(A["v_r" if t else "kT_r"], g + 1)
                else:
                    pe.wait_ge(A["o_r"], 8 * g + 2 * b - 1 + t)
                pe.wait_ge(A["kbd_r"], 4 * g + b + 1)
                mm(PA[:, t, :], qT[:, b, :], a_kbd[:, 4 * t:4 * t + 4, :].rearrange("p h t -> p (h t)"),
                   start=True, stop=True).then_inc(A["s_ps"], 1)

            def a_pv(g, b, t):
                yield
                pe.wait_ge(A["p_r"], 8 * g + 2 * b + t + 1)
                for h in range(4 * t, 4 * t + 4):
                    last = tp(PA[:, t, (h % 4) * T:(h % 4) * T + T], a_p[:, h, :], ident[:])
                last.then_inc(A["pt_ps"], 1)
                yield
                pe.wait_ge(A["pt_r"], 8 * g + 2 * b + t + 1)
                for h in range(4 * t, 4 * t + 4):
                    last = mm(PA[:, t, (h % 4) * 17:(h % 4) * 17 + 17], a_pt[:, h, :], vaug[:, b, h % 4, :],
                              start=True, stop=True)
                last.then_inc(A["pv_ps"], 1)

            def a_proj(g):
                yield from a_norm_T(g, 1)
                for b in range(GB):
                    last = mm(PA[:, 1, b * T:b * T + T], a_xnT[:, b, :], woe[:], start=True, stop=True)
                last.then_inc(A["y_ps"], 1)
                yield from a_norm_T(g, 2)

            def a_ctx(g):
                yield
                pe.wait_ge(A["cn_r"], g + 1)
                for b in range(GB):
                    last = tp(PA[:, 1, b * MC:b * MC + MC], cn[:, b, :], ident[0:MC, 0:MC])
                last.then_inc(A["cnT_ps"], 1)
                yield
                pe.wait_ge(A["cnT_r"], g + 1)
                mm(PA[:, 0, 0:GM], wqk[:], cnT[:], start=True, stop=True).then_inc(A["kq_ps"], 1)
                for b in range(GB):
                    yield
                    if b == 1:
                        pe.wait_ge(A["kq_r"], g + 1)
                    if b >= 2:
                        pe.wait_ge(A["vw_r"], 4 * g + b - 1)
                    mm(PA[0:MC, 1 - b % 2, 0:384], cnT[:, b * MC:b * MC + MC], wvi[:], start=True,
                       stop=True).then_inc(A["vw_ps"], 1)

            def thread_a(g, first=False):
                yield from a_qkv(g, first)
                yield from a_scores(g, 0, 0)
                for b in range(GB):
                    yield from a_scores(g, b, 1)
                    yield from a_pv(g, b, 0)
                    if b + 1 < GB:
                        yield from a_scores(g, b + 1, 0)
                    yield from a_pv(g, b, 1)
                yield from a_proj(g)
                yield from a_ctx(g)

            def s_round(g, t):
                u = 3 * g + t
                yield
                pe.wait_ge(S["sn_r"], u + 1)
                for b in range(GB):
                    last = tp(PS[:, 1, b * T:b * T + T], sn[:, b, :], ident[:])
                last.then_inc(S["snT_ps"], 1)
                yield
                if t == 0:
                    pe.wait_ge(A["kq_r"], g + 1)
                pe.wait_ge(S["snT_r"], u + 1)
                for b in range(GB):
                    last = mm(PS[0:MC, 0, b * T:b * T + T], kq[:, b, :], snT[:, b, :], start=True, stop=True)
                last.then_inc(S["sc_ps"], 1)
                yield
                pe.wait_ge(S["at_r"], u + 1)
                for b in range(GB):
                    last = tp(PS[:, 1, b * MC:b * MC + MC], s_e[:, b, :], ident[0:MC, 0:MC])
                last.then_inc(S["at_ps"], 1)
                yield
                pe.wait_ge(S["an_r"], u + 1)
                for b in range(GB):
                    last = tp(PS[0:MC, 0, b * T:b * T + T], s_an[:, b, :], ident[:])
                last.then_inc(S["anT_ps"], 1)
                if t == 0:
                    pe.wait_ge(A["xnT_r"], 3 * g + 3)
                mm(PS[:, 1, :], whh[:, 256:384], hT[:], start=True, stop=True).then_inc(S["g_ps"], 1)
                yield
                pe.wait_ge(S["anT_r"], u + 1)
                if t == 0:
                    pe.wait_ge(A["vw_r"], 4 * g + 4)
                for k, bank, free in ((0, 0, None), (1, 1, "hn_r"), (2, 0, "tr_r")):
                    if free:
                        yield
                        pe.wait_ge(S[free], u + 1)
                    if k < 2:
                        mm(PS[:, bank, :], whh[:, 128 * k:128 * k + 128], hT[:], start=True, stop=False,
                           skip_group_check=True)
                    for b in range(GB):
                        last = mm(PS[:, bank, b * T:b * T + T], vw[:, b, 128 * k:128 * k + 128], s_anT[:, b, :],
                                  start=(k == 2), stop=True, skip_group_check=True)
                    last.then_inc(S["g_ps"], 1)
                yield
                pe.wait_ge(S["h_r"], u + 1)
                for b in range(GB):
                    last = tp(PS[:, 0, b * T:b * T + T], hT[:, b * T:b * T + T], ident[:])
                last.then_inc(S["hp_ps"], 1)

            def thread_s(g):
                for t in range(3):
                    yield from s_round(g, t)

            def b_norm_T(g, u):
                for b in range(GB):
                    yield
                    pe.wait_ge(B["xn_r"], 8 * g + 4 * u + b + 1)
                    last = tp(PB[:, 0, b * T:b * T + T], b_xn[:, b, :], ident[:])
                last.then_inc(B["xnT_ps"], 1)
                yield
                pe.wait_ge(B["xl_r"], 2 * g + u + 1)

            def mm3(dst, lhs, rhs):
                (lh, ll), (rh, rl) = lhs, rhs
                mm(dst, lh, rh, start=True, stop=False)
                mm(dst, ll, rh, start=False, stop=False)
                return mm(dst, lh, rl, start=False, stop=True)

            b_x = [x[:].rearrange("p b t -> p (b t)") for x in (b_xh, b_xl)]

            def b_moe_up(g):
                yield from b_norm_T(g, 0)
                for b in range(GB):
                    last = mm3(PB[:, 1, b * NE:b * NE + NE], (b_xh[:, b, :], b_xl[:, b, :]), (mgate_h[:], mgate_l[:]))
                last.then_inc(B["mg_ps"], 1)
                for c in range(NCH):
                    yield
                    if c == 1:
                        pe.wait_ge(B["mt_r"], g + 1)
                    if c >= 2:
                        pe.wait_ge(B["relu_r"], NCH * g + c - 1)
                    cs = slice(128 * c, 128 * c + 128)
                    mm3(PB[:, c % 2, :], (wup_h[:, cs], wup_l[:, cs]), b_x).then_inc(B["up_ps"], 1)

            def b_moe_down(g, b):
                for f in range(2):
                    yield
                    if b == 0:
                        pe.wait_ge(B["sqv_r"], 8 * g + 4 + 4 * f)
                        pe.wait_ge(B["sqp_r"], 8 * g + 4 + 4 * f)
                        pe.wait_ge(B["relu_r"], NCH * g + NCH - 1 + f)
                    else:
                        pe.wait_ge(B["x3_r"], 8 * g + 2 * b - 1 + f)
                    for e in range(4 * f, 4 * f + 4):
                        for k in range(2):
                            last = mm(PB[:, f, (e % 4) * 128:(e % 4) * 128 + 128],
                                      m_h[:, 2 * e + k, b * T:b * T + T], wdn[:, 2 * e + k, :],
                                      start=(k == 0), stop=(k == 1))
                    last.then_inc(B["dn_ps"], 1)

            def b_qkv(g):
                yield from b_norm_T(g, 1)
                mm3(PB[:, 0, :], (wkv1_h[:, 0:128], wkv1_l[:, 0:128]), b_x).then_inc(B["k_ps"], 1)
                mm3(PB[:, 1, :], (wkv1_h[:, 128:256], wkv1_l[:, 128:256]), b_x).then_inc(B["v_ps"], 1)
                for h in range(H1):
                    yield
                    if h == 0:
                        pe.wait_ge(B["k_r"], g + 1)
                    elif h == 1:
                        pe.wait_ge(B["v_r"], g + 1)
                    else:
                        pe.wait_ge(B["q_r"], 8 * g + h - 1)
                    hs = slice(128 * h, 128 * h + 128)
                    mm3(PB[:, h % 2, :], (wq1_h[:, hs], wq1_l[:, hs]), b_x).then_inc(B["q_ps"], 1)
                for b in range(GB):
                    for f in range(2):
                        yield
                        if b == 0:
                            pe.wait_ge(B["q_r"], 8 * g + 7 + f)
                        else:
                            pe.wait_ge(B["vw_r"], 8 * g + 2 * b - 1 + f)
                        mm(PB[:, f, :], v1T[:, b, :], wo1[:, 4 * f:4 * f + 4, :].rearrange("p h d -> p (h d)"),
                           start=True, stop=True).then_inc(B["vw_ps"], 1)

            def b_scores(g, b, f):
                yield
                if b == 0:
                    pe.wait_ge(B["vw_r"], 8 * g + 7 + f)
                else:
                    pe.wait_ge(B["x4_r"], 8 * g + 2 * b - 1 + f)
                mm(PB[:, f, :], ident16[:], cmask16[:], start=True, stop=False, skip_group_check=True)
                for h in range(4 * f, 4 * f + 4):
                    last = mm(PB[:, f, (h % 4) * T:(h % 4) * T + T], q1[:, h, b * T:b * T + T], k1[:, b, :],
                              start=False, stop=True, skip_group_check=True)
                last.then_inc(B["s_ps"], 1)

            def b_pT(g, b, f):
                yield
                pe.wait_ge(B["pn_r"], 8 * g + 2 * b + f + 1)
                for h in range(4 * f, 4 * f + 4):
                    last = tp(PB[:, f, (h % 4) * T:(h % 4) * T + T], b_p[:, h, :], ident[:])
                last.then_inc(B["pt_ps"], 1)

            def b_out(g, b, f):
                yield
                pe.wait_ge(B["pt_r"], 8 * g + 2 * b + f + 1)
                for h in range(4 * f, 4 * f + 4):
                    last = mm(PB[:, f, 0:D], b_pt[:, h, :], vw1[:, b, h, :], start=(h % 4 == 0), stop=(h % 4 == 3))
                last.then_inc(B["o_ps"], 1)

            def thread_b(g):
                yield from b_moe_up(g)
                for b in range(GB):
                    yield from b_moe_down(g, b)
                yield from b_qkv(g)
                yield from b_scores(g, 0, 0)
                for b in range(GB):
                    yield from b_scores(g, b, 1)
                    yield from b_pT(g, b, 0)
                    yield from b_out(g, b, 0)
                    if b + 1 < GB:
                        yield from b_scores(g, b + 1, 0)
                    yield from b_pT(g, b, 1)
                    yield from b_out(g, b, 1)

            def c_norm_T(g, u):
                for b in range(GB):
                    yield
                    pe.wait_ge(C["xn_r"], 8 * g + 4 * u + b + 1)
                    last = tp(PC[:, 0, b * T:b * T + T], c_xn[:, b, :], ident[:])
                last.then_inc(C["xnT_ps"], 1)
                yield
                pe.wait_ge(C["xnT_r"], 2 * g + u + 1)

            def c_qkv(g):
                yield from c_norm_T(g, 0)
                mm(PC[:, 1, :], ywq[:], c_xnT[:].rearrange("p b t -> p (b t)"), start=True,
                   stop=True).then_inc(C["xq_ps"], 1)
                yield
                pe.wait_ge(cT_loaded, 16 * g + 16)
                mm(PC[:, 0, 0:GM], ywk[:], cT[:].rearrange("p b m -> p (b m)"), start=True,
                   stop=True).then_inc(C["xk_ps"], 1)
                yield
                pe.wait_ge(C["xq_r"], g + 1)
                for b in range(GB):
                    last = mm(PC[0:MC, 1, b * D:b * D + D], cT[:, b, :], ywv[:], start=True, stop=True)
                last.then_inc(C["xv_ps"], 1)
                for i, (j, w) in enumerate(JT):
                    yield
                    if i == 0:
                        pe.wait_ge(C["xk_r"], g + 1)
                        pe.wait_ge(C["xvl_r"], g + 1)
                    elif i >= 2:
                        pe.wait_ge(C["vbd_r"], 5 * g + i - 1)
                    mm(PC[0:w, i % 2, :], sel[:, j:j + w], vx_h[:].rearrange("p b d -> p (b d)"), start=True, stop=False)
                    mm(PC[0:w, i % 2, :], sel[:, j:j + w], vx_l[:].rearrange("p b d -> p (b d)"), start=False,
                       stop=True).then_inc(C["vbd_ps"], 1)

            def c_scores(g, b):
                yield
                if b == 0:
                    pe.wait_ge(C["kbd_r"], g + 1)
                    pe.wait_ge(C["vbd_r"], 5 * g + 5)
                else:
                    pe.wait_ge(C["o_r"], 4 * g + b)
                mm(PC[:, 0, 0:OFF[1]], qx[:, b, :], kbd[:, b, 0:OFF[1]], start=True, stop=True)
                mm(PC[:, 1, 0:JX - OFF[1]], qx[:, b, :], kbd[:, b, OFF[1]:JX], start=True,
                   stop=True).then_inc(C["s_ps"], 1)

            def c_pv(g, b):
                yield
                pe.wait_ge(C["pn_r"], 4 * g + b + 1)
                for i, (j, w) in enumerate(JT):
                    dst = PC[0:w, 0, i * T:i * T + T] if i < 4 else PC[0:w, 1, 0:T]
                    last = tp(dst, x_p[:, j:j + w], ident[:])
                last.then_inc(C["pt_ps"], 1)
                yield
                pe.wait_ge(C["pt_r"], 4 * g + b + 1)
                for i, (j, w) in enumerate(JT):
                    last = mm(PC[:, 1, T:2 * T], vbd[0:w, i, b, :], x_pt[0:w, i, :], start=(i == 0),
                              stop=(i == len(JT) - 1))
                last.then_inc(C["o_ps"], 1)

            def c_out(g):
                yield
                pe.wait_ge(C["o_r"], 4 * g + 4)
                for b in range(GB):
                    last = mm(PC[:, 0, b * T:b * T + T], x_oT[:, b, :], ywo[:], start=True, stop=True)
                last.then_inc(C["xy_ps"], 1)

            def c_ffn(g):
                yield from c_norm_T(g, 1)
                for b in range(GB):
                    last = mm(PC[:, 1, b * NE:b * NE + NE], c_xnT[:, b, :], fgate[:], start=True, stop=True)
                last.then_inc(C["fg_ps"], 1)
                yield
                pe.wait_ge(C["fw_r"], g + 1)
                for b in range(GB):
                    last = tp(PC[0:NE, 1, b * T:b * T + T], f_w[:, b, :], ident[:])
                last.then_inc(C["fwT_ps"], 1)
                yield
                pe.wait_ge(C["fwT_r"], g + 1)
                for b in range(GB):
                    last = mm(PC[:, 0, b * T:b * T + T], f_wT[:, b, :], fb[:], start=True, stop=True)
                last.then_inc(C["fb_ps"], 1)
                for i, (b, f) in enumerate((b, f) for b in range(GB) for f in (1, 0)):
                    yield
                    if i == 1:
                        pe.wait_ge(C["y0_r"], g + 1)
                    if i >= 2:
                        pe.wait_ge(C["y_r"], 8 * g + i - 1)
                    mm(PC[:, f, :], c_xnT[:, b, :], fw[:, 4 * f:4 * f + 4, :].rearrange("p e d -> p (e d)"),
                       start=True, stop=True).then_inc(C["ff_ps"], 1)

            def thread_c(g):
                yield from c_qkv(g)
                for b in range(GB):
                    yield from c_scores(g, b)
                    yield from c_pv(g, b)
                yield from c_out(g)
                yield from c_ffn(g)

            weave(ORDER["pe"], a=thread_a(0, first=True))
            weave(ORDER["pe"], a=thread_a(1), s=thread_s(0))
            pe.wait_ge(late_loaded, N_LATE)
            pe.wait_ge(lo_made, len(SPLIT))
            pe.wait_ge(hi_made, len(SPLIT) + 1)
            weave(ORDER["pe"], a=thread_a(2), s=thread_s(1), b=thread_b(0))
            with pe.Fori(0, NG - 3) as g:
                weave(ORDER["pe"], a=thread_a(g + 3), s=thread_s(g + 2), b=thread_b(g + 1), c=thread_c(g))
            weave(ORDER["pe"], s=thread_s(NG - 1), b=thread_b(NG - 2), c=thread_c(NG - 3))
            weave(ORDER["pe"], b=thread_b(NG - 1), c=thread_c(NG - 2))
            weave(ORDER["pe"], c=thread_c(NG - 1))

        @block.scalar
        def _(act):
            f = nc.scalar.activation

            load_weights(act, loads[1::2], w_loaded)
            act.wait_ge(set_vec, 1)
            f(warm[:], mhalf[:, 0:1], ACT.Exp)
            act.wait_ge(set_vec, 3)
            f(lam_e[:], lam_s[:], ACT.Exp).then_inc(set_act, 1)
            act.wait_ge(set_vec, 18)

            def a_xnT_out(g, u, dst):
                yield
                act.wait_ge(A["xnT_ps"], 3 * g + u + 1)
                f(dst, PA[:, 0, :], ACT.Copy).then_inc(A["xnT_r"], 1)

            def a_q(g):
                yield from a_xnT_out(g, 0, a_xnT[:].rearrange("p b t -> p (b t)"))
                yield
                act.wait_ge(A["qk_ps"], 2 * g + 1)
                f(qT[:].rearrange("p b t -> p (b t)"), PA[:, 1, :], ACT.Identity,
                  bias=vcol[:, V_BQ:V_BQ + 1]).then_inc(A["qT_r"], 1)

            def a_exp(g, b, t):
                yield
                act.wait_ge(A["ss_r"], 8 * g + 2 * b + t + 1)
                for h in range(4 * t, 4 * t + 4):
                    last = f(a_p[:, h, :], PA[:, t, (h % 4) * T:(h % 4) * T + T], ACT.Exp,
                             scale=HD0 ** -0.5, bias=a_nm[:, h:h + 1])
                last.then_inc(A["p_r"], 1)

            def a_pt_out(g, b, t):
                yield
                act.wait_ge(A["pt_ps"], 8 * g + 2 * b + t + 1)
                f(a_pt[:, 4 * t:4 * t + 4, :].rearrange("p h t -> p (h t)"), PA[:, t, :],
                  ACT.Copy).then_inc(A["pt_r"], 1)

            def a_ctx(g, first):
                yield
                if not first:
                    act.wait_ge(x2_ready, g)
                act.wait_ge(c_loaded, 16 * g + 16)
                for b in range(GB):
                    last = f(cn[:, b, :], cin[:, b, :], ACT.Square, accum_out=css[:, b:b + 1])
                last.then_inc(A["css_r"], 1)
                yield from a_xnT_out(g, 2, hT[:])
                yield
                act.wait_ge(A["cnT_ps"], g + 1)
                f(cnT[:], PA[:, 1, 0:GM], ACT.Copy).then_inc(A["cnT_r"], 1)
                for b in range(GB):
                    yield
                    act.wait_ge(A["vw_ps"], 4 * g + b + 1)
                    f(vw[:, b, :], PA[0:MC, 1 - b % 2, 0:384], ACT.Copy).then_inc(A["vw_r"], 1)

            def thread_a(g, first=False):
                yield from a_q(g)
                yield from a_exp(g, 0, 0)
                for b in range(GB):
                    yield from a_exp(g, b, 1)
                    yield from a_pt_out(g, b, 0)
                    if b + 1 < GB:
                        yield from a_exp(g, b + 1, 0)
                    yield from a_pt_out(g, b, 1)
                yield from a_xnT_out(g, 1, a_xnT[:].rearrange("p b t -> p (b t)"))
                yield from a_ctx(g, first)

            def s_round(g, t):
                u = 3 * g + t
                yield
                if t == 0:
                    act.wait_ge(A["xn_r"], 12 * g + 12)
                else:
                    act.wait_ge(S["hp_ps"], u)
                for b in range(GB):
                    src = sn[:, b, :] if t == 0 else PS[:, 0, b * T:b * T + T]
                    last = f(s_junk[:, b, :], src, ACT.Square, accum_out=s_sq[:, b:b + 1])
                last.then_inc(S["sq_r"], 1)
                yield
                act.wait_ge(S["srs_r"], u + 1)
                if t == 0:
                    act.wait_ge(A["xnT_ps"], 3 * g + 3)
                for b in range(GB):
                    src = sn[:, b, :] if t == 0 else PS[:, 0, b * T:b * T + T]
                    last = f(sn[:, b, :], src, ACT.Identity, scale=s_rs[:, b:b + 1])
                last.then_inc(S["sn_r"], 1)
                yield
                act.wait_ge(S["snT_ps"], u + 1)
                f(snT[:].rearrange("p b t -> p (b t)"), PS[:, 1, :], ACT.Copy).then_inc(S["snT_r"], 1)
                yield
                act.wait_ge(S["ex_r"], u + 1)
                for b in range(GB):
                    last = f(s_e[:, b, :], PS[0:MC, 0, b * T:b * T + T], ACT.Exp, scale=D ** -0.5,
                             bias=s_nm[:, b:b + 1], accum_out=s_sum[:, b:b + 1])
                last.then_inc(S["e_r"], 1)
                yield
                act.wait_ge(S["anT_ps"], u + 1)
                f(s_anT[:].rearrange("p b t -> p (b t)"), PS[0:MC, 0, :], ACT.Copy).then_inc(S["anT_r"], 1)
                yield
                act.wait_ge(S["g_ps"], 4 * u + 1)
                f(g_q[:], PS[:, 1, :], ACT.Identity, scale=0.5, bias=rzb[:, 2:3]).then_inc(S["hn_r"], 1)
                yield
                act.wait_ge(S["g_ps"], 4 * u + 2)
                f(g_tr[:], PS[:, 0, :], ACT.Tanh, scale=0.5, bias=rzb[:, 0:1]).then_inc(S["tr_r"], 1)
                yield
                act.wait_ge(S["g_ps"], 4 * u + 3)
                f(g_tz[:], PS[:, 1, :], ACT.Tanh, scale=0.5, bias=rzb[:, 1:2]).then_inc(S["tz_r"], 1)
                yield
                act.wait_ge(S["pre_r"], u + 1)
                f(g_n[:], g_q[:], ACT.Tanh, bias=vcol[:, V_BIH + 2:V_BIH + 3]).then_inc(S["n_r"], 1)

            def thread_s(g):
                for t in range(3):
                    yield from s_round(g, t)

            def b_xnT_out(g, u):
                yield
                act.wait_ge(B["xnT_ps"], 2 * g + u + 1)
                f(b_xh[:].rearrange("p b t -> p (b t)"), PB[:, 0, :], ACT.Copy).then_inc(B["xnT_r"], 1)

            def b_moe(g):
                yield from b_xnT_out(g, 0)
                yield
                act.wait_ge(B["mg_ps"], g + 1)
                f(m_t[:].rearrange("p b e -> p (b e)"), PB[:, 1, 0:GB * NE], ACT.Tanh,
                  scale=0.5).then_inc(B["mt_r"], 1)
                for c in range(NCH):
                    yield
                    act.wait_ge(B["up_ps"], NCH * g + c + 1)
                    if c >= 4:
                        act.wait_ge(B["sqp_r" if c % 2 else "sqv_r"], 8 * g + c // 2 - 1)
                    f(m_r[:, c % 4, :], PB[:, c % 2, :], ACT.Relu).then_inc(B["relu_r"], 1)

            def b_v(g):
                yield from b_xnT_out(g, 1)
                yield
                act.wait_ge(B["v_ps"], g + 1)
                f(v1T[:].rearrange("p b t -> p (b t)"), PB[:, 1, :], ACT.Identity,
                  bias=vcol[:, V_BV1:V_BV1 + 1]).then_inc(B["v_r"], 1)
                for b in range(GB):
                    for h in range(2):
                        yield
                        act.wait_ge(B["vw_ps"], 8 * g + 2 * b + h + 1)
                        f(vw1[:, b, 4 * h:4 * h + 4, :].rearrange("p h d -> p (h d)"), PB[:, h, :],
                          ACT.Copy).then_inc(B["vw_r"], 1)

            def b_exp(g, b, h):
                yield
                act.wait_ge(B["ss_r"], 8 * g + 2 * b + h + 1)
                for i in range(4):
                    j = 4 * h + i
                    last = f(b_p[:, j, :], PB[:, h, i * T:i * T + T], ACT.Exp, scale=D ** -0.5, bias=b_nm[:, j:j + 1],
                             accum_out=b_sum[:, j:j + 1])
                last.then_inc(B["p_r"], 1)

            def b_pt_out(g, b, h):
                yield
                act.wait_ge(B["pt_ps"], 8 * g + 2 * b + h + 1)
                f(b_pt[:, 4 * h:4 * h + 4, :].rearrange("p h t -> p (h t)"), PB[:, h, :],
                  ACT.Copy).then_inc(B["pt_r"], 1)

            def thread_b(g):
                yield from b_moe(g)
                yield from b_v(g)
                yield from b_exp(g, 0, 0)
                for b in range(GB):
                    yield from b_exp(g, b, 1)
                    yield from b_pt_out(g, b, 0)
                    if b + 1 < GB:
                        yield from b_exp(g, b + 1, 0)
                    yield from b_pt_out(g, b, 1)

            def c_xnT_out(g, u):
                yield
                act.wait_ge(C["xnT_ps"], 2 * g + u + 1)
                f(c_xnT[:].rearrange("p b t -> p (b t)"), PC[:, 0, :], ACT.Copy).then_inc(C["xnT_r"], 1)

            def c_qkv(g):
                yield from c_xnT_out(g, 0)
                yield
                act.wait_ge(C["xq_ps"], g + 1)
                f(qx[:].rearrange("p b t -> p (b t)"), PC[:, 1, :], ACT.Identity,
                  bias=vcol[:, V_XBQ:V_XBQ + 1]).then_inc(C["xq_r"], 1)
                yield
                act.wait_ge(C["xk_ps"], g + 1)
                f(kx.rearrange("p b m -> p (b m)"), PC[:, 0, 0:GM], ACT.Identity,
                  bias=vcol[:, V_XBK:V_XBK + 1]).then_inc(C["xk_r"], 1)
                yield
                act.wait_ge(C["xv_ps"], g + 1)
                f(vx_h[:].rearrange("p b d -> p (b d)"), PC[0:MC, 1, :], ACT.Copy).then_inc(C["xv_r"], 1)

            def c_sample(g, b):
                yield
                act.wait_ge(C["ss_r"], 4 * g + b + 1)
                f(x_p[:], x_p[:], ACT.Exp, scale=HDX ** -0.5).then_inc(C["p_r"], 1)
                yield
                act.wait_ge(C["pt_ps"], 4 * g + b + 1)
                f(x_pt[:, 0:4, :].rearrange("p j t -> p (j t)"), PC[:, 0, :], ACT.Copy)
                f(x_pt[0:JT[4][1], 4, :], PC[0:JT[4][1], 1, 0:T], ACT.Copy).then_inc(C["pt_r"], 1)
                yield
                act.wait_ge(C["o_ps"], 4 * g + b + 1)
                f(x_oT[:, b, :], PC[:, 1, T:2 * T], ACT.Identity,
                  bias=vcol[:, V_XBV:V_XBV + 1]).then_inc(C["o_r"], 1)

            def c_ffn(g):
                yield from c_xnT_out(g, 1)
                yield
                act.wait_ge(C["fs_r"], g + 1)
                f(f_e[:], f_s[:], ACT.Exp).then_inc(C["fe_r"], 1)
                yield
                act.wait_ge(C["fwT_ps"], g + 1)
                f(f_wT.rearrange("p b t -> p (b t)"), PC[0:NE, 1, :], ACT.Copy).then_inc(C["fwT_r"], 1)

            def thread_c(g):
                yield from c_qkv(g)
                for b in range(GB):
                    yield from c_sample(g, b)
                yield from c_ffn(g)

            weave(ORDER["act"], a=thread_a(0, first=True))
            act.wait_ge(late_loaded, N_LATE)
            for hi, _, w in SPLIT:
                f(hi[:], w, ACT.Copy).then_inc(hi_made, 1)
            f(sel[:], sel_in, ACT.Copy).then_inc(hi_made, 1)
            weave(ORDER["act"], a=thread_a(1), s=thread_s(0))
            weave(ORDER["act"], a=thread_a(2), s=thread_s(1), b=thread_b(0))
            with act.Fori(0, NG - 3) as g:
                weave(ORDER["act"], a=thread_a(g + 3), s=thread_s(g + 2), b=thread_b(g + 1), c=thread_c(g))
            weave(ORDER["act"], s=thread_s(NG - 1), b=thread_b(NG - 2), c=thread_c(NG - 3))
            weave(ORDER["act"], b=thread_b(NG - 1), c=thread_c(NG - 2))
            weave(ORDER["act"], c=thread_c(NG - 1))

        @block.gpsimd
        def _(pool):
            tt = nc.gpsimd.tensor_tensor
            pool.wait_ge(set_vec, 18)

            def a_rstd_(g, u):
                yield
                pool.wait_ge(A["var_r"], 3 * g + u + 1)
                tt(a_rstd[:], a_ve[:], mhalf[:], ALU.pow).then_inc(A["rstd_r"], 1)

            def a_keys(g, b):
                yield
                if b == 0:
                    pool.wait_ge(A["kT_r"], g + 1)
                else:
                    pool.wait_ge(A["s_ps"], 8 * g + 2 * b)
                tt(a_kbd[:], kT[:, b, :].unsqueeze(1).to_broadcast([128, H0, T]),
                   hmask[:].unsqueeze(2).to_broadcast([128, H0, T]), ALU.mult).then_inc(A["kbd_r"], 1)

            def thread_a(g):
                yield from a_rstd_(g, 0)
                tt(xc[:], xin[:], cb1[:].unsqueeze(1).to_broadcast([128, GB, D]), ALU.add).then_inc(A["xc_r"], 1)
                for b in range(GB):
                    yield from a_keys(g, b)
                yield from a_rstd_(g, 1)
                yield from a_rstd_(g, 2)
                yield
                pool.wait_ge(A["cve_r"], g + 1)
                tt(crs[:], cve[:], mhalf[0:MC, :], ALU.pow).then_inc(A["crs_r"], 1)

            def thread_s(g):
                for t in range(3):
                    yield
                    pool.wait_ge(S["sve_r"], 3 * g + t + 1)
                    tt(s_rs[:], s_ve[:], mhalf[:], ALU.pow).then_inc(S["srs_r"], 1)

            def b_rstd_(g, u):
                yield
                pool.wait_ge(B["var_r"], 2 * g + u + 1)
                tt(b_rstd[:], b_ve[:], mhalf[:], ALU.pow).then_inc(B["rstd_r"], 1)

            def b_squares(g):
                for c in range(1, NCH, 2):
                    yield
                    pool.wait_ge(B["relu_r"], NCH * g + c + 1)
                    tt(m_h[:, c, :], m_r[:, c % 4, :], m_r[:, c % 4, :], ALU.mult).then_inc(B["sqp_r"], 1)

            def thread_b(g):
                yield from b_rstd_(g, 0)
                yield from b_squares(g)
                yield from b_rstd_(g, 1)

            def c_rstd_(g, u):
                yield
                pool.wait_ge(C["var_r"], 2 * g + u + 1)
                tt(c_rstd[:], c_ve[:], mhalf[:], ALU.pow).then_inc(C["rstd_r"], 1)

            def c_probs(g, b):
                yield
                pool.wait_ge(C["rs_r"], 4 * g + b + 1)
                for c in range(NCLS):
                    v = x_p[:, OFF[c]:OFF[c + 1]].rearrange("p (h k) -> p h k", h=4)
                    last = tt(v, v, x_rs[:, 4 * c:4 * c + 4].unsqueeze(2).to_broadcast([128, 4, NK[c]]), ALU.mult)
                last.then_inc(C["pn_r"], 1)

            def thread_c(g):
                yield from c_rstd_(g, 0)
                tt(x4b[:], x4[:], ybo[:].unsqueeze(1).to_broadcast([128, GB, D]), ALU.add).then_inc(C["x4b_r"], 1)
                for b in range(GB):
                    yield from c_probs(g, b)
                yield from c_rstd_(g, 1)

            weave(ORDER["pool"], a=thread_a(0))
            pool.wait_ge(late_loaded, N_LATE)
            weave(ORDER["pool"], a=thread_a(1), s=thread_s(0))
            weave(ORDER["pool"], a=thread_a(2), s=thread_s(1), b=thread_b(0))
            with pool.Fori(0, NG - 3) as g:
                weave(ORDER["pool"], a=thread_a(g + 3), s=thread_s(g + 2), b=thread_b(g + 1), c=thread_c(g))
            weave(ORDER["pool"], s=thread_s(NG - 1), b=thread_b(NG - 2), c=thread_c(NG - 3))
            weave(ORDER["pool"], b=thread_b(NG - 1), c=thread_c(NG - 2))
            weave(ORDER["pool"], c=thread_c(NG - 1))


        @block.vector
        def _(dve):
            v = nc.vector
            bc = lambda ap, n: ap.unsqueeze(2).to_broadcast([*ap.shape, n])

            class Steps:

                def __init__(self, s, per_group):
                    self.s, self.per_group = s, per_group

                def begin(self, g):
                    self.base, self.n = g * self.per_group, 0

                def then(self, ins):
                    ins.then_inc(self.s, 1)
                    self.n += 1
                    value = self.base + self.n
                    yield
                    dve.wait_ge(self.s, value)

            steps_a, steps_s, steps_b, steps_c = (
                Steps(of[n + "_step"], p) for of, n, p in zip((A, S, B, C), "asbc", STEPS))

            count = [0]

            def setup(ins):
                ins.then_inc(set_vec, 1)
                count[0] += 1
                dve.wait_ge(set_vec, count[0])

            v.memset(vaug[:], 1.0)
            setup(v.memset(mhalf[:], -0.5))
            dve.wait_ge(w_loaded, N_LOADS)
            setup(v.tensor_tensor(lam_pr[:], lam_in[:, 0::2, :], lam_in[:, 1::2, :], ALU.mult))
            setup(v.tensor_reduce(lam_s[:], lam_pr[:], AX.X, ALU.add))
            setup(v.tensor_copy(ident16[:], ident[:]))
            setup(v.tensor_copy(cmask16[:], cmask))
            dve.wait_ge(set_act, 1)
            setup(v.tensor_tensor(nlam[:], lam_e[:, 1:2], lam_e[:, 0:1], ALU.subtract))
            setup(v.tensor_scalar(nlam[:], nlam[:], LAMBDA_INIT, None, ALU.subtract))
            dve.wait_ge(set_pe, 1)
            setup(v.tensor_copy(vcol[:], PA[:, 0, 0:NV]))
            setup(v.scalar_tensor_tensor(wvc[:], wv0[:, 64:128], nlam[:, 0:1], wv0[:, 0:64], ALU.mult, ALU.add))
            setup(v.scalar_tensor_tensor(bvc[:], bv0[:, 64:128], nlam[:, 0:1], bv0[:, 0:64], ALU.mult, ALU.add))
            setup(v.tensor_scalar(woe[:], wo0, vcol[:, V_LNW:V_LNW + 1], 1.0 - LAMBDA_INIT, ALU.mult, ALU.mult))
            setup(v.tensor_scalar(lnb, vcol[:, V_LNB:V_LNB + 1].to_broadcast([128, 128]), 1.0 - LAMBDA_INIT, None,
                                  ALU.mult))
            dve.wait_ge(set_pe, 2)
            setup(v.tensor_scalar(wqk[:], PA[:, 1, 0:128], vcol[:, V_WIN:V_WIN + 1], None, ALU.mult))
            dve.wait_ge(set_pe, 3)
            setup(v.tensor_scalar(wvi[:], PS[:, 0, 0:384], vcol[:, V_WIN:V_WIN + 1], None, ALU.mult))
            dve.wait_ge(set_pe, 4)
            setup(v.tensor_tensor(cb1[:], PS[:, 1, 0:128], cb1[:], ALU.add))
            setup(v.tensor_copy(rzb[:, 2:3], vcol[:, V_BHH + 2:V_BHH + 3]))
            setup(v.tensor_tensor(rzb[:, 0:2], vcol[:, V_BIH:V_BIH + 2], vcol[:, V_BHH:V_BHH + 2], ALU.add))
            setup(v.tensor_scalar(rzb[:], rzb[:], 0.5, None, ALU.mult))

            def hold(st):
                i = (steps_a, steps_b, steps_c).index(st)
                v.memset(held[:, i:i + 1], 0.0)

            def norm(st, S, src, dst, stt, mv, ve, rstd, uses, u, g):
                for b in range(GB):
                    last = v.bn_stats(stt[:, b, :], src[:, b, :])
                yield from st.then(last)
                hold(st)
                for b in range(GB):
                    last = v.bn_aggr(mv[:, b, :], stt[:, b, :])
                yield from st.then(last)
                v.tensor_scalar(ve[:], mv[:, :, 1], LN_EPS, None, ALU.add).then_inc(S["var_r"], 1)
                yield
                dve.wait_ge(S["rstd_r"], uses * g + u + 1)
                for b in range(GB):
                    v.tensor_scalar(dst[:, b, :], src[:, b, :], mv[:, b, 0:1], rstd[:, b:b + 1], ALU.subtract,
                                    ALU.mult).then_inc(S["xn_r"], 1)

            def a_norm(g, u, src, dst):
                yield from norm(steps_a, A, src, dst, a_st, a_mv, a_ve, a_rstd, 3, u, g)

            def b_norm(g, u, src):
                yield from norm(steps_b, B, src, b_xn, b_st, b_mv, b_ve, b_rstd, 2, u, g)

            def b_low(g, u):
                yield
                dve.wait_ge(B["xnT_r"], 2 * g + u + 1)
                v.tensor_tensor(b_xl[:].rearrange("p b t -> p (b t)"), PB[:, 0, :],
                                b_xh[:].rearrange("p b t -> p (b t)"), ALU.subtract).then_inc(B["xl_r"], 1)

            def c_norm(g, u, src):
                yield from norm(steps_c, C, src, c_xn, c_st, c_mv, c_ve, c_rstd, 2, u, g)

            def a_kv(g):
                yield
                dve.wait_ge(A["qk_ps"], 2 * g + 2)
                v.tensor_scalar(kT[:].rearrange("p b t -> p (b t)"), PA[:, 0, :],
                                vcol[:, V_BK:V_BK + 1], None, ALU.add).then_inc(A["kT_r"], 1)
                yield
                dve.wait_ge(A["v_ps"], g + 1)
                v.tensor_tensor(vaug[:, :, :, 0:HD0], PA[:, 1, 0:256].rearrange("p (b j d) -> p b j d", b=GB, d=HD0),
                                bvc[:].rearrange("p (j d) -> p j d", d=HD0).unsqueeze(1).to_broadcast([128, GB, 4, HD0]),
                                ALU.add).then_inc(A["v_r"], 1)

            def a_soft(g, b, t):
                yield
                dve.wait_ge(A["s_ps"], 8 * g + 2 * b + t + 1)
                hs = slice(4 * t, 4 * t + 4)
                yield from steps_a.then(v.tensor_reduce(a_mx[:, hs], PA[:, t, :].rearrange("p (h t) -> p h t", h=4),
                                                        AX.X, ALU.max))
                v.tensor_scalar(a_nm[:, hs], a_mx[:, hs], -HD0 ** -0.5, None, ALU.mult).then_inc(A["ss_r"], 1)

            def a_heads(g, b, t):
                yield
                dve.wait_ge(A["pv_ps"], 8 * g + 2 * b + t + 1)
                s = PA[:, t, 0:4 * 17].rearrange("p (n d) -> p n d", d=17)
                hs = slice(4 * t, 4 * t + 4)
                yield from steps_a.then(v.reciprocal(a_rd[:, hs], s[:, :, 16]))
                v.tensor_tensor(a_o[:, b, 64 * t:64 * t + 64].rearrange("p (h d) -> p h d", d=HD0),
                                s[:, :, 0:HD0], bc(a_rd[:, hs], HD0), ALU.mult).then_inc(A["o_r"], 1)

            def a_ctx(g):
                yield
                dve.wait_ge(A["css_r"], g + 1)
                v.tensor_scalar(cve[:], css[:], 1.0 / D, RMS_EPS, ALU.mult, ALU.add).then_inc(A["cve_r"], 1)
                yield
                dve.wait_ge(A["crs_r"], g + 1)
                for b in range(GB):
                    last = v.tensor_scalar(cn[:, b, :], cin[:, b, :], crs[:, b:b + 1], None, ALU.mult)
                last.then_inc(A["cn_r"], 1)
                yield
                dve.wait_ge(A["kq_ps"], g + 1)
                v.tensor_scalar(kq[:].rearrange("p b m -> p (b m)"), PA[:, 0, 0:GM], vcol[:, V_WS:V_WS + 1], None,
                                ALU.mult).then_inc(A["kq_r"], 1)

            def thread_a(g, first=False):
                steps_a.begin(g)
                yield
                dve.wait_ge(x_loaded, 16 * g + 16)
                yield from a_norm(g, 0, xin, a_xn)
                yield from a_kv(g)
                yield from a_soft(g, 0, 0)
                for b in range(GB):
                    yield from a_soft(g, b, 1)
                    yield from a_heads(g, b, 0)
                    if b + 1 < GB:
                        yield from a_soft(g, b + 1, 0)
                    yield from a_heads(g, b, 1)
                yield
                dve.wait_ge(A["o_r"], 8 * g + 8)
                yield from a_norm(g, 1, a_o, a_xn)
                yield
                dve.wait_ge(A["y_ps"], g + 1)
                dve.wait_ge(A["xc_r"], g + 1)
                if not first:
                    dve.wait_ge(x2_ready, g)
                yield from steps_a.then(v.tensor_tensor(x1[:].rearrange("p b d -> p (b d)"), PA[:, 1, :],
                                                        xc[:].rearrange("p b d -> p (b d)"), ALU.add))
                yield from a_norm(g, 2, x1, sn)
                yield from a_ctx(g)
                assert steps_a.n == STEPS[0], steps_a.n

            def s_round(g, t):
                u = 3 * g + t
                yield
                dve.wait_ge(S["sq_r"], u + 1)
                v.tensor_scalar(s_ve[:], s_sq[:], 1.0 / D, RMS_EPS, ALU.mult, ALU.add).then_inc(S["sve_r"], 1)
                yield
                dve.wait_ge(S["sc_ps"], u + 1)
                s = PS[0:MC, 0, :].rearrange("p (b t) -> p b t", b=GB)
                yield from steps_s.then(v.tensor_reduce(s_mx[:], s, AX.X, ALU.max))
                v.tensor_scalar(s_nm[:], s_mx[:], -D ** -0.5, None, ALU.mult).then_inc(S["ex_r"], 1)
                yield
                dve.wait_ge(S["e_r"], u + 1)
                yield from steps_s.then(v.reciprocal(s_rsum[:], s_sum[:]))
                v.tensor_tensor(s_e[:], s_e[:], bc(s_rsum[:], T), ALU.mult).then_inc(S["at_r"], 1)
                yield
                dve.wait_ge(S["at_ps"], u + 1)
                s = PS[:, 1, 0:GM].rearrange("p (b m) -> p b m", b=GB)
                yield from steps_s.then(v.tensor_reduce(s_row[:], s, AX.X, ALU.add))
                yield from steps_s.then(v.tensor_scalar(s_rowe[:], s_row[:], RMS_EPS, None, ALU.add))
                yield from steps_s.then(v.reciprocal(s_rrow[:], s_rowe[:]))
                v.tensor_tensor(s_an[:], s, bc(s_rrow[:], MC), ALU.mult).then_inc(S["an_r"], 1)
                yield
                dve.wait_ge(S["tr_r"], u + 1)
                dve.wait_ge(S["hn_r"], u + 1)
                yield from steps_s.then(v.scalar_tensor_tensor(g_q[:], g_tr[:], 1.0, g_q[:], ALU.add, ALU.mult))
                yield
                dve.wait_ge(S["g_ps"], 4 * u + 4)
                v.tensor_tensor(g_q[:], PS[:, 0, :], g_q[:], ALU.add).then_inc(S["pre_r"], 1)
                yield
                dve.wait_ge(S["n_r"], u + 1)
                yield from steps_s.then(v.tensor_tensor(g_d[:], hT[:], g_n[:], ALU.subtract))
                dve.wait_ge(S["tz_r"], u + 1)
                yield from steps_s.then(v.scalar_tensor_tensor(g_d[:], g_tz[:], 1.0, g_d[:], ALU.add, ALU.mult))
                v.scalar_tensor_tensor(hT[:], g_d[:], 0.5, g_n[:], ALU.mult, ALU.add).then_inc(S["h_r"], 1)

            def thread_s(g, first=False):
                steps_s.begin(g)
                for t in range(3):
                    yield from s_round(g, t)
                yield
                dve.wait_ge(S["hp_ps"], 3 * g + 3)
                if not first:
                    dve.wait_ge(B["x3_r"], 8 * g)
                v.tensor_tensor(x2[:].rearrange("p b d -> p (b d)"), PS[:, 0, :],
                                x1[:].rearrange("p b d -> p (b d)"), ALU.add).then_inc(x2_ready, 1)
                assert steps_s.n == STEPS[1], steps_s.n

            def b_route(g):
                yield
                dve.wait_ge(B["mt_r"], g + 1)
                st = steps_b
                yield from st.then(v.tensor_scalar(m_s[:], m_t[:], 0.5, 0.5, ALU.mult, ALU.add))
                yield from st.then(v.tensor_tensor(m_b[:], m_s[:], ebias[:].unsqueeze(1).to_broadcast([128, GB, NE]), ALU.add))
                hold(st)
                for b in range(GB):
                    last = v.max(m_top[:, b, :], m_b[:, b, :])
                yield from st.then(last)
                hold(st)
                for b in range(GB):
                    last = v.max_index(m_ix[:, b, :], m_top[:, b, :], m_b[:, b, :])
                yield from st.then(last)
                yield from st.then(v.tensor_copy(m_ixf[:], m_ix[:]))
                io = iota8[:].unsqueeze(1).to_broadcast([128, GB, NE])
                v.tensor_tensor(m_1[:], io, m_ixf[:, :, 0:1].to_broadcast([128, GB, NE]), ALU.is_equal)
                yield from st.then(v.tensor_tensor(m_2[:], io, m_ixf[:, :, 1:2].to_broadcast([128, GB, NE]), ALU.is_equal))
                yield from st.then(v.tensor_tensor(m_1[:], m_1[:], m_2[:], ALU.add))
                yield from st.then(v.tensor_tensor(m_w[:], m_1[:], m_s[:], ALU.mult))
                yield from st.then(v.tensor_tensor(m_w2[:], m_w[:], m_w[:], ALU.mult))

            def b_squares(g):
                for c in range(0, NCH, 2):
                    yield
                    dve.wait_ge(B["relu_r"], NCH * g + c + 1)
                    v.tensor_tensor(m_h[:, c, :], m_r[:, c % 4, :], m_r[:, c % 4, :], ALU.mult).then_inc(B["sqv_r"], 1)

            def b_combine(g, b):
                for f in range(2):
                    yield
                    dve.wait_ge(B["dn_ps"], 8 * g + 2 * b + f + 1)
                    for e in range(4 * f, 4 * f + 4):
                        ins = v.scalar_tensor_tensor(x3[:, b, :], PB[:, f, (e % 4) * 128:(e % 4) * 128 + 128],
                                                     m_w2[:, b, e:e + 1], x2[:, b, :] if e == 0 else x3[:, b, :],
                                                     ALU.mult, ALU.add)
                        if e % 4 < 3:
                            yield from steps_b.then(ins)
                    ins.then_inc(B["x3_r"], 1)
                    yield
                    dve.wait_ge(B["x3_r"], 8 * g + 2 * b + f + 1)

            def b_qk(g):
                pe4 = peT[:].unsqueeze(1).to_broadcast([128, GB, T])
                yield
                dve.wait_ge(B["k_ps"], g + 1)
                v.scalar_tensor_tensor(k1[:], PB[:, 0, :].rearrange("p (b t) -> p b t", b=GB),
                                       vcol[:, V_BK1:V_BK1 + 1], pe4, ALU.add, ALU.add).then_inc(B["k_r"], 1)
                for h in range(H1):
                    yield
                    dve.wait_ge(B["q_ps"], 8 * g + h + 1)
                    v.scalar_tensor_tensor(q1[:, h, :].rearrange("p (b t) -> p b t", b=GB),
                                           PB[:, h % 2, :].rearrange("p (b t) -> p b t", b=GB),
                                           vcol[:, V_BQ1 + h:V_BQ1 + h + 1], pe4, ALU.add, ALU.add).then_inc(B["q_r"], 1)

            def b_soft(g, b, f):
                yield
                dve.wait_ge(B["s_ps"], 8 * g + 2 * b + f + 1)
                s = PB[:, f, :].rearrange("p (h t) -> p h t", h=4)
                hs = slice(4 * f, 4 * f + 4)
                yield from steps_b.then(v.tensor_reduce(b_mx[:, hs], s, AX.X, ALU.max))
                v.tensor_scalar(b_nm[:, hs], b_mx[:, hs], -D ** -0.5, None, ALU.mult).then_inc(B["ss_r"], 1)

            def b_sums(g, b, f):
                yield
                dve.wait_ge(B["p_r"], 8 * g + 2 * b + f + 1)
                hs = slice(4 * f, 4 * f + 4)
                yield from steps_b.then(v.reciprocal(b_rs[:, hs], b_sum[:, hs]))
                v.tensor_tensor(b_p[:, hs, :], b_p[:, hs, :], bc(b_rs[:, hs], T), ALU.mult).then_inc(B["pn_r"], 1)

            def b_res(g, b, f):
                yield
                if f == 1:
                    dve.wait_ge(B["x4_r"], 8 * g + 2 * b + 1)
                dve.wait_ge(B["o_ps"], 8 * g + 2 * b + f + 1)
                v.tensor_tensor(x4[:, b, :], PB[:, f, 0:D], (x4 if f else x3)[:, b, :], ALU.add).then_inc(B["x4_r"], 1)

            def thread_b(g, first=False):
                steps_b.begin(g)
                yield
                dve.wait_ge(x2_ready, g + 1)
                yield from b_norm(g, 0, x2)
                yield from b_low(g, 0)
                yield from b_route(g)
                yield from b_squares(g)
                for b in range(GB):
                    yield from b_combine(g, b)
                yield from b_norm(g, 1, x3)
                yield from b_low(g, 1)
                yield from b_qk(g)
                yield from b_soft(g, 0, 0)
                for b in range(GB):
                    yield from b_soft(g, b, 1)
                    yield from b_sums(g, b, 0)
                    yield from b_sums(g, b, 1)
                    if b == 0:
                        yield
                        if not first:
                            dve.wait_ge(C["xn_r"], 8 * g - 4)
                            dve.wait_ge(C["x4b_r"], g)
                    yield from b_res(g, b, 0)
                    if b + 1 < GB:
                        yield from b_soft(g, b + 1, 0)
                    yield from b_res(g, b, 1)
                assert steps_b.n == STEPS[2], steps_b.n

            def cls(ap, c):
                return ap[:, OFF[c]:OFF[c + 1]].rearrange("p (h k) -> p h k", h=4)

            def c_blocks(g):
                yield
                dve.wait_ge(C["xv_r"], g + 1)
                v.tensor_tensor(vx_l[:].rearrange("p b d -> p (b d)"), PC[0:MC, 1, :],
                                vx_h[:].rearrange("p b d -> p (b d)"), ALU.subtract).then_inc(C["xvl_r"], 1)
                yield
                dve.wait_ge(C["xk_r"], g + 1)
                for c in range(NCLS):
                    for b in range(GB):
                        last = v.tensor_tensor(cls(kbd[:, b, :], c),
                                               kx[:, b, ::1 << c].unsqueeze(1).to_broadcast([128, 4, NK[c]]),
                                               bc(kmask[:, c, :], NK[c]), ALU.mult)
                last.then_inc(C["kbd_r"], 1)
                for i, (j, w) in enumerate(JT):
                    yield
                    dve.wait_ge(C["vbd_ps"], 5 * g + i + 1)
                    v.tensor_tensor(vbd[0:w, i, :, :], PC[0:w, i % 2, :].rearrange("p (b d) -> p b d", b=GB),
                                    vmask[0:w, i, :].unsqueeze(1).to_broadcast([w, GB, D]),
                                    ALU.mult).then_inc(C["vbd_r"], 1)

            def xps(c):
                if c == 0:
                    return PC[:, 0, 0:OFF[1]].rearrange("p (h k) -> p h k", h=4)
                return PC[:, 1, OFF[c] - OFF[1]:OFF[c + 1] - OFF[1]].rearrange("p (h k) -> p h k", h=4)

            def c_soft(g, b):
                yield
                dve.wait_ge(C["s_ps"], 4 * g + b + 1)
                for c in range(NCLS):
                    last = v.tensor_reduce(x_mx[:, 4 * c:4 * c + 4], xps(c), AX.X, ALU.max)
                yield from steps_c.then(last)
                for c in range(NCLS):
                    last = v.tensor_tensor(cls(x_p, c), xps(c), bc(x_mx[:, 4 * c:4 * c + 4], NK[c]), ALU.subtract)
                last.then_inc(C["ss_r"], 1)
                yield
                dve.wait_ge(C["p_r"], 4 * g + b + 1)
                for c in range(NCLS):
                    last = v.tensor_reduce(x_sum[:, 4 * c:4 * c + 4], cls(x_p, c), AX.X, ALU.add)
                yield from steps_c.then(last)
                v.reciprocal(x_rs[:], x_sum[:]).then_inc(C["rs_r"], 1)

            def c_mix(g):
                st = steps_c
                yield
                dve.wait_ge(C["fg_ps"], g + 1)
                yield from st.then(v.tensor_tensor(f_l[:], PC[:, 1, 0:GB * NE].rearrange("p (b e) -> p b e", b=GB),
                                        fgb[:].unsqueeze(1).to_broadcast([128, GB, NE]), ALU.add))
                yield from st.then(v.tensor_reduce(f_mx[:], f_l[:], AX.X, ALU.max))
                v.tensor_tensor(f_s[:], f_l[:], bc(f_mx[:], NE), ALU.subtract).then_inc(C["fs_r"], 1)
                yield
                dve.wait_ge(C["fe_r"], g + 1)
                yield from st.then(v.tensor_reduce(f_sum[:], f_e[:], AX.X, ALU.add))
                yield from st.then(v.reciprocal(f_r[:], f_sum[:]))
                yield from st.then(v.tensor_tensor(f_g[:], f_e[:], bc(f_r[:], NE), ALU.mult))
                yield from st.then(v.scalar_tensor_tensor(f_w0[:], f_g[:], 0.1, f_g[:], ALU.is_ge, ALU.mult))
                yield from st.then(v.tensor_reduce(f_ws[:], f_w0[:], AX.X, ALU.add))
                yield from st.then(v.tensor_scalar(f_z[:], f_ws[:], 0.0, None, ALU.is_equal))
                yield from st.then(v.tensor_tensor(f_wd[:], f_ws[:], f_z[:], ALU.add))
                yield from st.then(v.reciprocal(f_wr[:], f_wd[:]))
                v.tensor_tensor(f_w[:], f_w0[:], bc(f_wr[:], NE), ALU.mult).then_inc(C["fw_r"], 1)
                yield
                dve.wait_ge(C["fb_ps"], g + 1)
                dve.wait_ge(out_done, 16 * g + 16)
                v.tensor_tensor(y[:].rearrange("p b d -> p (b d)"), PC[:, 0, :],
                                x5[:].rearrange("p b d -> p (b d)"), ALU.add).then_inc(C["y0_r"], 1)
                yield
                dve.wait_ge(C["y0_r"], g + 1)
                for i, (b, f) in enumerate((b, f) for b in range(GB) for f in (1, 0)):
                    yield
                    dve.wait_ge(C["ff_ps"], 8 * g + i + 1)
                    for e in range(4 * f, 4 * f + 4):
                        ins = v.scalar_tensor_tensor(y[:, b, :], PC[:, f, (e % 4) * 128:(e % 4) * 128 + 128],
                                                     f_w[:, b, e:e + 1], y[:, b, :], ALU.mult, ALU.add)
                        if e % 4 < 3:
                            yield from st.then(ins)
                    ins.then_inc(C["y_r"], 1)
                    if i < 2 * GB - 1:
                        yield
                        dve.wait_ge(C["y_r"], 8 * g + i + 1)

            def thread_c(g):
                steps_c.begin(g)
                yield
                dve.wait_ge(B["x4_r"], 8 * g + 8)
                yield from c_norm(g, 0, x4)
                yield from c_blocks(g)
                for b in range(GB):
                    yield from c_soft(g, b)
                yield
                dve.wait_ge(C["xy_ps"], g + 1)
                dve.wait_ge(C["x4b_r"], g + 1)
                yield from steps_c.then(v.tensor_tensor(x5[:].rearrange("p b d -> p (b d)"), PC[:, 0, :],
                                             x4b[:].rearrange("p b d -> p (b d)"), ALU.add))
                yield from c_norm(g, 1, x5)
                yield from c_mix(g)
                assert steps_c.n == STEPS[3], steps_c.n

            weave(ORDER["dve"], a=thread_a(0, first=True))
            dve.wait_ge(late_loaded, N_LATE)
            for i, (hi, lo, w) in enumerate(SPLIT):
                dve.wait_ge(hi_made, i + 1)
                v.tensor_tensor(lo[:], w, hi[:], ALU.subtract).then_inc(lo_made, 1)
            weave(ORDER["dve"], a=thread_a(1), s=thread_s(0, first=True))
            weave(ORDER["dve"], a=thread_a(2), s=thread_s(1), b=thread_b(0, first=True))
            with dve.Fori(0, NG - 3) as g:
                weave(ORDER["dve"], a=thread_a(g + 3), s=thread_s(g + 2), b=thread_b(g + 1), c=thread_c(g))
            weave(ORDER["dve"], s=thread_s(NG - 1), b=thread_b(NG - 2), c=thread_c(NG - 3))
            weave(ORDER["dve"], b=thread_b(NG - 1), c=thread_c(NG - 2))
            weave(ORDER["dve"], c=thread_c(NG - 1))


def _layout(i):
    import numpy as np

    f = np.float32
    t = {k: np.asarray(v) for k, v in i.items()}
    vectors = {n: t[n].reshape(-1, 128) for n in (
        "L0_attn_bq", "L0_attn_bk", "L0_xattn_gru_bih", "L0_xattn_gru_bhh", "L0_xattn_slot_norm_w",
        "L0_xattn_input_norm_w", "L0_attn_ln_w", "L0_attn_ln_b", "L1_attn_bq", "L1_attn_bkv", "L1_xattn_bq",
        "L1_xattn_bk", "L1_xattn_bv")}
    w = {k: v for k, v in t.items() if k not in ("x", "ctx_1024", *vectors)}
    w["vectors"] = np.concatenate(list(vectors.values()))
    w["x"] = t["x"].transpose(1, 0, 2)
    w["ctx_tok"] = t["ctx_1024"].transpose(1, 0, 2)
    w["ctx_feat"] = t["ctx_1024"].transpose(2, 0, 1)
    for n in ("L0_xattn_gru_wih", "L0_xattn_gru_whh", "L0_ffn_gate_w", "L1_xattn_Wq", "L1_xattn_Wk", "L1_xattn_Wv",
              "L1_xattn_Wo"):
        w[n] = t[n].T
    w["L0_ffn_w_up"] = t["L0_ffn_w_up"].reshape(NE * HID, D).T
    w["L0_ffn_w_down"] = t["L0_ffn_w_down"].transpose(0, 2, 1).reshape(NCH, 128, D).transpose(1, 0, 2)
    w["L1_attn_Wo"] = t["L1_attn_Wo"].reshape(H1, 128, D).transpose(1, 0, 2)
    w["L1_ffn_expert_w"] = t["L1_ffn_expert_w"].transpose(1, 0, 2)
    p = np.arange(128)
    w["c_ident"] = np.eye(128, dtype=f)
    w["c_cmask"] = np.tile(np.where(p[None, :] > p[:, None], f(-1e30), f(0)), (1, 4)).astype(f)
    ang = p.astype(f)[:, None] * np.exp(f(-np.log(10000.0)) * np.arange(0, D, 2, dtype=f) / f(D))[None, :]
    pe = np.zeros((128, D), f)
    pe[:, 0::2], pe[:, 1::2] = np.sin(ang), np.cos(ang)
    w["c_peT"] = pe.T
    sel, vm, km = np.zeros((MC, JX), f), np.zeros((len(JT) * 128, D), f), np.zeros((128, NCLS, 4), f)
    for c in range(NCLS):
        for n in range(4):
            head = c + 4 * n
            km[head * HDX:(head + 1) * HDX, c, n] = 1
            for k in range(NK[c]):
                j = OFF[c] + n * NK[c] + k
                sel[k << c, j] = 1
                vm[j, head * HDX:(head + 1) * HDX] = 1
    w["c_sel"], w["c_kmask"] = sel, km
    w["c_hmask"] = np.repeat(np.eye(H0, dtype=f), HD0, axis=0)
    w["c_vmask"] = vm.reshape(len(JT), 128, D).transpose(1, 0, 2)
    w["c_iota8"] = np.tile(np.arange(NE, dtype=f), (128, 1))
    return {k: np.ascontiguousarray(v) for k, v in w.items()}


def kernel(**inputs):
    import concourse.bacc as _bacc
    from concourse import mybir as _mybir
    from concourse.bass_utils import run_bass_kernel_spmd as _run

    nc = _bacc.Bacc("TRN2", target_bir_lowering=False, num_devices=1)
    arrays, aps = {}, {}
    for name, arr in _layout(inputs).items():
        arrays[f"in_{name}_dram"] = arr
        aps[name] = nc.dram_tensor(f"in_{name}_dram", arr.shape, _mybir.dt.from_np(arr.dtype),
                                   kind="ExternalInput").ap()
    out = nc.dram_tensor("out_0_dram", (T, NS, D), F32, kind="ExternalOutput").ap()
    build(nc, aps, out)
    r = _run(nc, [arrays], core_ids=[0])
    return r.results[0]["out_0_dram"].transpose(1, 0, 2)
```
